# Optimizing a Trainium2 kernel written in Bass

```python
import numpy as np
import jax
import jax.numpy as jnp

def _softmax(x, axis=-1):
    return jax.nn.softmax(x, axis=axis)

def _gelu(x):
    return jax.nn.gelu(x, approximate=True)

def _silu(x):
    return jax.nn.silu(x)

def _sigmoid(x):
    return jax.nn.sigmoid(x)

def _layernorm(x, axis=-1, eps=1e-05):
    m = jnp.mean(x, axis=axis, keepdims=True)
    v = jnp.var(x, axis=axis, keepdims=True)
    return (x - m) / jnp.sqrt(v + eps)

def _scatter_add(tgt, idx, src, axis=0):
    return tgt.at[idx].add(src)

def _segment_sum(src, seg, n):
    return jax.ops.segment_sum(src, seg, n)
kernel_name = 'mk_gnn_resnorm_d4_gnn_r32_23cfbf'

def setup_inputs(seed: int=0):
    np.random.seed(seed)
    _w = jnp.asarray

    def _rec_inputs():
        import jax
        import jax.numpy as jnp
        _gk = jax.random.key(seed)
        x = -0.0003713 + 1 * jax.random.normal(jax.random.fold_in(_gk, 1), (50000, 128), jnp.float32)
        src = jax.random.randint(jax.random.fold_in(_gk, 2), (25000,), 0, 50000, jnp.int32)
        dst = jax.random.randint(jax.random.fold_in(_gk, 3), (25000,), 0, 50000, jnp.int32)
        _o = jnp.argsort(dst, stable=True)
        src = src[_o]
        dst = dst[_o]
        edge_attr_64 = 0.000102155 + 1.00015 * jax.random.normal(jax.random.fold_in(_gk, 11), (25000, 64), jnp.float32)
        return (x, src, dst, edge_attr_64)
    x, src, dst, edge_attr_64 = _rec_inputs()

    def _L0_gnn_setup():
        import jax, jax.numpy as jnp
        import numpy as np
        N_NODES = 3125
        N_EDGES = 50000
        D_IN = 128
        D_HID = 128
        EPS = 1e-12

        def _sage_conv(x, edge_index, W_l, W_r, b):
            src, dst = (edge_index[0], edge_index[1])
            msgs = x[src]
            summed = jax.ops.segment_sum(msgs, dst, num_segments=x.shape[0])
            cnt = jax.ops.segment_sum(jnp.ones((edge_index.shape[1],), x.dtype), dst, num_segments=x.shape[0])
            agg = summed / jnp.maximum(cnt, 1.0)[:, None]
            out = agg @ W_l + b + x @ W_r
            norm = jnp.linalg.norm(out, axis=-1, keepdims=True)
            return out / jnp.maximum(norm, EPS)
        key = jax.random.key(seed)
        ks = jax.random.split(key, 8)
        x = jax.random.normal(ks[0], (N_NODES, D_IN), dtype=jnp.float32)
        edge_index = jax.random.randint(ks[1], (2, N_EDGES), 0, N_NODES, dtype=jnp.int32)
        s1 = 1.0 / np.sqrt(D_IN)
        s2 = 1.0 / np.sqrt(D_HID)
        W1_l = jax.random.uniform(ks[2], (D_IN, D_HID), jnp.float32, -s1, s1)
        W1_r = jax.random.uniform(ks[3], (D_IN, D_HID), jnp.float32, -s1, s1)
        b1 = jnp.zeros((D_HID,), jnp.float32)
        W2_l = jax.random.uniform(ks[4], (D_HID, D_HID), jnp.float32, -s2, s2)
        W2_r = jax.random.uniform(ks[5], (D_HID, D_HID), jnp.float32, -s2, s2)
        b2 = jnp.zeros((D_HID,), jnp.float32)
        return {'x': x, 'edge_index': edge_index, 'W1_l': W1_l, 'W1_r': W1_r, 'b1': b1, 'W2_l': W2_l, 'W2_r': W2_r, 'b2': b2}
    _L0_gnn_all = _L0_gnn_setup()
    _L0_gnn_in = {k: v for k, v in _L0_gnn_all.items() if k in ('W1_l', 'W1_r', 'b1', 'W2_l', 'W2_r', 'b2')}
    del _L0_gnn_all

    def _L1_gnn_setup():
        import jax, jax.numpy as jnp
        import numpy as np
        N = 3125
        E = 50000
        D_IN = 128
        D_H = 128
        D_OUT = 128
        key = jax.random.key(seed)
        ks = jax.random.split(key, 11)
        x = jax.random.normal(ks[0], (N, D_IN), dtype=jnp.float32)
        edge_index = jax.random.randint(ks[1], (2, E), 0, N, dtype=jnp.int32)
        s_in = 1.0 / np.sqrt(D_IN)
        s_h = 1.0 / np.sqrt(D_H)
        return {'x': x, 'edge_index': edge_index, 'W_neigh1': jax.random.uniform(ks[2], (D_H, D_IN), jnp.float32, -s_in, s_in), 'b_neigh1': jax.random.uniform(ks[3], (D_H,), jnp.float32, -s_in, s_in), 'W_self1': jax.random.uniform(ks[4], (D_H, D_IN), jnp.float32, -s_in, s_in), 'b_self1': jax.random.uniform(ks[5], (D_H,), jnp.float32, -s_in, s_in), 'W_neigh2': jax.random.uniform(ks[6], (D_OUT, D_H), jnp.float32, -s_h, s_h), 'b_neigh2': jax.random.uniform(ks[7], (D_OUT,), jnp.float32, -s_h, s_h), 'W_self2': jax.random.uniform(ks[8], (D_OUT, D_H), jnp.float32, -s_h, s_h), 'b_self2': jax.random.uniform(ks[9], (D_OUT,), jnp.float32, -s_h, s_h)}
    _L1_gnn_all = _L1_gnn_setup()
    _L1_gnn_in = {k: v for k, v in _L1_gnn_all.items() if k in ('W_neigh1', 'b_neigh1', 'W_self1', 'b_self1', 'W_neigh2', 'b_neigh2', 'W_self2', 'b_self2')}
    del _L1_gnn_all

    def _L2_gnn_setup():
        import jax, jax.numpy as jnp
        import numpy as np
        N_NODES = 3125
        HIDDEN = 128
        OUT = 128
        N_EDGES = 50000

        def _sage_conv(x, src, dst, W_l, W_r, b):
            n = x.shape[0]
            msg_sum = jax.ops.segment_sum(x[src], dst, num_segments=n)
            deg = jax.ops.segment_sum(jnp.ones_like(dst, dtype=x.dtype), dst, num_segments=n)
            mean = msg_sum / jnp.maximum(deg, 1.0)[:, None]
            return mean @ W_l.T + b + x @ W_r.T
        key = jax.random.key(seed)
        ks = jax.random.split(key, 8)
        x = jax.random.normal(ks[0], (N_NODES, HIDDEN), dtype=jnp.float32)
        edge_index = jax.random.randint(ks[1], (2, N_EDGES), 0, N_NODES, dtype=jnp.int64)
        s = 1.0 / np.sqrt(HIDDEN)
        W1_l = jax.random.uniform(ks[2], (HIDDEN, HIDDEN), jnp.float32, -s, s)
        W1_r = jax.random.uniform(ks[3], (HIDDEN, HIDDEN), jnp.float32, -s, s)
        b1 = jnp.zeros((HIDDEN,), jnp.float32)
        W2_l = jax.random.uniform(ks[4], (OUT, HIDDEN), jnp.float32, -s, s)
        W2_r = jax.random.uniform(ks[5], (OUT, HIDDEN), jnp.float32, -s, s)
        b2 = jnp.zeros((OUT,), jnp.float32)
        return {'x': x, 'edge_index': edge_index, 'W1_l': W1_l, 'W1_r': W1_r, 'b1': b1, 'W2_l': W2_l, 'W2_r': W2_r, 'b2': b2}
    _L2_gnn_all = _L2_gnn_setup()
    _L2_gnn_in = {k: v for k, v in _L2_gnn_all.items() if k in ('W1_l', 'W1_r', 'b1', 'W2_l', 'W2_r', 'b2')}
    del _L2_gnn_all

    def _L3_gnn_setup():
        import jax, jax.numpy as jnp
        import numpy as np
        D_NODE = 128
        D_EDGE = 64
        N_NODES = 3125
        N_EDGES = 15625
        key = jax.random.key(seed)
        ks = jax.random.split(key, 12)

        def lin(k, fan_in, fan_out):
            bound = 1.0 / np.sqrt(fan_in)
            kw, kb = jax.random.split(k)
            W = jax.random.uniform(kw, (fan_in, fan_out), jnp.float32, -bound, bound)
            b = jax.random.uniform(kb, (fan_out,), jnp.float32, -bound, bound)
            return (W, b)
        node_features = jax.random.normal(ks[0], (N_NODES, D_NODE), jnp.float32)
        edge_index = jax.random.randint(ks[1], (2, N_EDGES), 0, N_NODES, jnp.int64 if jax.config.jax_enable_x64 else jnp.int32)
        edge_features = jax.random.normal(ks[2], (N_EDGES, D_EDGE), jnp.float32)
        W1, b1 = lin(ks[3], 2 * D_NODE + D_EDGE, D_NODE)
        W2, b2 = lin(ks[4], D_NODE, D_NODE)
        Wg, bg = lin(ks[5], 2 * D_NODE, D_NODE)
        Wt, bt = lin(ks[6], 2 * D_NODE, D_NODE)
        gamma = jnp.ones((D_NODE,), jnp.float32)
        beta = jnp.zeros((D_NODE,), jnp.float32)
        return {'node_features': node_features, 'edge_features': edge_features, 'W1': W1, 'b1': b1, 'W2': W2, 'b2': b2, 'Wg': Wg, 'bg': bg, 'Wt': Wt, 'bt': bt, 'gamma': gamma, 'beta': beta, 'edge_index': edge_index}
    _L3_gnn_all = _L3_gnn_setup()
    _L3_gnn_in = {k: v for k, v in _L3_gnn_all.items() if k in ('W1', 'b1', 'W2', 'b2', 'Wg', 'bg', 'Wt', 'bt', 'gamma', 'beta')}
    del _L3_gnn_all
    return {'x': x, 'src': src, 'dst': dst, 'edge_attr_64': edge_attr_64, 'L0_gnn_W1_l': _L0_gnn_in['W1_l'], 'L0_gnn_W1_r': _L0_gnn_in['W1_r'], 'L0_gnn_b1': _L0_gnn_in['b1'], 'L0_gnn_W2_l': _L0_gnn_in['W2_l'], 'L0_gnn_W2_r': _L0_gnn_in['W2_r'], 'L0_gnn_b2': _L0_gnn_in['b2'], 'L1_gnn_W_neigh1': _L1_gnn_in['W_neigh1'], 'L1_gnn_b_neigh1': _L1_gnn_in['b_neigh1'], 'L1_gnn_W_self1': _L1_gnn_in['W_self1'], 'L1_gnn_b_self1': _L1_gnn_in['b_self1'], 'L1_gnn_W_neigh2': _L1_gnn_in['W_neigh2'], 'L1_gnn_b_neigh2': _L1_gnn_in['b_neigh2'], 'L1_gnn_W_self2': _L1_gnn_in['W_self2'], 'L1_gnn_b_self2': _L1_gnn_in['b_self2'], 'L2_gnn_W1_l': _L2_gnn_in['W1_l'], 'L2_gnn_W1_r': _L2_gnn_in['W1_r'], 'L2_gnn_b1': _L2_gnn_in['b1'], 'L2_gnn_W2_l': _L2_gnn_in['W2_l'], 'L2_gnn_W2_r': _L2_gnn_in['W2_r'], 'L2_gnn_b2': _L2_gnn_in['b2'], 'L3_gnn_W1': _L3_gnn_in['W1'], 'L3_gnn_b1': _L3_gnn_in['b1'], 'L3_gnn_W2': _L3_gnn_in['W2'], 'L3_gnn_b2': _L3_gnn_in['b2'], 'L3_gnn_Wg': _L3_gnn_in['Wg'], 'L3_gnn_bg': _L3_gnn_in['bg'], 'L3_gnn_Wt': _L3_gnn_in['Wt'], 'L3_gnn_bt': _L3_gnn_in['bt'], 'L3_gnn_gamma': _L3_gnn_in['gamma'], 'L3_gnn_beta': _L3_gnn_in['beta']}

def reference(x, src, dst, edge_attr_64, L0_gnn_W1_l, L0_gnn_W1_r, L0_gnn_b1, L0_gnn_W2_l, L0_gnn_W2_r, L0_gnn_b2, L1_gnn_W_neigh1, L1_gnn_b_neigh1, L1_gnn_W_self1, L1_gnn_b_self1, L1_gnn_W_neigh2, L1_gnn_b_neigh2, L1_gnn_W_self2, L1_gnn_b_self2, L2_gnn_W1_l, L2_gnn_W1_r, L2_gnn_b1, L2_gnn_W2_l, L2_gnn_W2_r, L2_gnn_b2, L3_gnn_W1, L3_gnn_b1, L3_gnn_W2, L3_gnn_b2, L3_gnn_Wg, L3_gnn_bg, L3_gnn_Wt, L3_gnn_bt, L3_gnn_gamma, L3_gnn_beta):
    import jax
    import jax.numpy as jnp

    def _L0_gnn_ref(x, edge_index, W1_l, W1_r, b1, W2_l, W2_r, b2):
        import jax, jax.numpy as jnp
        import numpy as np
        N_NODES = 3125
        N_EDGES = 50000
        D_IN = 128
        D_HID = 128
        EPS = 1e-12

        def _sage_conv(x, edge_index, W_l, W_r, b):
            src, dst = (edge_index[0], edge_index[1])
            msgs = x[src]
            summed = jax.ops.segment_sum(msgs, dst, num_segments=x.shape[0])
            cnt = jax.ops.segment_sum(jnp.ones((edge_index.shape[1],), x.dtype), dst, num_segments=x.shape[0])
            agg = summed / jnp.maximum(cnt, 1.0)[:, None]
            out = agg @ W_l + b + x @ W_r
            norm = jnp.linalg.norm(out, axis=-1, keepdims=True)
            return out / jnp.maximum(norm, EPS)
        h = jax.nn.relu(_sage_conv(x, edge_index, W1_l, W1_r, b1))
        h = jax.nn.relu(_sage_conv(h, edge_index, W2_l, W2_r, b2))
        return h

    def _L1_gnn_ref(x, edge_index, W_neigh1, b_neigh1, W_self1, b_self1, W_neigh2, b_neigh2, W_self2, b_self2):
        import jax, jax.numpy as jnp
        import numpy as np
        N = 3125
        E = 50000
        D_IN = 128
        D_H = 128
        D_OUT = 128
        src, dst = (edge_index[0], edge_index[1])
        n = x.shape[0]
        deg = jax.ops.segment_sum(jnp.ones(src.shape[0], x.dtype), dst, num_segments=n)
        inv_deg = 1.0 / jnp.maximum(deg, 1.0)

        def agg(h):
            return jax.ops.segment_sum(h[src], dst, num_segments=n) * inv_deg[:, None]
        h1 = agg(x) @ W_neigh1.T + b_neigh1 + x @ W_self1.T + b_self1
        h1 = jax.nn.relu(h1)
        h2 = agg(h1) @ W_neigh2.T + b_neigh2 + h1 @ W_self2.T + b_self2
        return h2

    def _L2_gnn_ref(x, edge_index, W1_l, W1_r, b1, W2_l, W2_r, b2):
        import jax, jax.numpy as jnp
        import numpy as np
        N_NODES = 3125
        HIDDEN = 128
        OUT = 128
        N_EDGES = 50000

        def _sage_conv(x, src, dst, W_l, W_r, b):
            n = x.shape[0]
            msg_sum = jax.ops.segment_sum(x[src], dst, num_segments=n)
            deg = jax.ops.segment_sum(jnp.ones_like(dst, dtype=x.dtype), dst, num_segments=n)
            mean = msg_sum / jnp.maximum(deg, 1.0)[:, None]
            return mean @ W_l.T + b + x @ W_r.T
        src, dst = (edge_index[0], edge_index[1])
        h = jax.nn.relu(_sage_conv(x, src, dst, W1_l, W1_r, b1))
        out = _sage_conv(h, src, dst, W2_l, W2_r, b2)
        return out

    def _L3_gnn_ref(node_features, edge_features, W1, b1, W2, b2, Wg, bg, Wt, bt, gamma, beta, edge_index):
        import jax, jax.numpy as jnp
        import numpy as np
        D_NODE = 128
        D_EDGE = 64
        N_NODES = 3125
        N_EDGES = 15625
        num_nodes = node_features.shape[0]
        src, dst = (edge_index[0], edge_index[1])
        h_src = node_features[src]
        h_dst = node_features[dst]
        msg_in = jnp.concatenate([h_src, h_dst, edge_features], axis=-1)
        messages = jax.nn.silu(msg_in @ W1 + b1) @ W2 + b2
        aggregated = jax.ops.segment_sum(messages, dst, num_segments=num_nodes)
        count = jax.ops.segment_sum(jnp.ones((dst.shape[0],), messages.dtype), dst, num_segments=num_nodes)
        aggregated = aggregated / jnp.clip(count, 1.0)[:, None]
        gate_in = jnp.concatenate([node_features, aggregated], axis=-1)
        gate = jax.nn.sigmoid(gate_in @ Wg + bg)
        transform = jnp.tanh(gate_in @ Wt + bt)
        updated = gate * node_features + (1.0 - gate) * transform
        mu = jnp.mean(updated, axis=-1, keepdims=True)
        var = jnp.var(updated, axis=-1, keepdims=True)
        normed = (updated - mu) * jax.lax.rsqrt(var + 1e-05)
        return normed * gamma + beta
    edge_index = jnp.stack([src, dst])
    x = _layernorm(x + _L0_gnn_ref(x, edge_index, L0_gnn_W1_l, L0_gnn_W1_r, L0_gnn_b1, L0_gnn_W2_l, L0_gnn_W2_r, L0_gnn_b2), axis=-1)
    x = _layernorm(x + _L1_gnn_ref(x, edge_index, L1_gnn_W_neigh1, L1_gnn_b_neigh1, L1_gnn_W_self1, L1_gnn_b_self1, L1_gnn_W_neigh2, L1_gnn_b_neigh2, L1_gnn_W_self2, L1_gnn_b_self2), axis=-1)
    x = _layernorm(x + _L2_gnn_ref(x, edge_index, L2_gnn_W1_l, L2_gnn_W1_r, L2_gnn_b1, L2_gnn_W2_l, L2_gnn_W2_r, L2_gnn_b2), axis=-1)
    x = _layernorm(x + _L3_gnn_ref(x, edge_attr_64, L3_gnn_W1, L3_gnn_b1, L3_gnn_W2, L3_gnn_b2, L3_gnn_Wg, L3_gnn_bg, L3_gnn_Wt, L3_gnn_bt, L3_gnn_gamma, L3_gnn_beta, edge_index), axis=-1)
    return x

_drawn_inputs = setup_inputs


def setup_inputs(seed=0):
    import zlib

    import numpy as np

    out = dict(_drawn_inputs(seed))
    spreads = {'L0_gnn_b1': (0.0, 2.0),
     'L0_gnn_b2': (0.0, 0.1),
     'L2_gnn_b1': (0.0, 0.1),
     'L2_gnn_b2': (0.0, 0.1),
     'L3_gnn_gamma': (1.0, 0.2),
     'L3_gnn_beta': (0.0, 0.1)}
    factors = {'edge_attr_64': 6.028,
     'L0_gnn_W1_l': 24.022,
     'L0_gnn_W1_r': 2.884,
     'L0_gnn_W2_l': 4.516,
     'L3_gnn_W1': 2.693,
     'L3_gnn_b1': 39.237,
     'L3_gnn_b2': 8.0,
     'L3_gnn_bg': 6.309,
     'L3_gnn_bt': 4.168,
     'L0_gnn_W2_r': 2.854}
    for name, (base, spread) in spreads.items():
        noise = np.random.default_rng([zlib.crc32(name.encode()), seed]).standard_normal(out[name].shape)
        drawn = base * np.exp(spread * noise) if base else spread * noise
        out[name] = jnp.asarray(drawn.astype(out[name].dtype))
    for name, factor in factors.items():
        out[name] = (out[name] * factor).astype(out[name].dtype)
    return out
```

```python
from contextlib import ExitStack

import concourse.bass as bass
from concourse import mybir

F32 = mybir.dt.float32
BF16 = mybir.dt.bfloat16
I32 = mybir.dt.int32
ALU = mybir.AluOpType
ACT = mybir.ActivationFunctionType
AX_X = mybir.AxisListType.X

P = 128
N, D, E, DE = 50000, 128, 25000, 64
TILES = 3
GN = TILES * P
NG = -(-N // GN)
NP = NG * GN
WIN = GN // 2
HALF = WIN // TILES
NW = 2 * NG
WT = -(-NW // P)
ROW = -(-E // P)
EP = ROW * P
EPAD = EP + 2 * P
CH = 4
NEG = EP // P // CH
OUTSIDE = 1 << 20
SLOTS = 4
LEAD = 3
LN_EPS, NORM_EPS = 1e-5, 1e-12
CREDIT = 4

WEIGHTS = ["L0_gnn_W1_l", "L0_gnn_W1_r", "L0_gnn_W2_l", "L0_gnn_W2_r",
           "L1_gnn_W_neigh1", "L1_gnn_W_self1", "L1_gnn_W_neigh2", "L1_gnn_W_self2",
           "L2_gnn_W1_l", "L2_gnn_W1_r", "L2_gnn_W2_l", "L2_gnn_W2_r",
           "W1_src", "W1_dst", "W1_edge", "L3_gnn_W2", "Wg_self", "Wt_self", "Wg_agg", "Wt_agg"]
BIASES = ["L0_gnn_b1", "L0_gnn_b2", "L1_gnn_b_neigh1", "L1_gnn_b_neigh2", "L2_gnn_b1", "L2_gnn_b2",
          "L3_gnn_b2", "L3_gnn_bg", "L3_gnn_bt",
          "L1_gnn_b_self1", "L1_gnn_b_self2", "L3_gnn_gamma", "L3_gnn_beta"]
NB = 9


class Count:

    def __init__(self, sem, unit=1, start=0):
        self.sem, self.unit, self.base = sem, unit, start


class Group:

    def __init__(self, eng, it, c, kept):
        self.eng, self.it, self.c, self.kept = eng, it, c, kept

    def __add__(self, k):
        return Group(self.eng, self.it, self.c + k, self.kept)

    @property
    def slot(self):
        return self.c % SLOTS

    @property
    def turn(self):
        return self.c % 2

    @property
    def number(self):
        return self.c if self.it is None else self.it * SLOTS + self.c

    def below(self, n):
        return self.it is not None or self.c < n

    def value(self, unit, const):
        if self.it is None:
            return const
        if (unit, const) not in self.kept:
            self.kept[unit, const] = self.eng.snap(self.it * unit + const)
        return self.kept[unit, const]

    def wait(self, count, ago=0):
        const = count.base + count.unit * (self.c + 1 - ago)
        self.eng.wait_ge(count.sem, self.value(SLOTS * count.unit, const))

    def wait_slot(self, counts, ago=0):
        count = counts[self.slot]
        const = count.base + count.unit * (self.c // SLOTS + 1 - ago)
        self.eng.wait_ge(count.sem, self.value(count.unit, const))


def each_group(eng, n, ahead, step):
    loops = (n - ahead) // SLOTS
    with eng.Fori(0, loops) as it:
        kept = {}
        for c in range(SLOTS):
            step(Group(eng, it, c, kept))
    for c in range(SLOTS * loops, n):
        step(Group(eng, None, c, {}))


def first(eng, c):
    return Group(eng, None, c, {})


def gnn_kernel(nc, x, src_flat, dst_flat, dst_before, dst_after, edge_cols, edge_attr, weights,
               biases, b1_col, out):
    ctx = ExitStack()
    with ctx:
        def sb(name, shape, dt=F32):
            return ctx.enter_context(nc.sbuf_tensor(name, shape, dt))

        def sem(name):
            return ctx.enter_context(nc.semaphore(name))

        def count(name, start=CREDIT):
            return Count(sem(name), 1, start)

        def ring(name, unit, start=0):
            return [Count(sem(f"{name}{s}"), unit, start) for s in range(SLOTS)]

        h1, x1, h2, x2, h3, x3 = [nc.dram_tensor(n, (NP, D), F32, kind="Internal").ap()
                                  for n in ("h1", "x1", "h2", "x2", "h3", "x3")]
        message_rows = nc.dram_tensor("message_rows", (EPAD, D), F32, kind="Internal").ap()
        inv_flat = nc.dram_tensor("inv_flat", (EPAD, 1), F32, kind="Internal").ap()

        w_sb = sb("w_sb", [P, len(WEIGHTS) * P])
        b_sb = sb("b_sb", [P, len(BIASES) * P])
        b1_sb = sb("b1_sb", [P, 1])
        bias_conv = sb("bias_conv", [P, 6, GN], BF16)
        bias_edge = sb("bias_edge", [P, CH * P], BF16)
        bias_gate = sb("bias_gate", [P, 2, 2 * P], BF16)
        ident = sb("ident", [P, P])
        ones_row = sb("ones_row", [1, P])
        ones_b = sb("ones_b", [P, P], BF16)
        node_of_col = sb("node_of_col", [P, WIN])
        eps_ln = sb("eps_ln", [P, 1])
        minus_half = sb("minus_half", [P, TILES])
        t_src = sb("t_src", [P, WT * P])
        t_pos = sb("t_pos", [P, WT * P])
        t_dst = sb("t_dst", [P, WT * P])
        t_inv = sb("t_inv", [P, WT * P])
        e_idx = sb("e_idx", [P, NEG * 2 * CH], I32)

        own = sb("own", [P, SLOTS, GN])
        res = sb("res", [P, SLOTS, GN])
        msg = sb("msg", [P, SLOTS, 2, P])
        spread = sb("spread", [P, SLOTS, 2, WIN])
        done = sb("done", [P, SLOTS, GN])
        idx = sb("idx", [P, SLOTS, 2 * CH], I32)
        own_t = sb("own_t", [P, 2, GN])
        agg_t = sb("agg_t", [P, 2, GN])
        squares = sb("squares", [P, 2, GN])
        gate = sb("gate", [P, 2, GN])
        trans = sb("trans", [P, 2, GN])
        y_all = sb("y", [P, 2, GN])
        u_all = sb("u", [P, 2, GN])
        hb_all = sb("hb", [P, 2, GN])
        stats = sb("stats", [P, TILES, 6])
        mv = sb("mv", [P, TILES, 2])
        sumsq = sb("sumsq", [P, TILES])
        root = sb("root", [P, TILES])
        root_ln = sb("root_ln", [P, TILES])
        capped = sb("capped", [P, TILES])
        rinv = sb("rinv", [P, TILES])
        rstd = sb("rstd", [P, TILES])
        vpe = sb("vpe", [P, TILES])
        e_attr = sb("e_attr", [P, SLOTS, CH, DE])
        hs = sb("hs", [P, SLOTS, CH, P])
        hd = sb("hd", [P, SLOTS, CH, P])
        hs_t = sb("hs_t", [P, 2, CH * P])
        hd_t = sb("hd_t", [P, 2, CH * P])
        ea_t = sb("ea_t", [DE, 2, CH * P])
        hidden_t = sb("hidden_t", [P, 2, CH * P])
        e_out = sb("e_out", [P, SLOTS, CH, P])

        pair = [ctx.enter_context(nc.psum_tensor(f"banks{2 * i}", [P, 1024], F32)) for i in range(4)]
        bank = [pair[i // 2][:, 512 * (i % 2):512 * (i % 2) + 512] for i in range(8)]

        def w(name):
            k = WEIGHTS.index(name)
            return w_sb[:, k * P:(k + 1) * P]

        def b(name):
            k = BIASES.index(name)
            return b_sb[:, k * P:(k + 1) * P]

        def tiles(ap):
            return ap.rearrange("p (t f) -> p t f", t=TILES)

        loaded = sem("loaded")
        shaped = sem("shaped")
        prep_v = sem("prep_v")
        cols_ready = sem("cols_ready")
        rows_ready = sem("rows_ready")
        prep_t = sem("prep_t")
        inv_ready = sem("inv_ready")
        inv_out = sem("inv_out")
        rows_wanted = sem("rows_wanted")
        rows_in = sem("rows_in")
        wins_wanted = sem("wins_wanted")
        wins_in = sem("wins_in")
        wins_ready = sem("wins_ready")
        tables_ready = sem("tables_ready")
        tail_in = sem("tail_in")
        tail_out = sem("tail_out")
        pad_out = sem("pad_out")
        more_cols = sem("more_cols")
        more_at = sem("more_at")
        more_in = sem("more_in")
        more_dst = sem("more_dst")
        more_spread = sem("more_spread")
        more_passed_pool, more_passed_pe, more_passed_v = [sem(f"more_passed_{e}") for e in ("pool", "pe", "v")]
        gathers_begun = sem("gathers_begun")
        more_used = sem("more_used")
        phase_done = sem("phase_done")

        own_in = ring("own_in", 16)
        res_in = ring("res_in", 16)
        msg_in = ring("msg_in", 32)
        hs_in = ring("hs_in", 32 * CH)
        out_left = ring("out_left", 16, 16)
        idx_set = count("idx_set")
        own_turned = count("own_turned")
        own_kept = count("own_kept")
        agg_made = count("agg_made")
        agg_kept_a = count("agg_kept_a")
        agg_kept_v = count("agg_kept_v")
        spread_set = count("spread_set")
        out_made = count("out_made")
        relu_done = count("relu_done")
        sq_done = count("sq_done")
        sum_done = count("sum_done")
        root_done = count("root_done")
        cap_done = count("cap_done")
        rinv_done = count("rinv_done")
        unit_done = count("unit_done")
        sum_res = count("sum_res")
        stats_done = count("stats_done")
        mv_done = count("mv_done")
        std_done = count("std_done")
        rstd_done = count("rstd_done")
        done_v = count("done_v")
        hidden_done = count("hidden_done")
        messages_made = count("messages_made")
        gates_done = count("gates_done")
        diff_done = count("diff_done")
        gated_done = count("gated_done")
        upd_done = count("upd_done")
        inner_stats = count("inner_stats")
        inner_mean = count("inner_mean")
        inner_mv = count("inner_mv")
        outer_mean = count("outer_mean")
        inner_pow = count("inner_pow")
        beta_done = count("beta_done")
        gamma_done = count("gamma_done")
        outer_pow = count("outer_pow")

        PHASES = [
            dict(kind="unit", own=x, res=None, out=h1, wl="L0_gnn_W1_l", wr="L0_gnn_W1_r", bias=0),
            dict(kind="unit_ln", own=h1, res=x, out=x1, wl="L0_gnn_W2_l", wr="L0_gnn_W2_r", bias=1),
            dict(kind="relu", own=x1, res=None, out=h2, wl="L1_gnn_W_neigh1", wr="L1_gnn_W_self1", bias=2),
            dict(kind="ln", own=h2, res=x1, out=x2, wl="L1_gnn_W_neigh2", wr="L1_gnn_W_self2", bias=3),
            dict(kind="relu", own=x2, res=None, out=h3, wl="L2_gnn_W1_l", wr="L2_gnn_W1_r", bias=4),
            dict(kind="ln", own=h3, res=x2, out=x3, wl="L2_gnn_W2_l", wr="L2_gnn_W2_r", bias=5),
            dict(kind="edge"),
            dict(kind="gate", own=x3, res=None, out=out),
        ]
        NODE = [idx_set, own_turned, own_kept, agg_made, spread_set, out_made]
        UNIT = [agg_kept_a, sq_done, sum_done, root_done, cap_done, rinv_done]
        NORM = [sum_res, stats_done, mv_done, done_v]
        STEPS = {
            "unit": NODE + UNIT + [done_v],
            "unit_ln": NODE + UNIT + [unit_done, std_done, rstd_done] + NORM,
            "relu": NODE + [agg_kept_v, relu_done],
            "ln": NODE + [agg_kept_a, std_done, rstd_done] + NORM,
            "edge": [idx_set, own_turned, own_kept, agg_kept_v, out_made, hidden_done, messages_made, done_v],
            "gate": NODE + [agg_kept_a, gates_done, diff_done, gated_done,
                            upd_done, inner_stats, inner_mean, inner_mv, outer_mean, inner_pow, beta_done, gamma_done,
                            outer_pow] + NORM,
        }
        ACT_COUNTS = [idx_set, own_kept, agg_kept_a, sq_done, root_done, std_done, relu_done, hidden_done,
                      gates_done]
        DVE_COUNTS = [spread_set, agg_kept_v, sum_done, cap_done, rinv_done, unit_done, sum_res,
                      stats_done, mv_done, rstd_done, done_v, diff_done, gated_done, upd_done,
                      inner_stats, inner_mean, inner_mv, outer_mean, beta_done, gamma_done]
        PE_COUNTS = [own_turned, agg_made, out_made, messages_made]
        POOL_COUNTS = [inner_pow, outer_pow]

        def walk(eng, program):
            for c in ACT_COUNTS + DVE_COUNTS + PE_COUNTS + POOL_COUNTS:
                c.base = CREDIT
            for r, start in ((own_in, 0), (res_in, 0), (msg_in, 0), (hs_in, 0), (out_left, 16)):
                for c in r:
                    c.base = start
            for ph, phase in enumerate(PHASES):
                if ph:
                    eng.wait_ge(phase_done, ph)
                program(phase)
                n = NEG if phase["kind"] == "edge" else NG
                for c in STEPS[phase["kind"]]:
                    c.base += n
                rings = [own_in, out_left, hs_in if phase["kind"] == "edge" else msg_in]
                for r in rings + ([res_in] if phase.get("res") is not None else []):
                    for s, c in enumerate(r):
                        c.base += c.unit * len(range(s, n, SLOTS))

        def of_group(table, g):
            rows = table.shape[0] // GN * GN
            return table[0:rows, :].rearrange("(g p t) f -> p g (t f)", p=P, t=TILES)[
                :, bass.ds(g.number, 1), :].rearrange("p g f -> p (g f)")

        def last_pieces(table, tile):
            at = (NG - 1) * GN
            whole, rest = divmod(N - at, TILES)
            assert rest
            return ((tile[0:whole, :],
                     table[at:at + whole * TILES, :].rearrange("(p t) f -> p (t f)", t=TILES)),
                    (tile[whole:whole + 1, 0:rest * D],
                     table[at + whole * TILES:N, :].rearrange("(p t) f -> p (t f)", t=rest)))

        def of_chunks(table, g):
            rows = CH * P
            whole = table.shape[0] // rows * rows
            return table[0:whole, :].rearrange("(g c p) f -> p (g c) f", p=P, c=CH)[
                :, bass.ds(g.number * CH, CH), :]

        start_row = sb("start_row", [1, WT * P], I32)
        more_row = sb("more_row", [1, NW], I32)
        more_any = sb("more_any", [1, 1], I32)
        x_zero = sb("x_zero", [P, (EPAD - EP) // P * D])
        x_src = sb("x_src", [P, 1], I32)
        x_dst = sb("x_dst", [P, 1], I32)
        x_inv = sb("x_inv", [P, 1])
        x_local = sb("x_local", [P, 1])
        x_msg = sb("x_msg", [P, P])
        x_spread = sb("x_spread", [P, WIN])
        win_base = sb("win_base", [P, NW])

        class Extra:

            def __init__(self, eng, passed):
                self.eng = eng
                self.most = eng.value_load(more_any[:, :], min_val=0, max_val=ROW)
                self.passed = passed
                self.item = eng.alloc_register("extra_item")
                eng.reg_mov(self.item, 0)

            def rounds(self, g, k, body):
                eng = self.eng
                window = g.number * 2 + k
                more = eng.value_load(more_row[:, bass.ds(window, 1)], min_val=0, max_val=ROW)
                with eng.If(more > 0):
                    with eng.Fori(0, more) as r:
                        eng.reg_add(self.item, self.item, 1)
                        body(r, window)
                    eng.nop()
                with eng.Else():
                    eng.nop()

            def choose(self, phase_program):
                with self.eng.If(self.most > 0):
                    phase_program(True)
                    self.eng.nop()
                with self.eng.Else():
                    phase_program(False)
                    self.eng.nop()

            def wait(self, *counted):
                eng = self.eng
                item = eng.snap(self.item, min_val=1, max_val=1 << 20)
                values = [eng.snap(item * unit) for _, unit in counted]
                for (one, _), value in zip(counted, values):
                    eng.wait_ge(one, value)
                eng.sem_inc(self.passed, 1)

        dst_i = sb("dst_i", [P, ROW], I32)
        before_i = sb("before_i", [P, ROW], I32)
        after_i = sb("after_i", [P, ROW], I32)
        pos_i = sb("pos_i", [P, ROW], I32)
        thr_i = sb("thr_i", [P, WT], I32)
        node_i = sb("node_i", [P, WIN], I32)
        edge_i = sb("edge_i", [P, P], I32)
        part_i = sb("part_i", [P, 1], I32)
        base_i = sb("base_i", [P, NW], I32)
        start_line = sb("start_line", [1, WT * P])
        more_f = sb("more_f", [1, NW])
        more_i = sb("more_i", [1, NW], I32)
        most_f = sb("most_f", [1, 1])
        dst_f = sb("dst_f", [P, ROW])
        before_f = sb("before_f", [P, ROW])
        after_f = sb("after_f", [P, ROW])
        pos_f = sb("pos_f", [P, ROW])
        thr = sb("thr", [P, WT])
        edge_f = sb("edge_f", [P, P])
        part_f = sb("part_f", [P, 1])
        starts = sb("starts", [P, ROW])
        ends = sb("ends", [P, ROW])
        inv_rows = sb("inv_rows", [P, ROW])
        line = sb("line", [1, 3, P])
        scanned = sb("scanned", [1, 2, P])
        shifted = sb("shifted", [1, 2, P])
        carry = sb("carry", [P, 2])
        junk = sb("junk", [P, ROW])
        cnt = sb("cnt", [P, WT])
        row_f = sb("row_f", [P, WT])
        row_i = sb("row_i", [P, WT], I32)
        got_i = sb("got_i", [P, WT, ROW], I32)
        got_f = sb("got_f", [P, WT, ROW])
        start_f = sb("start_f", [P, WT])
        start_i = sb("start_i", [P, WT], I32)
        win_dst = sb("win_dst", [P, WT, P], I32)
        win_src = sb("win_src", [P, WT, P], I32)
        win_inv = sb("win_inv", [P, WT, P])
        by_win = sb("by_win", [P, 3, WT, P])
        skip = sb("skip", [P, WT, P])
        mask = sb("mask", [P, 3])
        hi = sb("hi", [P, NB * P], BF16)
        mid = sb("mid", [P, NB * P], BF16)
        lo = sb("lo", [P, NB * P], BF16)
        rest_f = sb("rest_f", [P, NB * P])

        LOADS = [(dst_i[:, :], dst_flat[0:EP, :].rearrange("(p k) o -> p (k o)", p=P)),
                 (before_i[:, :], dst_before), (after_i[:, :], dst_after),
                 (b_sb[:, :], biases), (b1_sb[:, :], b1_col), (e_idx[:, :], edge_cols), (w_sb[:, :], weights)]

        block = ctx.enter_context(nc.Block())

        @block.sync
        def _(sp):
            for tile, source in LOADS:
                sp.dma_start(tile, source).then_inc(loaded, 16)
            sp.wait_ge(inv_ready, 1)
            sp.dma_start(inv_flat[0:EP, :].rearrange("(p k) o -> p (k o)", p=P), inv_rows[:, :]) \
                .then_inc(inv_out, 16)
            sp.dma_start(inv_flat[EP:EPAD, :].rearrange("(p k) o -> p (k o)", k=P), inv_rows[0:2, 0:P]) \
                .then_inc(inv_out, 16)
            sp.wait_ge(shaped, 3)
            sp.dma_start(message_rows[EP:EPAD, :].rearrange("(p k) f -> p (k f)", p=P),
                         x_zero[:, :]).then_inc(pad_out, 16)
            sp.wait_ge(pad_out, 16)
            for c in out_left:
                sp.sem_inc(c.sem, 16)
            tails = [0]

            def load_pieces(pieces, into):
                (to, source), (to_rest, source_rest) = pieces
                sp.dma_start(to, source).then_inc(tail_in, 16)
                tails[0] += 1
                sp.wait_ge(tail_in, 16 * tails[0])
                sp.dma_start(to_rest, source_rest).then_inc(into.sem, 16)

            def load(g, table, tile, into):
                if table is x and g.it is None and g.c == NG - 1:
                    load_pieces(last_pieces(x, tile), into)
                else:
                    sp.dma_start(tile, of_group(table, g)).then_inc(into.sem, 16)

            def stores_landed(n):
                for s, c in enumerate(out_left):
                    sp.wait_ge(c.sem, c.base + c.unit * len(range(s, n, SLOTS)))
                sp.sem_inc(phase_done, 1)

            def node_phase(phase):
                last_read = {"gate": beta_done}.get(phase["kind"], own_turned)
                result = relu_done if phase["kind"] == "relu" else done_v

                def loads(g):
                    g.wait(last_read, ago=SLOTS)
                    load(g, phase["own"], own[:, g.slot, :], own_in[g.slot])
                    if phase["res"] is not None:
                        g.wait(sum_res, ago=SLOTS)
                        load(g, phase["res"], res[:, g.slot, :], res_in[g.slot])

                def step(g):
                    if g.below(NG - LEAD):
                        loads(g + LEAD)
                    g.wait(result)
                    if phase["out"] is out and g.it is None and g.c == NG - 1:
                        (tile, rows), (tile_rest, rows_rest) = last_pieces(out, done[:, g.slot, :])
                        sp.dma_start(rows, tile).then_inc(tail_out, 16)
                        sp.dma_start(rows_rest, tile_rest).then_inc(out_left[g.slot].sem, 16)
                        sp.wait_ge(tail_out, 16)
                    else:
                        sp.dma_start(of_group(phase["out"], g), done[:, g.slot, :]) \
                            .then_inc(out_left[g.slot].sem, 16)

                for c in range(LEAD):
                    loads(first(sp, c))
                each_group(sp, NG, LEAD + 1, step)
                stores_landed(NG)

            def edge_phase():
                def loads(g):
                    g.wait(own_turned, ago=SLOTS)
                    into = own_in[g.slot]
                    if g.it is None and g.c == NEG - 1:
                        at = g.c * CH * P
                        whole, rest = divmod(E - at, P)
                        split = at + whole * P
                        load_pieces(((e_attr[:, g.slot, 0:whole, :],
                                      edge_attr[at:split, :].rearrange("(c p) f -> p c f", p=P)),
                                     (e_attr[0:rest, g.slot, whole, :], edge_attr[split:E, :])), into)
                    else:
                        sp.dma_start(e_attr[:, g.slot, :, :], of_chunks(edge_attr, g)).then_inc(into.sem, 16)

                def step(g):
                    if g.below(NEG - LEAD):
                        loads(g + LEAD)
                    g.wait(done_v)
                    sp.dma_start(of_chunks(message_rows, g), e_out[:, g.slot, :, :]) \
                        .then_inc(out_left[g.slot].sem, 16)

                for c in range(LEAD):
                    loads(first(sp, c))
                each_group(sp, NEG, LEAD + 1, step)
                stores_landed(NEG)

            walk(sp, lambda phase: edge_phase() if phase["kind"] == "edge" else node_phase(phase))

        @block.gpsimd
        def _(pool):
            for c in POOL_COUNTS:
                pool.sem_inc(c.sem, CREDIT)
            pool.iota(pos_i[:, :], pattern=[[1, ROW]], base=0, channel_multiplier=ROW)
            pool.iota(thr_i[:, :], pattern=[[WIN * P, WT]], base=0, channel_multiplier=WIN)
            pool.iota(node_i[:, :], pattern=[[1, TILES], [TILES, HALF]], base=0, channel_multiplier=0)
            pool.iota(edge_i[:, :], pattern=[[1, P]], base=0, channel_multiplier=0)
            pool.iota(base_i[:, :], pattern=[[WIN, NW]], base=0, channel_multiplier=0)
            pool.iota(part_i[:, :], pattern=[[1, 1]], base=0, channel_multiplier=1).then_inc(shaped, 1)
            pool.memset(ident[:, :], 0.0).then_inc(shaped, 1)
            pool.memset(ones_row[:, :], 1.0)
            pool.memset(ones_b[:, :], 1.0)
            pool.memset(x_zero[:, :], 0.0)
            pool.memset(eps_ln[:, :], LN_EPS)
            pool.memset(minus_half[:, :], -0.5)
            pool.memset(msg[:, :, :, :], 0.0)
            pool.memset(hs[:, :, :, :], 0.0)
            pool.memset(hd[:, :, :, :], 0.0).then_inc(shaped, 1)
            pool.wait_ge(shaped, 3)
            pool.affine_select(out=ident[:, :], in_=ident[:, :], compare_op=ALU.not_equal, fill=1.0,
                               base=0, pattern=[[-1, P]], channel_multiplier=1).then_inc(shaped, 1)

            def fetch(into, table, at, bound, counted):
                pool.indirect_dma_start(into, None, table, bass.IndirectOffsetOnAxis(ap=at, axis=0),
                                        bounds_check=bound, oob_is_err=False) \
                    .then_inc(counted, 16)

            pool.wait_ge(rows_wanted, 1)
            dst_rows = dst_flat[0:EP, :].rearrange("(p k) o -> p (k o)", p=P)
            for t in range(WT):
                fetch(got_i[:, t, :], dst_rows, row_i[:, t:t + 1], P - 1, rows_in)
            pool.wait_ge(wins_wanted, 1)
            pool.wait_ge(inv_out, 32)
            for t in range(WT):
                for into, table in ((win_dst, dst_flat), (win_src, src_flat), (win_inv, inv_flat)):
                    fetch(into[:, t, :], table, start_i[:, t:t + 1], EPAD - P, wins_in)

            pool.wait_ge(tables_ready, 1)
            extra = Extra(pool, more_passed_pool)

            def node_phase(phase, extra_rounds):
                table = message_rows if phase["kind"] == "gate" else phase["own"]
                bound = (E if phase["kind"] == "gate" else N) - 1

                def gather(g):
                    g.wait(idx_set)
                    g.wait(agg_made, ago=SLOTS)
                    pool.sem_inc(gathers_begun, 1)
                    for k in range(2):
                        fetch(msg[:, g.slot, k, :], table, idx[:, g.slot, k:k + 1], bound, msg_in[g.slot].sem)

                def more(g):
                    for k in range(2):
                        extra.rounds(g, k, lambda r, window: fetch_round(r, window))

                def fetch_round(r, window):
                    start = pool.value_load(start_row[:, bass.ds(window, 1)], min_val=0, max_val=EP)
                    at = nc.s_assert_within(start + r * P + P, 0, EPAD - P)
                    extra.wait((more_used, 1))
                    pool.dma_start(x_dst[:, :], dst_flat[bass.ds(at, P), :]).then_inc(more_at, 16)
                    pool.dma_start(x_inv[:, :], inv_flat[bass.ds(at, P), :]).then_inc(more_at, 16)
                    if phase["kind"] == "gate":
                        pool.dma_start(x_msg[:, :], message_rows[bass.ds(at, P), :]).then_inc(more_at, 16)
                        extra.wait((more_at, 48))
                        pool.dma_start(x_src[:, :], src_flat[bass.ds(at, P), :]).then_inc(more_in, 16)
                    else:
                        pool.dma_start(x_src[:, :], src_flat[bass.ds(at, P), :]).then_inc(more_at, 16)
                        extra.wait((more_at, 48))
                        fetch(x_msg[:, :], table, x_src[:, :], N - 1, more_in)

                def step(g):
                    if g.below(NG - LEAD):
                        gather(g + LEAD)
                    if extra_rounds and g.below(NG - 1):
                        more(g + 1)
                    if phase["kind"] != "gate":
                        return
                    for variance, power in ((inner_mv, inner_pow), (mv_done, outer_pow)):
                        g.wait(variance)
                        pool.tensor_tensor(rstd[:, :], vpe[:, :], minus_half[:, :], ALU.pow) \
                            .then_inc(power.sem, 1)

                for c in range(LEAD):
                    gather(first(pool, c))
                if extra_rounds:
                    more(first(pool, 0))
                each_group(pool, NG, LEAD, step)

            def edge_phase():
                def gathers(g):
                    g.wait(idx_set)
                    g.wait(own_turned, ago=SLOTS)
                    pool.sem_inc(gathers_begun, 1)
                    for c in range(CH):
                        for k, rows in enumerate((hs, hd)):
                            at = k * CH + c
                            fetch(rows[:, g.slot, c, :], x3, idx[:, g.slot, at:at + 1], N - 1,
                                  hs_in[g.slot].sem)

                each_group(pool, NEG, 0, gathers)

            walk(pool, lambda phase: edge_phase() if phase["kind"] == "edge" else
                 extra.choose(lambda extra_rounds: node_phase(phase, extra_rounds)))

        @block.scalar
        def _(act):
            for c in ACT_COUNTS:
                act.sem_inc(c.sem, CREDIT)
            act.wait_ge(tables_ready, 1)

            def node_phase(phase):
                kind = phase["kind"]
                table = t_pos if kind == "gate" else t_src

                def stage(g):
                    act.activation(idx[:, g.slot, 0:2], table[:, bass.ds(g.number * 2, 2)], ACT.Copy) \
                        .then_inc(idx_set.sem, 1)

                def keep(g):
                    g.wait(own_turned)
                    g.wait(out_made, ago=2)
                    act.activation(own_t[:, g.turn, :], bank[g.turn][:, 0:GN], ACT.Copy).then_inc(own_kept.sem, 1)
                    if kind != "relu":
                        g.wait(agg_made)
                        act.activation(agg_t[:, g.turn, :], bank[2 + g.turn][:, 0:GN], ACT.Copy) \
                            .then_inc(agg_kept_a.sem, 1)

                def step(g):
                    made = bank[4 + g.turn][:, 0:GN]
                    if g.below(NG - 1):
                        keep(g + 1)
                    if g.below(NG - SLOTS):
                        g.wait(agg_made)
                        stage(g + SLOTS)
                    g.wait(out_made)
                    if kind == "relu":
                        g.wait_slot(out_left, ago=1)
                        act.activation(done[:, g.slot, :], made, ACT.Relu).then_inc(relu_done.sem, 1)
                    if kind in ("unit", "unit_ln"):
                        g.wait(sum_done, ago=2)
                        act.activation(squares[:, g.turn, :], made, ACT.Square).then_inc(sq_done.sem, 1)
                        g.wait(sum_done)
                        act.activation(root[:, :], sumsq[:, :], ACT.Sqrt).then_inc(root_done.sem, 1)
                    if kind in ("unit_ln", "ln"):
                        g.wait(mv_done)
                        act.activation(root_ln[:, :], mv[:, :, 1], ACT.Sqrt, bias=eps_ln[:, :]) \
                            .then_inc(std_done.sem, 1)
                    if kind == "gate":
                        g.wait(upd_done, ago=2)
                        made = pair[2][:, 0:TILES * 2 * P].rearrange("p (t k f) -> p t k f", t=TILES, k=2)
                        act.activation(tiles(gate[:, g.turn, :]), made[:, :, 0, :], ACT.Sigmoid)
                        act.activation(tiles(trans[:, g.turn, :]), made[:, :, 1, :], ACT.Tanh) \
                            .then_inc(gates_done.sem, 1)

                for c in range(SLOTS):
                    stage(first(act, c))
                keep(first(act, 0))
                each_group(act, NG, SLOTS, step)

            def edge_phase():
                def stage(g):
                    act.activation(idx[:, g.slot, :], e_idx[:, bass.ds(g.number * 2 * CH, 2 * CH)], ACT.Copy) \
                        .then_inc(idx_set.sem, 1)

                def keep(g):
                    g.wait(own_turned)
                    g.wait(out_made, ago=2)
                    act.activation(hs_t[:, g.turn, :], bank[g.turn], ACT.Copy).then_inc(own_kept.sem, 1)

                def step(g):
                    if g.below(NEG - 1):
                        keep(g + 1)
                    if g.below(NEG - SLOTS):
                        g.wait(own_turned)
                        stage(g + SLOTS)
                    g.wait(out_made)
                    g.wait(messages_made, ago=2)
                    act.activation(hidden_t[:, g.turn, :], bank[6], ACT.Silu, bias=b1_sb[:, :]) \
                        .then_inc(hidden_done.sem, 1)

                for c in range(SLOTS):
                    stage(first(act, c))
                keep(first(act, 0))
                each_group(act, NEG, SLOTS, step)

            walk(act, lambda phase: edge_phase() if phase["kind"] == "edge" else node_phase(phase))

        @block.tensor
        def _(pe):
            for c in PE_COUNTS:
                pe.sem_inc(c.sem, CREDIT)
            pe.wait_ge(shaped, 4)
            pe.wait_ge(cols_ready, 1)
            for k, col in enumerate((starts[:, ROW - 1:ROW], ends[:, 0:1], dst_f[:, 0:1])):
                turned = pe.transpose(bank[0][0:1, k * P:(k + 1) * P], col, ident[:, :])
            turned.then_inc(prep_t, 1)
            pe.wait_ge(rows_ready, 1)
            for k in range(2):
                pe.matmul(bank[1][:, k:k + 1], shifted[:, k, :], ones_row[:, 0:1], start=True, stop=True)
            pe.matmul(bank[1][:, P:2 * P], ones_row[:, :], line[:, 2, :], start=True, stop=True) \
                .then_inc(prep_t, 1)
            pe.wait_ge(wins_ready, 1)
            for k in range(4):
                for t in range(WT):
                    source = by_win[:, k, t, :] if k < 3 else win_inv[:, t, :]
                    turned = pe.transpose(bank[2 + k][:, t * P:(t + 1) * P], source, ident[:, :])
            turned.then_inc(prep_t, 1)
            pe.wait_ge(more_cols, 1)
            for t in range(WT):
                turned = pe.transpose(bank[6][0:1, t * P:(t + 1) * P], start_f[:, t:t + 1], ident[:, :])
            turned.then_inc(prep_t, 1)
            pe.wait_ge(tables_ready, 1)
            pe.sem_inc(more_used, 1)
            extra = Extra(pe, more_passed_pe)

            def node_phase(phase, extra_rounds):
                kind = phase["kind"]

                def front(g):
                    g.wait_slot(own_in)
                    g.wait(own_kept, ago=2)
                    for t in range(TILES):
                        turned = pe.transpose(bank[g.turn][:, t * P:(t + 1) * P],
                                              own[:, g.slot, t * P:(t + 1) * P], ident[:, :])
                    turned.then_inc(own_turned.sem, 1)
                    g.wait_slot(msg_in)
                    g.wait(spread_set)
                    g.wait(agg_kept_v if kind == "relu" else agg_kept_a, ago=2)
                    agg = tiles(bank[2 + g.turn][:, 0:GN])
                    half = [agg[:, :, k * HALF:(k + 1) * HALF] for k in range(2)]
                    pe.matmul(half[0], msg[:, g.slot, 0, :], spread[:, g.slot, 0, :], start=True, stop=False)
                    if extra_rounds:
                        for k in range(2):
                            extra.rounds(g, k, lambda r, window: add_round(half[k]))
                    pe.matmul(half[1], msg[:, g.slot, 1, :], spread[:, g.slot, 1, :], start=False,
                              stop=True).then_inc(agg_made.sem, 1)

                def add_round(sums):
                    extra.wait((more_in, 16), (more_spread, 1))
                    pe.matmul(sums, x_msg[:, :], x_spread[:, :], start=False, stop=False) \
                        .then_inc(more_used, 1)

                def convolve(g):
                    g.wait(own_kept)
                    g.wait(agg_kept_v if kind == "relu" else agg_kept_a)
                    g.wait({"relu": relu_done, "unit": done_v, "unit_ln": unit_done, "ln": sum_res}[kind], ago=2)
                    o = bank[4 + g.turn][:, 0:GN]
                    pe.matmul(o, ones_b[:, :], bias_conv[:, phase["bias"], :], start=True, stop=False)
                    for t in range(TILES):
                        tile = slice(t * P, (t + 1) * P)
                        pe.matmul(o[:, tile], own_t[:, g.turn, tile], w(phase["wr"]), start=False, stop=False)
                        made = pe.matmul(o[:, tile], agg_t[:, g.turn, tile], w(phase["wl"]), start=False,
                                         stop=t == TILES - 1)
                    made.then_inc(out_made.sem, 1)

                def gates(g):
                    g.wait(own_kept)
                    g.wait(agg_kept_a)
                    g.wait(gates_done, ago=1)
                    o = pair[2]
                    pe.matmul(o[:, 0:4 * P], ones_b[:, :], bias_gate[:, :, :], start=True, stop=False)
                    pe.matmul(o[:, 4 * P:6 * P], ones_b[:, :], bias_gate[:, 0, :], start=True, stop=False)
                    k = WEIGHTS.index("Wg_self") * P
                    for t in range(TILES):
                        tile = slice(t * P, (t + 1) * P)
                        both = o[:, 2 * t * P:2 * (t + 1) * P]
                        pe.matmul(both, own_t[:, g.turn, tile], w_sb[:, k:k + 2 * P], start=False, stop=False)
                        made = pe.matmul(both, agg_t[:, g.turn, tile], w_sb[:, k + 2 * P:k + 4 * P],
                                         start=False, stop=t > 0)
                    made.then_inc(out_made.sem, 1)

                def step(g):
                    if g.below(NG - 1):
                        front(g + 1)
                    (gates if kind == "gate" else convolve)(g)

                front(first(pe, 0))
                each_group(pe, NG, 1, step)

            def edge_phase():
                def front(g):
                    g.wait_slot(own_in)
                    g.wait_slot(hs_in)
                    g.wait(own_kept, ago=2)
                    g.wait(agg_kept_v, ago=2)
                    for c in range(CH):
                        chunk = slice(c * P, (c + 1) * P)
                        pe.transpose(bank[g.turn][:, chunk], hs[:, g.slot, c, :], ident[:, :])
                        pe.transpose(bank[2 + g.turn][:, chunk], hd[:, g.slot, c, :], ident[:, :])
                        turned = pe.transpose(bank[4 + g.turn][0:DE, chunk], e_attr[:, g.slot, c, :], ident[:, :])
                    turned.then_inc(own_turned.sem, 1)

                def hidden(g):
                    g.wait(own_kept)
                    g.wait(agg_kept_v)
                    g.wait(hidden_done, ago=1)
                    pe.matmul(bank[6], w("W1_src"), hs_t[:, g.turn, :], start=True, stop=False)
                    pe.matmul(bank[6], w("W1_dst"), hd_t[:, g.turn, :], start=False, stop=False)
                    pe.matmul(bank[6], w("W1_edge")[0:DE, :], ea_t[:, g.turn, :], start=False, stop=True) \
                        .then_inc(out_made.sem, 1)

                def messages(g):
                    g.wait(hidden_done)
                    g.wait(done_v, ago=1)
                    pe.matmul(bank[7], ones_b[:, :], bias_edge[:, :], start=True, stop=False)
                    for c in range(CH):
                        chunk = slice(c * P, (c + 1) * P)
                        made = pe.matmul(bank[7][:, chunk], hidden_t[:, g.turn, chunk], w("L3_gnn_W2"),
                                         start=False, stop=c == CH - 1)
                    made.then_inc(messages_made.sem, 1)

                def step(g):
                    if g.below(NEG - 1):
                        front(g + 1)
                    hidden(g)
                    messages(g)

                front(first(pe, 0))
                each_group(pe, NEG, 1, step)

            walk(pe, lambda phase: edge_phase() if phase["kind"] == "edge" else
                 extra.choose(lambda extra_rounds: node_phase(phase, extra_rounds)))

        @block.vector
        def _(v):
            for c in DVE_COUNTS:
                v.sem_inc(c.sem, CREDIT)
            steps = [0]

            def then(ins):
                ins.then_inc(prep_v, 1)
                steps[0] += 1
                v.wait_ge(prep_v, steps[0])

            v.wait_ge(shaped, 1)
            for to, frm in ((pos_f, pos_i), (thr, thr_i), (edge_f, edge_i), (node_of_col, node_i), (win_base, base_i)):
                v.tensor_copy(to[:, :], frm[:, :])
            then(v.tensor_copy(part_f[:, :], part_i[:, :]))
            v.wait_ge(loaded, 16 * len(LOADS))
            for to, frm in ((dst_f, dst_i), (before_f, before_i)):
                v.tensor_copy(to[:, :], frm[:, :])
            then(v.tensor_copy(after_f[:, :], after_i[:, :]))
            v.tensor_tensor(before_f[:, :], dst_f[:, :], before_f[:, :], ALU.not_equal)
            then(v.tensor_tensor(after_f[:, :], dst_f[:, :], after_f[:, :], ALU.not_equal))
            v.tensor_tensor(before_f[:, :], before_f[:, :], pos_f[:, :], ALU.mult)
            then(v.tensor_scalar(junk[:, :], pos_f[:, :], 1.0 - OUTSIDE, None, ALU.add))
            then(v.tensor_tensor(after_f[:, :], after_f[:, :], junk[:, :], ALU.mult))
            then(v.tensor_scalar(after_f[:, :], after_f[:, :], float(OUTSIDE), None, ALU.add))
            v.tensor_tensor_scan(starts[:, :], before_f[:, :], before_f[:, :], 0.0, ALU.max, ALU.max)
            then(v.tensor_tensor_scan(ends[:, ::-1], after_f[:, ::-1], after_f[:, ::-1], float(OUTSIDE),
                                      ALU.min, ALU.min))
            v.sem_inc(cols_ready, 1)
            v.wait_ge(prep_t, 1)
            then(v.tensor_copy(line[:, :, :], bank[0][0:1, 0:3 * P].rearrange("o (k p) -> o k p", k=3)))
            v.tensor_tensor_scan(scanned[:, 0, :], line[:, 0, :], line[:, 0, :], 0.0, ALU.max, ALU.max)
            v.tensor_tensor_scan(scanned[:, 1, ::-1], line[:, 1, ::-1], line[:, 1, ::-1], float(OUTSIDE),
                                 ALU.min, ALU.min)
            v.memset(shifted[:, 0, 0:1], 0.0)
            then(v.memset(shifted[:, 1, P - 1:P], float(OUTSIDE)))
            v.tensor_copy(shifted[:, 0, 1:P], scanned[:, 0, 0:P - 1])
            v.tensor_copy(shifted[:, 1, 0:P - 1], scanned[:, 1, 1:P]).then_inc(rows_ready, 1)
            v.wait_ge(prep_t, 2)
            then(v.tensor_copy(carry[:, :], bank[1][:, 0:2]))
            v.tensor_scalar(starts[:, :], starts[:, :], carry[:, 0:1], None, ALU.max)
            then(v.tensor_scalar(ends[:, :], ends[:, :], carry[:, 1:2], None, ALU.min))
            then(v.tensor_tensor(ends[:, :], ends[:, :], starts[:, :], ALU.subtract))
            v.reciprocal(inv_rows[:, :], ends[:, :]).then_inc(inv_ready, 1)
            for t in range(WT):
                then(v.tensor_scalar(junk[:, 0:P], bank[1][:, P:2 * P], thr[:, t:t + 1], None, ALU.is_lt,
                                     ALU.add, accum_out=cnt[:, t:t + 1]))
            then(v.tensor_scalar(row_f[:, :], cnt[:, :], -1.0, 0.0, ALU.add, ALU.max))
            v.tensor_copy(row_i[:, :], row_f[:, :]).then_inc(rows_wanted, 1)
            for one, other in (("L1_gnn_b_neigh1", "L1_gnn_b_self1"), ("L1_gnn_b_neigh2", "L1_gnn_b_self2")):
                then(v.tensor_tensor(b(one), b(one), b(other), ALU.add))
            whole = b_sb[:, 0:NB * P]
            for k in range(3):
                v.tensor_scalar(mask[:, k:k + 1], part_f[:, :], float(k), None, ALU.is_equal)
            then(v.tensor_copy(hi[:, :], whole))
            then(v.tensor_tensor(rest_f[:, :], whole, hi[:, :], ALU.subtract))
            then(v.tensor_copy(mid[:, :], rest_f[:, :]))
            then(v.tensor_tensor(rest_f[:, :], rest_f[:, :], mid[:, :], ALU.subtract))
            then(v.tensor_copy(lo[:, :], rest_f[:, :]))
            then(v.tensor_scalar(hi[:, :], hi[:, :], mask[:, 0:1], None, ALU.mult))
            then(v.scalar_tensor_tensor(hi[:, :], mid[:, :], mask[:, 1:2], hi[:, :], ALU.mult, ALU.add))
            then(v.scalar_tensor_tensor(hi[:, :], lo[:, :], mask[:, 2:3], hi[:, :], ALU.mult, ALU.add))
            for k in range(6):
                for t in range(TILES):
                    v.tensor_copy(bias_conv[:, k, t * P:(t + 1) * P], hi[:, k * P:(k + 1) * P])
            for c in range(CH):
                v.tensor_copy(bias_edge[:, c * P:(c + 1) * P], hi[:, 6 * P:7 * P])
            for k in range(2):
                v.tensor_copy(bias_gate[:, k, :], hi[:, 7 * P:9 * P])
            v.wait_ge(rows_in, 16 * WT)
            then(v.tensor_copy(got_f[:, :, :], got_i[:, :, :]))
            for t in range(WT):
                then(v.tensor_scalar(junk[:, :], got_f[:, t, :], thr[:, t:t + 1], None, ALU.is_lt, ALU.add,
                                     accum_out=cnt[:, t:t + 1]))
            then(v.scalar_tensor_tensor(start_f[:, :], row_f[:, :], float(ROW), cnt[:, :], ALU.mult, ALU.add))
            v.tensor_copy(start_i[:, :], start_f[:, :]).then_inc(wins_wanted, 1)
            v.sem_inc(more_cols, 1)
            v.wait_ge(wins_in, 16 * 3 * WT)
            for t in range(WT):
                v.tensor_scalar(by_win[:, 2, t, :], win_dst[:, t, :], thr[:, t:t + 1], None, ALU.subtract)
                then(v.tensor_scalar(by_win[:, 1, t, :], edge_f[:, :], start_f[:, t:t + 1], None, ALU.add))
            then(v.tensor_scalar(skip[:, :, :], by_win[:, 2, :, :], float(WIN), float(OUTSIDE), ALU.is_ge,
                                 ALU.mult))
            v.tensor_tensor(by_win[:, 0, :, :], win_src[:, :, :], skip[:, :, :], ALU.add)
            v.tensor_tensor(by_win[:, 1, :, :], by_win[:, 1, :, :], skip[:, :, :], ALU.add) \
                .then_inc(wins_ready, 1)
            v.wait_ge(prep_t, 3)
            v.wait_ge(prep_t, 4)
            then(v.tensor_copy(start_line[:, :], bank[6][0:1, 0:WT * P]))
            v.tensor_copy(start_row[:, :], start_line[:, :])
            then(v.tensor_tensor(more_f[:, :], start_line[:, 1:NW + 1], start_line[:, 0:NW], ALU.subtract))
            then(v.tensor_scalar(more_i[:, :], more_f[:, :], float(P - 1), None, ALU.add))
            then(v.tensor_scalar(more_i[:, :], more_i[:, :], P.bit_length() - 1, None, ALU.arith_shift_right))
            then(v.tensor_scalar(more_f[:, :], more_i[:, :], -1.0, 0.0, ALU.add, ALU.max))
            then(v.tensor_reduce(most_f[:, :], more_f[:, :], AX_X, ALU.max))
            v.tensor_copy(more_row[:, :], more_f[:, :])
            v.tensor_copy(more_any[:, :], most_f[:, :])
            for k, table in enumerate((t_src, t_pos, t_dst, t_inv)):
                copied = v.tensor_copy(table[:, :], bank[2 + k][:, 0:WT * P])
            copied.then_inc(tables_ready, 1)
            v.wait_ge(tables_ready, 1)
            extra = Extra(v, more_passed_v)

            def spread_round(r, window):
                extra.wait((more_at, 48))
                v.tensor_tensor(x_local[:, :], x_dst[:, :], win_base[:, bass.ds(window, 1)], ALU.subtract) \
                    .then_inc(more_dst, 1)
                extra.wait((more_dst, 1))
                v.tensor_scalar(x_spread[:, :], node_of_col[:, :], x_local[:, :], x_inv[:, :], ALU.is_equal,
                                ALU.mult).then_inc(more_spread, 1)

            def more(g):
                for k in range(2):
                    extra.rounds(g, k, spread_round)

            def inc(ins, counted):
                ins.then_inc(counted.sem, 1)

            def node_phase(phase, extra_rounds):
                kind = phase["kind"]

                def build(g, k):
                    if k == 0:
                        g.wait(agg_made, ago=SLOTS)
                    at = bass.ds(g.number * 2 + k, 1)
                    return v.tensor_scalar(spread[:, g.slot, k, :], node_of_col[:, :], t_dst[:, at],
                                           t_inv[:, at], ALU.is_equal, ALU.mult)

                def build_both(g):
                    build(g, 0)
                    inc(build(g, 1), spread_set)

                def keep(g):
                    if kind == "relu":
                        g.wait(agg_made)
                        g.wait(out_made, ago=2)
                        inc(v.tensor_copy(agg_t[:, g.turn, :], bank[2 + g.turn][:, 0:GN]), agg_kept_v)

                def take_stats(rows, sums, counted):
                    sums()
                    for t in range(TILES):
                        taken = v.bn_stats(stats[:, t, :], rows[:, t * P:(t + 1) * P])
                    inc(taken, counted)

                def take_mv(counted):
                    for t in range(TILES):
                        taken = v.bn_aggr(mv[:, t, :], stats[:, t, :])
                    inc(taken, counted)

                def normalise(g, rows, scale):
                    g.wait_slot(out_left, ago=1)
                    for t in range(TILES):
                        tile = slice(t * P, (t + 1) * P)
                        last = v.tensor_scalar(done[:, g.slot, tile], rows[:, tile], mv[:, t, 0:1],
                                               scale[:, t:t + 1], ALU.subtract, ALU.mult)
                    inc(last, done_v)

                def step(g):
                    ahead = g.below(NG - LEAD)
                    made = bank[4 + g.turn][:, 0:GN]
                    if extra_rounds and g.below(NG - 1):
                        more(g + 1)
                    y, u, hb = (rows[:, g.turn, :] for rows in (y_all, u_all, hb_all))
                    if kind == "relu":
                        if ahead:
                            build_both(g + LEAD)
                        if g.below(NG - 1):
                            keep(g + 1)
                        return
                    if kind in ("unit", "unit_ln"):
                        g.wait(sq_done)
                        inc(v.tensor_reduce(sumsq[:, :], tiles(squares[:, g.turn, :]), AX_X, ALU.add), sum_done)
                        if ahead and kind == "unit":
                            build_both(g + LEAD)
                        g.wait(root_done)
                        inc(v.tensor_scalar(capped[:, :], root[:, :], NORM_EPS, None, ALU.max), cap_done)
                        g.wait(cap_done)
                        inc(v.reciprocal(rinv[:, :], capped[:, :]), rinv_done)
                        g.wait(rinv_done)
                        if kind == "unit":
                            g.wait_slot(out_left, ago=1)
                        rows = done[:, g.slot, :] if kind == "unit" else u
                        for t in range(TILES):
                            tile = slice(t * P, (t + 1) * P)
                            last = v.tensor_scalar(rows[:, tile], made[:, tile], rinv[:, t:t + 1], 0.0,
                                                   ALU.mult, ALU.max)
                        inc(last, done_v if kind == "unit" else unit_done)
                        if kind == "unit":
                            return
                        g.wait(unit_done)
                        g.wait_slot(res_in)
                        inc(v.tensor_tensor(y, u, res[:, g.slot, :], ALU.add), sum_res)
                    if kind == "ln":
                        g.wait(out_made)
                        g.wait_slot(res_in)
                        inc(v.tensor_tensor(y, made, res[:, g.slot, :], ALU.add), sum_res)
                        if ahead:
                            build(g + LEAD, 0)
                    if kind == "gate":
                        g.wait(gates_done)
                        h, gt, tr = own[:, g.slot, :], gate[:, g.turn, :], trans[:, g.turn, :]
                        inc(v.tensor_tensor(u, h, tr, ALU.subtract), diff_done)
                        if ahead:
                            build(g + LEAD, 0)
                        g.wait(diff_done)
                        inc(v.tensor_tensor(u, u, gt, ALU.mult), gated_done)
                        g.wait(gated_done)
                        inc(v.tensor_tensor(u, u, tr, ALU.add), upd_done)
                        take_stats(u, lambda: g.wait(upd_done), inner_stats)
                        g.wait(inner_stats)
                        beta = b("L3_gnn_beta").rearrange("p (o f) -> p o f", o=1).to_broadcast([P, TILES, P])
                        inc(v.tensor_tensor(tiles(hb), tiles(h), beta, ALU.add), beta_done)
                        take_mv(inner_mean)
                        g.wait(inner_mean)
                        inc(v.tensor_scalar(vpe[:, :], mv[:, :, 1], LN_EPS, None, ALU.add), inner_mv)
                        for t in range(TILES):
                            tile = slice(t * P, (t + 1) * P)
                            last = v.scalar_tensor_tensor(u[:, tile], u[:, tile], mv[:, t, 0:1],
                                                          b("L3_gnn_gamma"), ALU.subtract, ALU.mult)
                        inc(last, gamma_done)
                        g.wait(gamma_done)
                        g.wait(inner_pow)
                        for t in range(TILES):
                            tile = slice(t * P, (t + 1) * P)
                            last = v.scalar_tensor_tensor(y[:, tile], u[:, tile], rstd[:, t:t + 1],
                                                          hb[:, tile], ALU.mult, ALU.add)
                        inc(last, sum_res)
                    take_stats(y, lambda: g.wait(sum_res), stats_done)
                    g.wait(stats_done)
                    if ahead and kind == "unit_ln":
                        build(g + LEAD, 0)
                    if ahead:
                        inc(build(g + LEAD, 1), spread_set)
                    if kind == "gate":
                        take_mv(outer_mean)
                        g.wait(outer_mean)
                        inc(v.tensor_scalar(vpe[:, :], mv[:, :, 1], LN_EPS, None, ALU.add), mv_done)
                        g.wait(outer_pow)
                        normalise(g, y, rstd)
                        return
                    take_mv(mv_done)
                    g.wait(std_done)
                    inc(v.reciprocal(rstd[:, :], root_ln[:, :]), rstd_done)
                    g.wait(rstd_done)
                    normalise(g, y, rstd)

                for c in range(LEAD):
                    build_both(first(v, c))
                if extra_rounds:
                    more(first(v, 0))
                keep(first(v, 0))
                each_group(v, NG, LEAD, step)

            def edge_phase():
                def keep(g):
                    g.wait(own_turned)
                    g.wait(out_made, ago=2)
                    v.tensor_copy(hd_t[:, g.turn, :], bank[2 + g.turn])
                    inc(v.tensor_copy(ea_t[:, g.turn, :], bank[4 + g.turn][0:DE, :]), agg_kept_v)

                def step(g):
                    if g.below(NEG - 1):
                        keep(g + 1)
                    g.wait(messages_made)
                    g.wait_slot(out_left, ago=1)
                    inc(v.tensor_copy(e_out[:, g.slot, :, :].rearrange("p c f -> p (c f)"), bank[7]), done_v)

                keep(first(v, 0))
                each_group(v, NEG, 1, step)

            walk(v, lambda phase: edge_phase() if phase["kind"] == "edge" else
                 extra.choose(lambda extra_rounds: node_phase(phase, extra_rounds)))


def kernel(**inputs):
    import numpy as _np
    import concourse.bacc as _bacc
    from concourse import mybir as _mybir
    from concourse.bass_utils import run_bass_kernel_spmd as _run

    a = {name: _np.ascontiguousarray(value) for name, value in inputs.items()}
    dst = _np.concatenate([a["dst"], _np.full(EPAD - E, NP, a["dst"].dtype)])
    src = _np.concatenate([a["src"], _np.zeros(EPAD - E, a["src"].dtype)])
    before = _np.concatenate([_np.full(1, -1, dst.dtype), dst[:EP - 1]])

    def columns(edges):
        return edges[:EP].reshape(NEG, CH, P).transpose(2, 0, 1)

    w1, wg, wt = a["L3_gnn_W1"], a["L3_gnn_Wg"], a["L3_gnn_Wt"]
    made = {"W1_src": w1[:D], "W1_dst": w1[D:2 * D],
            "W1_edge": _np.concatenate([w1[2 * D:], _np.zeros((P - DE, D), w1.dtype)]),
            "Wg_self": wg[:D], "Wt_self": wt[:D], "Wg_agg": wg[D:], "Wt_agg": wt[D:]}
    turned = [n for n in WEIGHTS if n.startswith(("L1_", "L2_"))]
    weights = [made[n] if n in made else a[n].T if n in turned else a[n] for n in WEIGHTS]
    feeds = {
        "x": a["x"], "src_flat": src.reshape(-1, 1), "dst_flat": dst.reshape(-1, 1),
        "dst_before": before.reshape(P, ROW), "dst_after": dst[1:EP + 1].reshape(P, ROW),
        "edge_cols": _np.concatenate([columns(src), columns(dst)], axis=2).reshape(P, -1),
        "edge_attr": a["edge_attr_64"], "weights": _np.concatenate(weights, axis=1),
        "biases": _np.tile(_np.concatenate([a[n] for n in BIASES])[None, :], (P, 1)),
        "b1_col": a["L3_gnn_b1"].reshape(P, 1),
    }
    nc = _bacc.Bacc("TRN2", target_bir_lowering=False, num_devices=1)
    arrays, args = {}, []
    for name, value in feeds.items():
        value = _np.ascontiguousarray(value)
        arrays[f"in_{name}"] = value
        args.append(nc.dram_tensor(f"in_{name}", value.shape, _mybir.dt.from_np(value.dtype),
                                   kind="ExternalInput").ap())
    out = nc.dram_tensor("out_x", (N, D), F32, kind="ExternalOutput").ap()
    gnn_kernel(nc, *args, out)
    return _run(nc, [arrays], core_ids=[0]).results[0]["out_x"]
```

```python
from contextlib import ExitStack

import concourse.bass as bass
from concourse import mybir

F32 = mybir.dt.float32
BF16 = mybir.dt.bfloat16
I32 = mybir.dt.int32
ALU = mybir.AluOpType
ACT = mybir.ActivationFunctionType
AX_X = mybir.AxisListType.X

P = 128
N, D, E, DE = 50000, 128, 25000, 64
TILES = 3
GN = TILES * P
NG = -(-N // GN)
NP = NG * GN
WIN = GN // 2
HALF = WIN // TILES
NW = 2 * NG
WT = -(-NW // P)
ROW = -(-E // P)
EP = ROW * P
EPAD = EP + 2 * P
CH = 4
NEG = EP // P // CH
OUTSIDE = 1 << 20
SLOTS = 4
LEAD = 3
LN_EPS, NORM_EPS = 1e-5, 1e-12
CREDIT = 4

WEIGHTS = ["L0_gnn_W1_l", "L0_gnn_W1_r", "L0_gnn_W2_l", "L0_gnn_W2_r",
           "L1_gnn_W_neigh1", "L1_gnn_W_self1", "L1_gnn_W_neigh2", "L1_gnn_W_self2",
           "L2_gnn_W1_l", "L2_gnn_W1_r", "L2_gnn_W2_l", "L2_gnn_W2_r",
           "W1_src", "W1_dst", "W1_edge", "L3_gnn_W2", "Wg_self", "Wt_self", "Wg_agg", "Wt_agg"]
BIASES = ["L0_gnn_b1", "L0_gnn_b2", "L1_gnn_b_neigh1", "L1_gnn_b_neigh2", "L2_gnn_b1", "L2_gnn_b2",
          "L3_gnn_b2", "L3_gnn_bg", "L3_gnn_bt",
          "L1_gnn_b_self1", "L1_gnn_b_self2", "L3_gnn_gamma", "L3_gnn_beta"]
NB = 9


class Count:

    def __init__(self, sem, unit=1, start=0):
        self.sem, self.unit, self.base = sem, unit, start


class Group:

    def __init__(self, eng, it, c, kept):
        self.eng, self.it, self.c, self.kept = eng, it, c, kept

    def __add__(self, k):
        return Group(self.eng, self.it, self.c + k, self.kept)

    def __sub__(self, k):
        return self + -k

    @property
    def slot(self):
        return self.c % SLOTS

    @property
    def turn(self):
        return self.c % 2

    @property
    def number(self):
        return self.c if self.it is None else self.it * SLOTS + self.c

    def exists(self, n=NG):
        return self.it is not None or 0 <= self.c < n

    def value(self, unit, const):
        if self.it is None:
            return const
        if (unit, const) not in self.kept:
            self.kept[unit, const] = self.eng.snap(self.it * unit + const)
        return self.kept[unit, const]

    def wait(self, count, ago=0):
        const = count.base + count.unit * (self.c + 1 - ago)
        self.eng.wait_ge(count.sem, self.value(SLOTS * count.unit, const))

    def wait_slot(self, counts, ago=0):
        count = counts[self.slot]
        const = count.base + count.unit * (self.c // SLOTS + 1 - ago)
        self.eng.wait_ge(count.sem, self.value(count.unit, const))


def each_group(eng, n, ahead, step, behind=0):
    from_loop, loops = -(-behind // SLOTS), (n - ahead) // SLOTS
    for c in range(SLOTS * from_loop):
        step(Group(eng, None, c, {}))
    with eng.Fori(from_loop, loops) as it:
        kept = {}
        for c in range(SLOTS):
            step(Group(eng, it, c, kept))
    for c in range(SLOTS * loops, n + behind):
        step(Group(eng, None, c, {}))


def first(eng, c):
    return Group(eng, None, c, {})


def gnn_kernel(nc, x, src_flat, dst_flat, dst_before, dst_after, edge_cols, edge_attr, weights,
               biases, b1_col, out):
    ctx = ExitStack()
    with ctx:
        def sb(name, shape, dt=F32):
            return ctx.enter_context(nc.sbuf_tensor(name, shape, dt))

        def sem(name):
            return ctx.enter_context(nc.semaphore(name))

        def count(name, start=CREDIT):
            return Count(sem(name), 1, start)

        def ring(name, unit, start=0):
            return [Count(sem(f"{name}{s}"), unit, start) for s in range(SLOTS)]

        h1, x1, h2, x2, h3, x3 = [nc.dram_tensor(n, (NP, D), F32, kind="Internal").ap()
                                  for n in ("h1", "x1", "h2", "x2", "h3", "x3")]
        message_rows = nc.dram_tensor("message_rows", (EPAD, D), F32, kind="Internal").ap()
        inv_flat = nc.dram_tensor("inv_flat", (EPAD, 1), F32, kind="Internal").ap()

        w_sb = sb("w_sb", [P, len(WEIGHTS) * P])
        b_sb = sb("b_sb", [P, len(BIASES) * P])
        b1_sb = sb("b1_sb", [P, 1])
        bias_conv = sb("bias_conv", [P, 6, GN], BF16)
        bias_edge = sb("bias_edge", [P, CH * P], BF16)
        bias_gate = sb("bias_gate", [P, 2, 2 * P], BF16)
        ident = sb("ident", [P, P])
        ones_row = sb("ones_row", [1, P])
        ones_b = sb("ones_b", [P, P], BF16)
        node_of_col = sb("node_of_col", [P, WIN])
        eps_ln = sb("eps_ln", [P, 1])
        minus_half = sb("minus_half", [P, TILES])
        t_src = sb("t_src", [P, WT * P])
        t_pos = sb("t_pos", [P, WT * P])
        t_dst = sb("t_dst", [P, WT * P])
        t_inv = sb("t_inv", [P, WT * P])
        e_idx = sb("e_idx", [P, NEG * 2 * CH], I32)

        own = sb("own", [P, SLOTS, GN])
        res = sb("res", [P, SLOTS, GN])
        msg = sb("msg", [P, SLOTS, 2, P])
        spread = sb("spread", [P, SLOTS, 2, WIN])
        done = sb("done", [P, SLOTS, GN])
        idx = sb("idx", [P, SLOTS, 2 * CH], I32)
        own_t = sb("own_t", [P, 2, GN])
        agg_t = sb("agg_t", [P, 2, GN])
        squares = sb("squares", [P, 2, GN])
        positive = sb("positive", [P, SLOTS, GN])
        gate = sb("gate", [P, 2, GN])
        trans = sb("trans", [P, 2, GN])
        y_all = sb("y", [P, SLOTS, GN])
        u_all = sb("u", [P, SLOTS, GN])
        hb_all = sb("hb", [P, SLOTS, GN])
        stats_in = sb("stats_in", [P, SLOTS, TILES, 6])
        stats = sb("stats", [P, SLOTS, TILES, 6])
        mv_in = sb("mv_in", [P, SLOTS, TILES, 2])
        mv = sb("mv", [P, SLOTS, TILES, 2])
        sumsq = sb("sumsq", [P, SLOTS, TILES])
        root = sb("root", [P, SLOTS, TILES])
        root_ln = sb("root_ln", [P, SLOTS, TILES])
        capped = sb("capped", [P, TILES])
        rinv = sb("rinv", [P, TILES])
        rstd_in = sb("rstd_in", [P, SLOTS, TILES])
        rstd = sb("rstd", [P, SLOTS, TILES])
        vpe_in = sb("vpe_in", [P, SLOTS, TILES])
        vpe = sb("vpe", [P, SLOTS, TILES])
        shift = sb("shift", [P, SLOTS, TILES])
        e_attr = sb("e_attr", [P, SLOTS, CH, DE])
        hs = sb("hs", [P, SLOTS, CH, P])
        hd = sb("hd", [P, SLOTS, CH, P])
        hs_t = sb("hs_t", [P, 2, CH * P])
        hd_t = sb("hd_t", [P, 2, CH * P])
        ea_t = sb("ea_t", [DE, 2, CH * P])
        hidden_t = sb("hidden_t", [P, 2, CH * P])
        e_out = sb("e_out", [P, SLOTS, CH, P])

        pair = [ctx.enter_context(nc.psum_tensor(f"banks{2 * i}", [P, 1024], F32)) for i in range(4)]
        bank = [pair[i // 2][:, 512 * (i % 2):512 * (i % 2) + 512] for i in range(8)]

        def w(name):
            k = WEIGHTS.index(name)
            return w_sb[:, k * P:(k + 1) * P]

        def b(name):
            k = BIASES.index(name)
            return b_sb[:, k * P:(k + 1) * P]

        def tiles(ap):
            return ap.rearrange("p (t f) -> p t f", t=TILES)

        loaded = sem("loaded")
        shaped = sem("shaped")
        prep_v = sem("prep_v")
        cols_ready = sem("cols_ready")
        rows_ready = sem("rows_ready")
        prep_t = sem("prep_t")
        inv_ready = sem("inv_ready")
        inv_out = sem("inv_out")
        rows_wanted = sem("rows_wanted")
        rows_in = sem("rows_in")
        wins_wanted = sem("wins_wanted")
        wins_in = sem("wins_in")
        wins_ready = sem("wins_ready")
        tables_ready = sem("tables_ready")
        tail_in = sem("tail_in")
        tail_out = sem("tail_out")
        pad_out = sem("pad_out")
        more_cols = sem("more_cols")
        more_at = sem("more_at")
        more_in = sem("more_in")
        more_dst = sem("more_dst")
        more_spread = sem("more_spread")
        more_passed_pool, more_passed_pe, more_passed_v = [sem(f"more_passed_{e}") for e in ("pool", "pe", "v")]
        gathers_begun = sem("gathers_begun")
        more_used = sem("more_used")
        phase_done = sem("phase_done")

        own_in = ring("own_in", 16)
        res_in = ring("res_in", 16)
        msg_in = ring("msg_in", 32)
        hs_in = ring("hs_in", 32 * CH)
        out_left = ring("out_left", 16, 16)
        idx_set = count("idx_set")
        own_turned = count("own_turned")
        own_kept = count("own_kept")
        agg_made = count("agg_made")
        agg_kept_a = count("agg_kept_a")
        agg_kept_v = count("agg_kept_v")
        spread_set = count("spread_set")
        out_made = count("out_made")
        relu_done = count("relu_done")
        sq_done = count("sq_done")
        root_done = count("root_done")
        cap_done = count("cap_done")
        rinv_done = count("rinv_done")
        sum_res = count("sum_res")
        stats_done = count("stats_done")
        mv_done = count("mv_done")
        std_done = count("std_done")
        rstd_done = count("rstd_done")
        shift_done = count("shift_done")
        done_v = count("done_v")
        done_a = count("done_a")
        hidden_done = count("hidden_done")
        messages_made = count("messages_made")
        gates_done = count("gates_done")
        diff_done = count("diff_done")
        gated_done = count("gated_done")
        upd_done = count("upd_done")
        inner_stats = count("inner_stats")
        inner_mean = count("inner_mean")
        inner_mv = count("inner_mv")
        outer_mean = count("outer_mean")
        inner_pow = count("inner_pow")
        beta_done = count("beta_done")
        gamma_done = count("gamma_done")
        outer_pow = count("outer_pow")

        PHASES = [
            dict(kind="unit", own=x, res=None, out=h1, wl="L0_gnn_W1_l", wr="L0_gnn_W1_r", bias=0),
            dict(kind="unit_ln", own=h1, res=x, out=x1, wl="L0_gnn_W2_l", wr="L0_gnn_W2_r", bias=1),
            dict(kind="relu", own=x1, res=None, out=h2, wl="L1_gnn_W_neigh1", wr="L1_gnn_W_self1", bias=2),
            dict(kind="ln", own=h2, res=x1, out=x2, wl="L1_gnn_W_neigh2", wr="L1_gnn_W_self2", bias=3),
            dict(kind="relu", own=x2, res=None, out=h3, wl="L2_gnn_W1_l", wr="L2_gnn_W1_r", bias=4),
            dict(kind="ln", own=h3, res=x2, out=x3, wl="L2_gnn_W2_l", wr="L2_gnn_W2_r", bias=5),
            dict(kind="edge"),
            dict(kind="gate", own=x3, res=None, out=out),
        ]
        NODE = [idx_set, own_turned, own_kept, agg_made, spread_set, out_made]
        UNIT = [agg_kept_a, sq_done, root_done, cap_done, rinv_done]
        NORM = [sum_res, stats_done, mv_done]
        STEPS = {
            "unit": NODE + UNIT + [done_v],
            "unit_ln": NODE + UNIT + [std_done, rstd_done, done_v] + NORM,
            "relu": NODE + [agg_kept_v, relu_done],
            "ln": NODE + [agg_kept_a, std_done, rstd_done, done_v] + NORM,
            "edge": [idx_set, own_turned, own_kept, agg_kept_v, out_made, hidden_done, messages_made, done_v],
            "gate": NODE + [agg_kept_a, gates_done, diff_done, gated_done, upd_done, inner_stats,
                            inner_mean, inner_mv, inner_pow, beta_done, gamma_done, outer_mean,
                            outer_pow, shift_done, done_a] + NORM,
        }
        ACT_COUNTS = [idx_set, own_kept, agg_kept_a, sq_done, root_done, std_done, relu_done, hidden_done,
                      gates_done, done_a]
        DVE_COUNTS = [spread_set, agg_kept_v, cap_done, rinv_done, sum_res, shift_done,
                      stats_done, mv_done, rstd_done, done_v, diff_done, gated_done, upd_done,
                      inner_stats, inner_mean, inner_mv, outer_mean, beta_done, gamma_done]
        PE_COUNTS = [own_turned, agg_made, out_made, messages_made]
        POOL_COUNTS = [inner_pow, outer_pow]

        def walk(eng, program):
            for c in ACT_COUNTS + DVE_COUNTS + PE_COUNTS + POOL_COUNTS:
                c.base = CREDIT
            for r, start in ((own_in, 0), (res_in, 0), (msg_in, 0), (hs_in, 0), (out_left, 16)):
                for c in r:
                    c.base = start
            for ph, phase in enumerate(PHASES):
                if ph:
                    eng.wait_ge(phase_done, ph)
                program(phase)
                n = NEG if phase["kind"] == "edge" else NG
                for c in STEPS[phase["kind"]]:
                    c.base += n
                rings = [own_in, out_left, hs_in if phase["kind"] == "edge" else msg_in]
                for r in rings + ([res_in] if phase.get("res") is not None else []):
                    for s, c in enumerate(r):
                        c.base += c.unit * len(range(s, n, SLOTS))

        def of_group(table, g):
            rows = table.shape[0] // GN * GN
            return table[0:rows, :].rearrange("(g p t) f -> p g (t f)", p=P, t=TILES)[
                :, bass.ds(g.number, 1), :].rearrange("p g f -> p (g f)")

        def last_pieces(table, tile):
            at = (NG - 1) * GN
            whole, rest = divmod(N - at, TILES)
            assert rest
            return ((tile[0:whole, :],
                     table[at:at + whole * TILES, :].rearrange("(p t) f -> p (t f)", t=TILES)),
                    (tile[whole:whole + 1, 0:rest * D],
                     table[at + whole * TILES:N, :].rearrange("(p t) f -> p (t f)", t=rest)))

        def of_chunks(table, g):
            rows = CH * P
            whole = table.shape[0] // rows * rows
            return table[0:whole, :].rearrange("(g c p) f -> p (g c) f", p=P, c=CH)[
                :, bass.ds(g.number * CH, CH), :]

        start_row = sb("start_row", [1, WT * P], I32)
        more_row = sb("more_row", [1, NW], I32)
        more_any = sb("more_any", [1, 1], I32)
        x_zero = sb("x_zero", [P, (EPAD - EP) // P * D])
        x_src = sb("x_src", [P, 1], I32)
        x_dst = sb("x_dst", [P, 1], I32)
        x_inv = sb("x_inv", [P, 1])
        x_local = sb("x_local", [P, 1])
        x_msg = sb("x_msg", [P, P])
        x_spread = sb("x_spread", [P, WIN])
        win_base = sb("win_base", [P, NW])

        class Extra:

            def __init__(self, eng, passed):
                self.eng = eng
                self.most = eng.value_load(more_any[:, :], min_val=0, max_val=ROW)
                self.passed = passed
                self.item = eng.alloc_register("extra_item")
                eng.reg_mov(self.item, 0)

            def rounds(self, g, k, body):
                eng = self.eng
                window = g.number * 2 + k
                more = eng.value_load(more_row[:, bass.ds(window, 1)], min_val=0, max_val=ROW)
                with eng.If(more > 0):
                    with eng.Fori(0, more) as r:
                        eng.reg_add(self.item, self.item, 1)
                        body(r, window)
                    eng.nop()
                with eng.Else():
                    eng.nop()

            def choose(self, phase_program):
                with self.eng.If(self.most > 0):
                    phase_program(True)
                    self.eng.nop()
                with self.eng.Else():
                    phase_program(False)
                    self.eng.nop()

            def wait(self, *counted):
                eng = self.eng
                item = eng.snap(self.item, min_val=1, max_val=1 << 20)
                values = [eng.snap(item * unit) for _, unit in counted]
                for (one, _), value in zip(counted, values):
                    eng.wait_ge(one, value)
                eng.sem_inc(self.passed, 1)

        dst_i = sb("dst_i", [P, ROW], I32)
        before_i = sb("before_i", [P, ROW], I32)
        after_i = sb("after_i", [P, ROW], I32)
        pos_i = sb("pos_i", [P, ROW], I32)
        thr_i = sb("thr_i", [P, WT], I32)
        node_i = sb("node_i", [P, WIN], I32)
        edge_i = sb("edge_i", [P, P], I32)
        part_i = sb("part_i", [P, 1], I32)
        base_i = sb("base_i", [P, NW], I32)
        start_line = sb("start_line", [1, WT * P])
        more_f = sb("more_f", [1, NW])
        more_i = sb("more_i", [1, NW], I32)
        most_f = sb("most_f", [1, 1])
        dst_f = sb("dst_f", [P, ROW])
        before_f = sb("before_f", [P, ROW])
        after_f = sb("after_f", [P, ROW])
        pos_f = sb("pos_f", [P, ROW])
        thr = sb("thr", [P, WT])
        edge_f = sb("edge_f", [P, P])
        part_f = sb("part_f", [P, 1])
        starts = sb("starts", [P, ROW])
        ends = sb("ends", [P, ROW])
        inv_rows = sb("inv_rows", [P, ROW])
        line = sb("line", [1, 3, P])
        scanned = sb("scanned", [1, 2, P])
        shifted = sb("shifted", [1, 2, P])
        carry = sb("carry", [P, 2])
        junk = sb("junk", [P, ROW])
        cnt = sb("cnt", [P, WT])
        row_f = sb("row_f", [P, WT])
        row_i = sb("row_i", [P, WT], I32)
        got_i = sb("got_i", [P, WT, ROW], I32)
        got_f = sb("got_f", [P, WT, ROW])
        start_f = sb("start_f", [P, WT])
        start_i = sb("start_i", [P, WT], I32)
        win_dst = sb("win_dst", [P, WT, P], I32)
        win_src = sb("win_src", [P, WT, P], I32)
        win_inv = sb("win_inv", [P, WT, P])
        by_win = sb("by_win", [P, 3, WT, P])
        skip = sb("skip", [P, WT, P])
        mask = sb("mask", [P, 3])
        hi = sb("hi", [P, NB * P], BF16)
        mid = sb("mid", [P, NB * P], BF16)
        lo = sb("lo", [P, NB * P], BF16)
        rest_f = sb("rest_f", [P, NB * P])

        LOADS = [(dst_i[:, :], dst_flat[0:EP, :].rearrange("(p k) o -> p (k o)", p=P)),
                 (before_i[:, :], dst_before), (after_i[:, :], dst_after),
                 (b_sb[:, :], biases), (b1_sb[:, :], b1_col), (e_idx[:, :], edge_cols), (w_sb[:, :], weights)]

        block = ctx.enter_context(nc.Block())

        @block.sync
        def _(sp):
            for tile, source in LOADS:
                sp.dma_start(tile, source).then_inc(loaded, 16)
            sp.wait_ge(inv_ready, 1)
            sp.dma_start(inv_flat[0:EP, :].rearrange("(p k) o -> p (k o)", p=P), inv_rows[:, :]) \
                .then_inc(inv_out, 16)
            sp.dma_start(inv_flat[EP:EPAD, :].rearrange("(p k) o -> p (k o)", k=P), inv_rows[0:2, 0:P]) \
                .then_inc(inv_out, 16)
            sp.wait_ge(shaped, 3)
            sp.dma_start(message_rows[EP:EPAD, :].rearrange("(p k) f -> p (k f)", p=P),
                         x_zero[:, :]).then_inc(pad_out, 16)
            sp.wait_ge(pad_out, 16)
            for c in out_left:
                sp.sem_inc(c.sem, 16)
            tails = [0]

            def load_pieces(pieces, into):
                (to, source), (to_rest, source_rest) = pieces
                sp.dma_start(to, source).then_inc(tail_in, 16)
                tails[0] += 1
                sp.wait_ge(tail_in, 16 * tails[0])
                sp.dma_start(to_rest, source_rest).then_inc(into.sem, 16)

            def load(g, table, tile, into):
                if table is x and g.it is None and g.c == NG - 1:
                    load_pieces(last_pieces(x, tile), into)
                else:
                    sp.dma_start(tile, of_group(table, g)).then_inc(into.sem, 16)

            def stores_landed(n):
                for s, c in enumerate(out_left):
                    sp.wait_ge(c.sem, c.base + c.unit * len(range(s, n, SLOTS)))
                sp.sem_inc(phase_done, 1)

            def node_phase(phase):
                last_read = {"gate": beta_done}.get(phase["kind"], own_turned)
                result, late = {"relu": (relu_done, 0), "unit": (done_v, 1), "unit_ln": (done_v, 2),
                                "ln": (done_v, 1), "gate": (done_a, 2)}[phase["kind"]]

                def loads(g):
                    g.wait(last_read, ago=SLOTS)
                    load(g, phase["own"], own[:, g.slot, :], own_in[g.slot])
                    if phase["res"] is not None:
                        g.wait(sum_res, ago=SLOTS)
                        load(g, phase["res"], res[:, g.slot, :], res_in[g.slot])

                def step(g):
                    if (g + LEAD).exists():
                        loads(g + LEAD)
                    if (g - late).exists():
                        store(g - late)

                def store(g):
                    g.wait(result)
                    if phase["out"] is out and g.it is None and g.c == NG - 1:
                        (tile, rows), (tile_rest, rows_rest) = last_pieces(out, done[:, g.slot, :])
                        sp.dma_start(rows, tile).then_inc(tail_out, 16)
                        sp.dma_start(rows_rest, tile_rest).then_inc(out_left[g.slot].sem, 16)
                        sp.wait_ge(tail_out, 16)
                    else:
                        sp.dma_start(of_group(phase["out"], g), done[:, g.slot, :]) \
                            .then_inc(out_left[g.slot].sem, 16)

                for c in range(LEAD):
                    loads(first(sp, c))
                each_group(sp, NG, LEAD + 1, step, behind=late)
                stores_landed(NG)

            def edge_phase():
                def loads(g):
                    g.wait(own_turned, ago=SLOTS)
                    into = own_in[g.slot]
                    if g.it is None and g.c == NEG - 1:
                        at = g.c * CH * P
                        whole, rest = divmod(E - at, P)
                        split = at + whole * P
                        load_pieces(((e_attr[:, g.slot, 0:whole, :],
                                      edge_attr[at:split, :].rearrange("(c p) f -> p c f", p=P)),
                                     (e_attr[0:rest, g.slot, whole, :], edge_attr[split:E, :])), into)
                    else:
                        sp.dma_start(e_attr[:, g.slot, :, :], of_chunks(edge_attr, g)).then_inc(into.sem, 16)

                def step(g):
                    if (g + LEAD).exists(NEG):
                        loads(g + LEAD)
                    g.wait(done_v)
                    sp.dma_start(of_chunks(message_rows, g), e_out[:, g.slot, :, :]) \
                        .then_inc(out_left[g.slot].sem, 16)

                for c in range(LEAD):
                    loads(first(sp, c))
                each_group(sp, NEG, LEAD + 1, step)
                stores_landed(NEG)

            walk(sp, lambda phase: edge_phase() if phase["kind"] == "edge" else node_phase(phase))

        @block.gpsimd
        def _(pool):
            for c in POOL_COUNTS:
                pool.sem_inc(c.sem, CREDIT)
            pool.iota(pos_i[:, :], pattern=[[1, ROW]], base=0, channel_multiplier=ROW)
            pool.iota(thr_i[:, :], pattern=[[WIN * P, WT]], base=0, channel_multiplier=WIN)
            pool.iota(node_i[:, :], pattern=[[1, TILES], [TILES, HALF]], base=0, channel_multiplier=0)
            pool.iota(edge_i[:, :], pattern=[[1, P]], base=0, channel_multiplier=0)
            pool.iota(base_i[:, :], pattern=[[WIN, NW]], base=0, channel_multiplier=0)
            pool.iota(part_i[:, :], pattern=[[1, 1]], base=0, channel_multiplier=1).then_inc(shaped, 1)
            pool.memset(ident[:, :], 0.0).then_inc(shaped, 1)
            pool.memset(ones_row[:, :], 1.0)
            pool.memset(ones_b[:, :], 1.0)
            pool.memset(x_zero[:, :], 0.0)
            pool.memset(eps_ln[:, :], LN_EPS)
            pool.memset(minus_half[:, :], -0.5)
            pool.memset(msg[:, :, :, :], 0.0)
            pool.memset(hs[:, :, :, :], 0.0)
            pool.memset(hd[:, :, :, :], 0.0).then_inc(shaped, 1)
            pool.wait_ge(shaped, 3)
            pool.affine_select(out=ident[:, :], in_=ident[:, :], compare_op=ALU.not_equal, fill=1.0,
                               base=0, pattern=[[-1, P]], channel_multiplier=1).then_inc(shaped, 1)

            def fetch(into, table, at, bound, counted):
                pool.indirect_dma_start(into, None, table, bass.IndirectOffsetOnAxis(ap=at, axis=0),
                                        bounds_check=bound, oob_is_err=False) \
                    .then_inc(counted, 16)

            pool.wait_ge(rows_wanted, 1)
            dst_rows = dst_flat[0:EP, :].rearrange("(p k) o -> p (k o)", p=P)
            for t in range(WT):
                fetch(got_i[:, t, :], dst_rows, row_i[:, t:t + 1], P - 1, rows_in)
            pool.wait_ge(wins_wanted, 1)
            pool.wait_ge(inv_out, 32)
            for t in range(WT):
                for into, table in ((win_dst, dst_flat), (win_src, src_flat), (win_inv, inv_flat)):
                    fetch(into[:, t, :], table, start_i[:, t:t + 1], EPAD - P, wins_in)

            pool.wait_ge(tables_ready, 1)
            extra = Extra(pool, more_passed_pool)

            def node_phase(phase, extra_rounds):
                table = message_rows if phase["kind"] == "gate" else phase["own"]
                bound = (E if phase["kind"] == "gate" else N) - 1

                def gather(g):
                    g.wait(idx_set)
                    g.wait(agg_made, ago=SLOTS)
                    pool.sem_inc(gathers_begun, 1)
                    for k in range(2):
                        fetch(msg[:, g.slot, k, :], table, idx[:, g.slot, k:k + 1], bound, msg_in[g.slot].sem)

                def more(g):
                    for k in range(2):
                        extra.rounds(g, k, lambda r, window: fetch_round(r, window))

                def fetch_round(r, window):
                    start = pool.value_load(start_row[:, bass.ds(window, 1)], min_val=0, max_val=EP)
                    at = nc.s_assert_within(start + r * P + P, 0, EPAD - P)
                    extra.wait((more_used, 1))
                    pool.dma_start(x_dst[:, :], dst_flat[bass.ds(at, P), :]).then_inc(more_at, 16)
                    pool.dma_start(x_inv[:, :], inv_flat[bass.ds(at, P), :]).then_inc(more_at, 16)
                    if phase["kind"] == "gate":
                        pool.dma_start(x_msg[:, :], message_rows[bass.ds(at, P), :]).then_inc(more_at, 16)
                        extra.wait((more_at, 48))
                        pool.dma_start(x_src[:, :], src_flat[bass.ds(at, P), :]).then_inc(more_in, 16)
                    else:
                        pool.dma_start(x_src[:, :], src_flat[bass.ds(at, P), :]).then_inc(more_at, 16)
                        extra.wait((more_at, 48))
                        fetch(x_msg[:, :], table, x_src[:, :], N - 1, more_in)

                def power(g, variance, to, source, counted):
                    g.wait(variance)
                    pool.tensor_tensor(to[:, g.slot, :], source[:, g.slot, :], minus_half[:, :], ALU.pow) \
                        .then_inc(counted.sem, 1)

                def step(g):
                    if (g + LEAD).exists():
                        gather(g + LEAD)
                    if extra_rounds and (g + 1).exists():
                        more(g + 1)
                    if phase["kind"] == "gate" and g.exists():
                        power(g, inner_mv, rstd_in, vpe_in, inner_pow)
                    if phase["kind"] == "gate" and (g - 1).exists():
                        power(g - 1, mv_done, rstd, vpe, outer_pow)

                for c in range(LEAD):
                    gather(first(pool, c))
                if extra_rounds:
                    more(first(pool, 0))
                each_group(pool, NG, LEAD, step, behind=1 if phase["kind"] == "gate" else 0)

            def edge_phase():
                def gathers(g):
                    g.wait(idx_set)
                    g.wait(own_turned, ago=SLOTS)
                    pool.sem_inc(gathers_begun, 1)
                    for c in range(CH):
                        for k, rows in enumerate((hs, hd)):
                            at = k * CH + c
                            fetch(rows[:, g.slot, c, :], x3, idx[:, g.slot, at:at + 1], N - 1,
                                  hs_in[g.slot].sem)

                each_group(pool, NEG, 0, gathers)

            walk(pool, lambda phase: edge_phase() if phase["kind"] == "edge" else
                 extra.choose(lambda extra_rounds: node_phase(phase, extra_rounds)))

        @block.scalar
        def _(act):
            for c in ACT_COUNTS:
                act.sem_inc(c.sem, CREDIT)
            act.wait_ge(tables_ready, 1)

            def node_phase(phase):
                kind = phase["kind"]
                table = t_pos if kind == "gate" else t_src

                def stage(g):
                    act.activation(idx[:, g.slot, 0:2], table[:, bass.ds(g.number * 2, 2)], ACT.Copy) \
                        .then_inc(idx_set.sem, 1)

                def keep(g):
                    g.wait(own_turned)
                    g.wait(out_made, ago=2)
                    act.activation(own_t[:, g.turn, :], bank[g.turn][:, 0:GN], ACT.Copy).then_inc(own_kept.sem, 1)
                    if kind != "relu":
                        g.wait(agg_made)
                        act.activation(agg_t[:, g.turn, :], bank[2 + g.turn][:, 0:GN], ACT.Copy) \
                            .then_inc(agg_kept_a.sem, 1)

                def relu(g):
                    g.wait(out_made)
                    g.wait_slot(out_left, ago=1)
                    act.activation(done[:, g.slot, :], bank[4 + g.turn][:, 0:GN], ACT.Relu) \
                        .then_inc(relu_done.sem, 1)

                def norms(g):
                    made = bank[4 + g.turn][:, 0:GN]
                    g.wait(out_made)
                    g.wait(done_v if kind == "unit" else sum_res, ago=SLOTS)
                    act.activation(positive[:, g.slot, :], made, ACT.Relu)
                    for t in range(TILES):
                        squared = act.activation(squares[:, g.turn, t * P:(t + 1) * P], made[:, t * P:(t + 1) * P], ACT.Square,
                                                 accum_out=sumsq[:, g.slot, t:t + 1])
                    squared.then_inc(sq_done.sem, 1)
                    g.wait(sq_done)
                    act.activation(root[:, g.slot, :], sumsq[:, g.slot, :], ACT.Sqrt).then_inc(root_done.sem, 1)

                def deviation(g):
                    g.wait(mv_done)
                    act.activation(root_ln[:, g.slot, :], mv[:, g.slot, :, 1], ACT.Sqrt, bias=eps_ln[:, :]) \
                        .then_inc(std_done.sem, 1)

                def gates(g):
                    g.wait(out_made)
                    g.wait(upd_done, ago=2)
                    made = pair[2 + g.turn][:, 0:TILES * 2 * P].rearrange("p (t k f) -> p t k f", t=TILES, k=2)
                    act.activation(tiles(gate[:, g.turn, :]), made[:, :, 0, :], ACT.Sigmoid)
                    act.activation(tiles(trans[:, g.turn, :]), made[:, :, 1, :], ACT.Tanh) \
                        .then_inc(gates_done.sem, 1)

                def normalise(g):
                    g.wait(shift_done)
                    g.wait_slot(out_left, ago=1)
                    for t in range(TILES):
                        tile = slice(t * P, (t + 1) * P)
                        last = act.activation(done[:, g.slot, tile], y_all[:, g.slot, tile], ACT.Identity,
                                              scale=rstd[:, g.slot, t:t + 1], bias=shift[:, g.slot, t:t + 1])
                    last.then_inc(done_a.sem, 1)

                def step(g):
                    if (g + 1).exists():
                        keep(g + 1)
                    if (g + SLOTS).exists():
                        g.wait(agg_made)
                        stage(g + SLOTS)
                    late = {"ln": 1, "unit_ln": 2}.get(kind)
                    if late and (g - late).exists():
                        deviation(g - late)
                    if g.exists():
                        {"relu": relu, "unit": norms, "unit_ln": norms, "gate": gates}.get(kind, lambda g: None)(g)
                    if kind == "gate" and (g - 2).exists():
                        normalise(g - 2)

                for c in range(SLOTS):
                    stage(first(act, c))
                keep(first(act, 0))
                each_group(act, NG, SLOTS, step, behind={"ln": 1, "unit_ln": 2, "gate": 2}.get(kind, 0))

            def edge_phase():
                def stage(g):
                    act.activation(idx[:, g.slot, :], e_idx[:, bass.ds(g.number * 2 * CH, 2 * CH)], ACT.Copy) \
                        .then_inc(idx_set.sem, 1)

                def keep(g):
                    g.wait(own_turned)
                    g.wait(out_made, ago=2)
                    act.activation(hs_t[:, g.turn, :], bank[g.turn], ACT.Copy).then_inc(own_kept.sem, 1)

                def step(g):
                    if (g + 1).exists(NEG):
                        keep(g + 1)
                    if (g + SLOTS).exists(NEG):
                        g.wait(own_turned)
                        stage(g + SLOTS)
                    g.wait(out_made)
                    g.wait(messages_made, ago=2)
                    act.activation(hidden_t[:, g.turn, :], bank[6], ACT.Silu, bias=b1_sb[:, :]) \
                        .then_inc(hidden_done.sem, 1)

                for c in range(SLOTS):
                    stage(first(act, c))
                keep(first(act, 0))
                each_group(act, NEG, SLOTS, step)

            walk(act, lambda phase: edge_phase() if phase["kind"] == "edge" else node_phase(phase))

        @block.tensor
        def _(pe):
            for c in PE_COUNTS:
                pe.sem_inc(c.sem, CREDIT)
            pe.wait_ge(shaped, 4)
            pe.wait_ge(cols_ready, 1)
            for k, col in enumerate((starts[:, ROW - 1:ROW], ends[:, 0:1], dst_f[:, 0:1])):
                turned = pe.transpose(bank[0][0:1, k * P:(k + 1) * P], col, ident[:, :])
            turned.then_inc(prep_t, 1)
            pe.wait_ge(rows_ready, 1)
            for k in range(2):
                pe.matmul(bank[1][:, k:k + 1], shifted[:, k, :], ones_row[:, 0:1], start=True, stop=True)
            pe.matmul(bank[1][:, P:2 * P], ones_row[:, :], line[:, 2, :], start=True, stop=True) \
                .then_inc(prep_t, 1)
            pe.wait_ge(wins_ready, 1)
            for k in range(4):
                for t in range(WT):
                    source = by_win[:, k, t, :] if k < 3 else win_inv[:, t, :]
                    turned = pe.transpose(bank[2 + k][:, t * P:(t + 1) * P], source, ident[:, :])
            turned.then_inc(prep_t, 1)
            pe.wait_ge(more_cols, 1)
            for t in range(WT):
                turned = pe.transpose(bank[6][0:1, t * P:(t + 1) * P], start_f[:, t:t + 1], ident[:, :])
            turned.then_inc(prep_t, 1)
            pe.wait_ge(tables_ready, 1)
            pe.sem_inc(more_used, 1)
            extra = Extra(pe, more_passed_pe)

            def node_phase(phase, extra_rounds):
                kind = phase["kind"]

                def front(g):
                    g.wait_slot(own_in)
                    g.wait(own_kept, ago=2)
                    for t in range(TILES):
                        turned = pe.transpose(bank[g.turn][:, t * P:(t + 1) * P],
                                              own[:, g.slot, t * P:(t + 1) * P], ident[:, :])
                    turned.then_inc(own_turned.sem, 1)
                    g.wait_slot(msg_in)
                    g.wait(spread_set)
                    g.wait(agg_kept_v if kind == "relu" else agg_kept_a, ago=2)
                    agg = tiles(bank[2 + g.turn][:, 0:GN])
                    half = [agg[:, :, k * HALF:(k + 1) * HALF] for k in range(2)]
                    pe.matmul(half[0], msg[:, g.slot, 0, :], spread[:, g.slot, 0, :], start=True, stop=False)
                    if extra_rounds:
                        for k in range(2):
                            extra.rounds(g, k, lambda r, window: add_round(half[k]))
                    pe.matmul(half[1], msg[:, g.slot, 1, :], spread[:, g.slot, 1, :], start=False,
                              stop=True).then_inc(agg_made.sem, 1)

                def add_round(sums):
                    extra.wait((more_in, 16), (more_spread, 1))
                    pe.matmul(sums, x_msg[:, :], x_spread[:, :], start=False, stop=False) \
                        .then_inc(more_used, 1)

                def convolve(g):
                    g.wait(own_kept)
                    g.wait(agg_kept_v if kind == "relu" else agg_kept_a)
                    g.wait({"relu": relu_done, "unit": sq_done, "unit_ln": sq_done, "ln": sum_res}[kind], ago=2)
                    o = bank[4 + g.turn][:, 0:GN]
                    pe.matmul(o, ones_b[:, :], bias_conv[:, phase["bias"], :], start=True, stop=False)
                    for t in range(TILES):
                        tile = slice(t * P, (t + 1) * P)
                        pe.matmul(o[:, tile], own_t[:, g.turn, tile], w(phase["wr"]), start=False, stop=False)
                        made = pe.matmul(o[:, tile], agg_t[:, g.turn, tile], w(phase["wl"]), start=False,
                                         stop=t == TILES - 1)
                    made.then_inc(out_made.sem, 1)

                def gates(g):
                    g.wait(own_kept)
                    g.wait(agg_kept_a)
                    g.wait(gates_done, ago=2)
                    o = pair[2 + g.turn]
                    pe.matmul(o[:, 0:4 * P], ones_b[:, :], bias_gate[:, :, :], start=True, stop=False)
                    pe.matmul(o[:, 4 * P:6 * P], ones_b[:, :], bias_gate[:, 0, :], start=True, stop=False)
                    k = WEIGHTS.index("Wg_self") * P
                    for t in range(TILES):
                        tile = slice(t * P, (t + 1) * P)
                        both = o[:, 2 * t * P:2 * (t + 1) * P]
                        pe.matmul(both, own_t[:, g.turn, tile], w_sb[:, k:k + 2 * P], start=False, stop=False)
                        made = pe.matmul(both, agg_t[:, g.turn, tile], w_sb[:, k + 2 * P:k + 4 * P],
                                         start=False, stop=t > 0)
                    made.then_inc(out_made.sem, 1)

                def step(g):
                    if (g + 1).exists():
                        front(g + 1)
                    (gates if kind == "gate" else convolve)(g)

                front(first(pe, 0))
                each_group(pe, NG, 1, step)

            def edge_phase():
                def front(g):
                    g.wait_slot(own_in)
                    g.wait_slot(hs_in)
                    g.wait(own_kept, ago=2)
                    g.wait(agg_kept_v, ago=2)
                    for c in range(CH):
                        chunk = slice(c * P, (c + 1) * P)
                        pe.transpose(bank[g.turn][:, chunk], hs[:, g.slot, c, :], ident[:, :])
                        pe.transpose(bank[2 + g.turn][:, chunk], hd[:, g.slot, c, :], ident[:, :])
                        turned = pe.transpose(bank[4 + g.turn][0:DE, chunk], e_attr[:, g.slot, c, :], ident[:, :])
                    turned.then_inc(own_turned.sem, 1)

                def hidden(g):
                    g.wait(own_kept)
                    g.wait(agg_kept_v)
                    g.wait(hidden_done, ago=1)
                    pe.matmul(bank[6], w("W1_src"), hs_t[:, g.turn, :], start=True, stop=False)
                    pe.matmul(bank[6], w("W1_dst"), hd_t[:, g.turn, :], start=False, stop=False)
                    pe.matmul(bank[6], w("W1_edge")[0:DE, :], ea_t[:, g.turn, :], start=False, stop=True) \
                        .then_inc(out_made.sem, 1)

                def messages(g):
                    g.wait(hidden_done)
                    g.wait(done_v, ago=1)
                    pe.matmul(bank[7], ones_b[:, :], bias_edge[:, :], start=True, stop=False)
                    for c in range(CH):
                        chunk = slice(c * P, (c + 1) * P)
                        made = pe.matmul(bank[7][:, chunk], hidden_t[:, g.turn, chunk], w("L3_gnn_W2"),
                                         start=False, stop=c == CH - 1)
                    made.then_inc(messages_made.sem, 1)

                def step(g):
                    if (g + 1).exists(NEG):
                        front(g + 1)
                    hidden(g)
                    messages(g)

                front(first(pe, 0))
                each_group(pe, NEG, 1, step)

            walk(pe, lambda phase: edge_phase() if phase["kind"] == "edge" else
                 extra.choose(lambda extra_rounds: node_phase(phase, extra_rounds)))

        @block.vector
        def _(v):
            for c in DVE_COUNTS:
                v.sem_inc(c.sem, CREDIT)
            steps = [0]

            def then(ins):
                ins.then_inc(prep_v, 1)
                steps[0] += 1
                v.wait_ge(prep_v, steps[0])

            v.wait_ge(shaped, 1)
            for to, frm in ((pos_f, pos_i), (thr, thr_i), (edge_f, edge_i), (node_of_col, node_i), (win_base, base_i)):
                v.tensor_copy(to[:, :], frm[:, :])
            then(v.tensor_copy(part_f[:, :], part_i[:, :]))
            v.wait_ge(loaded, 16 * len(LOADS))
            for to, frm in ((dst_f, dst_i), (before_f, before_i)):
                v.tensor_copy(to[:, :], frm[:, :])
            then(v.tensor_copy(after_f[:, :], after_i[:, :]))
            v.tensor_tensor(before_f[:, :], dst_f[:, :], before_f[:, :], ALU.not_equal)
            then(v.tensor_tensor(after_f[:, :], dst_f[:, :], after_f[:, :], ALU.not_equal))
            v.tensor_tensor(before_f[:, :], before_f[:, :], pos_f[:, :], ALU.mult)
            then(v.tensor_scalar(junk[:, :], pos_f[:, :], 1.0 - OUTSIDE, None, ALU.add))
            then(v.tensor_tensor(after_f[:, :], after_f[:, :], junk[:, :], ALU.mult))
            then(v.tensor_scalar(after_f[:, :], after_f[:, :], float(OUTSIDE), None, ALU.add))
            v.tensor_tensor_scan(starts[:, :], before_f[:, :], before_f[:, :], 0.0, ALU.max, ALU.max)
            then(v.tensor_tensor_scan(ends[:, ::-1], after_f[:, ::-1], after_f[:, ::-1], float(OUTSIDE),
                                      ALU.min, ALU.min))
            v.sem_inc(cols_ready, 1)
            v.wait_ge(prep_t, 1)
            then(v.tensor_copy(line[:, :, :], bank[0][0:1, 0:3 * P].rearrange("o (k p) -> o k p", k=3)))
            v.tensor_tensor_scan(scanned[:, 0, :], line[:, 0, :], line[:, 0, :], 0.0, ALU.max, ALU.max)
            v.tensor_tensor_scan(scanned[:, 1, ::-1], line[:, 1, ::-1], line[:, 1, ::-1], float(OUTSIDE),
                                 ALU.min, ALU.min)
            v.memset(shifted[:, 0, 0:1], 0.0)
            then(v.memset(shifted[:, 1, P - 1:P], float(OUTSIDE)))
            v.tensor_copy(shifted[:, 0, 1:P], scanned[:, 0, 0:P - 1])
            v.tensor_copy(shifted[:, 1, 0:P - 1], scanned[:, 1, 1:P]).then_inc(rows_ready, 1)
            v.wait_ge(prep_t, 2)
            then(v.tensor_copy(carry[:, :], bank[1][:, 0:2]))
            v.tensor_scalar(starts[:, :], starts[:, :], carry[:, 0:1], None, ALU.max)
            then(v.tensor_scalar(ends[:, :], ends[:, :], carry[:, 1:2], None, ALU.min))
            then(v.tensor_tensor(ends[:, :], ends[:, :], starts[:, :], ALU.subtract))
            v.reciprocal(inv_rows[:, :], ends[:, :]).then_inc(inv_ready, 1)
            for t in range(WT):
                then(v.tensor_scalar(junk[:, 0:P], bank[1][:, P:2 * P], thr[:, t:t + 1], None, ALU.is_lt,
                                     ALU.add, accum_out=cnt[:, t:t + 1]))
            then(v.tensor_scalar(row_f[:, :], cnt[:, :], -1.0, 0.0, ALU.add, ALU.max))
            v.tensor_copy(row_i[:, :], row_f[:, :]).then_inc(rows_wanted, 1)
            for one, other in (("L1_gnn_b_neigh1", "L1_gnn_b_self1"), ("L1_gnn_b_neigh2", "L1_gnn_b_self2")):
                then(v.tensor_tensor(b(one), b(one), b(other), ALU.add))
            whole = b_sb[:, 0:NB * P]
            for k in range(3):
                v.tensor_scalar(mask[:, k:k + 1], part_f[:, :], float(k), None, ALU.is_equal)
            then(v.tensor_copy(hi[:, :], whole))
            then(v.tensor_tensor(rest_f[:, :], whole, hi[:, :], ALU.subtract))
            then(v.tensor_copy(mid[:, :], rest_f[:, :]))
            then(v.tensor_tensor(rest_f[:, :], rest_f[:, :], mid[:, :], ALU.subtract))
            then(v.tensor_copy(lo[:, :], rest_f[:, :]))
            then(v.tensor_scalar(hi[:, :], hi[:, :], mask[:, 0:1], None, ALU.mult))
            then(v.scalar_tensor_tensor(hi[:, :], mid[:, :], mask[:, 1:2], hi[:, :], ALU.mult, ALU.add))
            then(v.scalar_tensor_tensor(hi[:, :], lo[:, :], mask[:, 2:3], hi[:, :], ALU.mult, ALU.add))
            for k in range(6):
                for t in range(TILES):
                    v.tensor_copy(bias_conv[:, k, t * P:(t + 1) * P], hi[:, k * P:(k + 1) * P])
            for c in range(CH):
                v.tensor_copy(bias_edge[:, c * P:(c + 1) * P], hi[:, 6 * P:7 * P])
            for k in range(2):
                v.tensor_copy(bias_gate[:, k, :], hi[:, 7 * P:9 * P])
            v.wait_ge(rows_in, 16 * WT)
            then(v.tensor_copy(got_f[:, :, :], got_i[:, :, :]))
            for t in range(WT):
                then(v.tensor_scalar(junk[:, :], got_f[:, t, :], thr[:, t:t + 1], None, ALU.is_lt, ALU.add,
                                     accum_out=cnt[:, t:t + 1]))
            then(v.scalar_tensor_tensor(start_f[:, :], row_f[:, :], float(ROW), cnt[:, :], ALU.mult, ALU.add))
            v.tensor_copy(start_i[:, :], start_f[:, :]).then_inc(wins_wanted, 1)
            v.sem_inc(more_cols, 1)
            v.wait_ge(wins_in, 16 * 3 * WT)
            for t in range(WT):
                v.tensor_scalar(by_win[:, 2, t, :], win_dst[:, t, :], thr[:, t:t + 1], None, ALU.subtract)
                then(v.tensor_scalar(by_win[:, 1, t, :], edge_f[:, :], start_f[:, t:t + 1], None, ALU.add))
            then(v.tensor_scalar(skip[:, :, :], by_win[:, 2, :, :], float(WIN), float(OUTSIDE), ALU.is_ge,
                                 ALU.mult))
            v.tensor_tensor(by_win[:, 0, :, :], win_src[:, :, :], skip[:, :, :], ALU.add)
            v.tensor_tensor(by_win[:, 1, :, :], by_win[:, 1, :, :], skip[:, :, :], ALU.add) \
                .then_inc(wins_ready, 1)
            v.wait_ge(prep_t, 3)
            v.wait_ge(prep_t, 4)
            then(v.tensor_copy(start_line[:, :], bank[6][0:1, 0:WT * P]))
            v.tensor_copy(start_row[:, :], start_line[:, :])
            then(v.tensor_tensor(more_f[:, :], start_line[:, 1:NW + 1], start_line[:, 0:NW], ALU.subtract))
            then(v.tensor_scalar(more_i[:, :], more_f[:, :], float(P - 1), None, ALU.add))
            then(v.tensor_scalar(more_i[:, :], more_i[:, :], P.bit_length() - 1, None, ALU.arith_shift_right))
            then(v.tensor_scalar(more_f[:, :], more_i[:, :], -1.0, 0.0, ALU.add, ALU.max))
            then(v.tensor_reduce(most_f[:, :], more_f[:, :], AX_X, ALU.max))
            v.tensor_copy(more_row[:, :], more_f[:, :])
            v.tensor_copy(more_any[:, :], most_f[:, :])
            for k, table in enumerate((t_src, t_pos, t_dst, t_inv)):
                copied = v.tensor_copy(table[:, :], bank[2 + k][:, 0:WT * P])
            copied.then_inc(tables_ready, 1)
            v.wait_ge(tables_ready, 1)
            extra = Extra(v, more_passed_v)

            def spread_round(r, window):
                extra.wait((more_at, 48))
                v.tensor_tensor(x_local[:, :], x_dst[:, :], win_base[:, bass.ds(window, 1)], ALU.subtract) \
                    .then_inc(more_dst, 1)
                extra.wait((more_dst, 1))
                v.tensor_scalar(x_spread[:, :], node_of_col[:, :], x_local[:, :], x_inv[:, :], ALU.is_equal,
                                ALU.mult).then_inc(more_spread, 1)

            def more(g):
                for k in range(2):
                    extra.rounds(g, k, spread_round)

            def inc(ins, counted):
                ins.then_inc(counted.sem, 1)

            def node_phase(phase, extra_rounds):
                kind = phase["kind"]

                def build(g, k):
                    if k == 0:
                        g.wait(agg_made, ago=SLOTS)
                    at = bass.ds(g.number * 2 + k, 1)
                    return v.tensor_scalar(spread[:, g.slot, k, :], node_of_col[:, :], t_dst[:, at],
                                           t_inv[:, at], ALU.is_equal, ALU.mult)

                def build_both(g):
                    build(g, 0)
                    inc(build(g, 1), spread_set)

                def keep(g):
                    if kind == "relu":
                        g.wait(agg_made)
                        g.wait(out_made, ago=2)
                        inc(v.tensor_copy(agg_t[:, g.turn, :], bank[2 + g.turn][:, 0:GN]), agg_kept_v)

                def unit_rows(g):
                    g.wait(root_done)
                    inc(v.tensor_scalar(capped[:, :], root[:, g.slot, :], NORM_EPS, None, ALU.max), cap_done)
                    g.wait(cap_done)
                    inc(v.reciprocal(rinv[:, :], capped[:, :]), rinv_done)
                    g.wait(rinv_done)
                    if kind == "unit":
                        g.wait_slot(out_left, ago=1)
                    else:
                        g.wait_slot(res_in)
                    for t in range(TILES):
                        tile = slice(t * P, (t + 1) * P)
                        if kind == "unit":
                            last = v.tensor_scalar(done[:, g.slot, tile], positive[:, g.slot, tile],
                                                   rinv[:, t:t + 1], None, ALU.mult)
                        else:
                            last = v.scalar_tensor_tensor(y_all[:, g.slot, tile], positive[:, g.slot, tile],
                                                          rinv[:, t:t + 1], res[:, g.slot, tile], ALU.mult, ALU.add)
                    inc(last, done_v if kind == "unit" else sum_res)

                def add_residual(g):
                    g.wait(out_made)
                    g.wait_slot(res_in)
                    inc(v.tensor_tensor(y_all[:, g.slot, :], bank[4 + g.turn][:, 0:GN], res[:, g.slot, :], ALU.add),
                        sum_res)

                def take_stats(g, rows, to, written, counted):
                    g.wait(written)
                    for t in range(TILES):
                        taken = v.bn_stats(to[:, g.slot, t, :], rows[:, g.slot, t * P:(t + 1) * P])
                    inc(taken, counted)

                def take_moments(g, to, source, taken, between, counted):
                    g.wait(taken)
                    between()
                    for t in range(TILES):
                        last = v.bn_aggr(to[:, g.slot, t, :], source[:, g.slot, t, :])
                    inc(last, counted)

                def normalise(g):
                    g.wait(std_done)
                    inc(v.reciprocal(rstd[:, g.slot, :], root_ln[:, g.slot, :]), rstd_done)
                    g.wait(rstd_done)
                    g.wait_slot(out_left, ago=1)
                    for t in range(TILES):
                        tile = slice(t * P, (t + 1) * P)
                        last = v.tensor_scalar(done[:, g.slot, tile], y_all[:, g.slot, tile], mv[:, g.slot, t, 0:1],
                                               rstd[:, g.slot, t:t + 1], ALU.subtract, ALU.mult)
                    inc(last, done_v)

                def update(g):
                    h, gt, tr, u = own[:, g.slot, :], gate[:, g.turn, :], trans[:, g.turn, :], u_all[:, g.slot, :]
                    g.wait(gates_done)
                    inc(v.tensor_tensor(u, h, tr, ALU.subtract), diff_done)
                    g.wait(diff_done)
                    inc(v.tensor_tensor(u, u, gt, ALU.mult), gated_done)
                    g.wait(gated_done)
                    inc(v.tensor_tensor(u, u, tr, ALU.add), upd_done)

                def add_beta(g):
                    beta = b("L3_gnn_beta").rearrange("p (o f) -> p o f", o=1).to_broadcast([P, TILES, P])
                    inc(v.tensor_tensor(tiles(hb_all[:, g.slot, :]), tiles(own[:, g.slot, :]), beta, ALU.add), beta_done)

                def inner_norm(g):
                    g.wait(inner_mean)
                    inc(v.tensor_scalar(vpe_in[:, g.slot, :], mv_in[:, g.slot, :, 1], LN_EPS, None, ALU.add), inner_mv)
                    u = u_all[:, g.slot, :]
                    for t in range(TILES):
                        tile = slice(t * P, (t + 1) * P)
                        last = v.scalar_tensor_tensor(u[:, tile], u[:, tile], mv_in[:, g.slot, t, 0:1],
                                                      b("L3_gnn_gamma"), ALU.subtract, ALU.mult)
                    inc(last, gamma_done)

                def add_own(g):
                    g.wait(gamma_done)
                    g.wait(inner_pow)
                    g.wait(done_a, ago=SLOTS)
                    for t in range(TILES):
                        tile = slice(t * P, (t + 1) * P)
                        last = v.scalar_tensor_tensor(y_all[:, g.slot, tile], u_all[:, g.slot, tile],
                                                      rstd_in[:, g.slot, t:t + 1], hb_all[:, g.slot, tile],
                                                      ALU.mult, ALU.add)
                    inc(last, sum_res)

                def outer_variance(g):
                    g.wait(outer_mean)
                    inc(v.tensor_scalar(vpe[:, g.slot, :], mv[:, g.slot, :, 1], LN_EPS, None, ALU.add), mv_done)

                def outer_shift(g):
                    g.wait(outer_pow)
                    inc(v.scalar_tensor_tensor(shift[:, g.slot, :], mv[:, g.slot, :, 0], -1.0, rstd[:, g.slot, :],
                                               ALU.mult, ALU.mult), shift_done)

                def step(g):
                    ahead = (g + LEAD).exists()

                    def build_first():
                        if ahead:
                            build(g + LEAD, 0)

                    def build_second():
                        if ahead:
                            inc(build(g + LEAD, 1), spread_set)

                    if extra_rounds and (g + 1).exists():
                        more(g + 1)
                    if kind == "relu":
                        build_first()
                        build_second()
                        if (g + 1).exists():
                            keep(g + 1)
                    if kind == "unit":
                        build_first()
                        build_second()
                        if (g - 1).exists():
                            unit_rows(g - 1)
                    if kind == "unit_ln":
                        build_first()
                        if (g - 1).exists():
                            unit_rows(g - 1)
                        if (g - 2).exists():
                            normalise(g - 2)
                        if (g - 1).exists():
                            take_stats(g - 1, y_all, stats, sum_res, stats_done)
                            take_moments(g - 1, mv, stats, stats_done, build_second, mv_done)
                        else:
                            build_second()
                    if kind == "ln":
                        if g.exists():
                            add_residual(g)
                        build_first()
                        if (g - 1).exists():
                            normalise(g - 1)
                        if g.exists():
                            take_stats(g, y_all, stats, sum_res, stats_done)
                            take_moments(g, mv, stats, stats_done, build_second, mv_done)
                    if kind == "gate":
                        if g.exists():
                            update(g)
                            add_beta(g)
                        if (g - 2).exists():
                            outer_shift(g - 2)
                        if g.exists():
                            take_stats(g, u_all, stats_in, upd_done, inner_stats)
                            take_moments(g, mv_in, stats_in, inner_stats, build_first, inner_mean)
                        if (g - 1).exists():
                            add_own(g - 1)
                        if g.exists():
                            inner_norm(g)
                        if (g - 1).exists():
                            take_stats(g - 1, y_all, stats, sum_res, stats_done)
                            take_moments(g - 1, mv, stats, stats_done, build_second, outer_mean)
                            outer_variance(g - 1)
                        else:
                            build_second()

                for c in range(LEAD):
                    build_both(first(v, c))
                if extra_rounds:
                    more(first(v, 0))
                keep(first(v, 0))
                each_group(v, NG, LEAD, step, behind={"unit": 1, "unit_ln": 2, "ln": 1, "gate": 2}.get(kind, 0))

            def edge_phase():
                def keep(g):
                    g.wait(own_turned)
                    g.wait(out_made, ago=2)
                    v.tensor_copy(hd_t[:, g.turn, :], bank[2 + g.turn])
                    inc(v.tensor_copy(ea_t[:, g.turn, :], bank[4 + g.turn][0:DE, :]), agg_kept_v)

                def step(g):
                    if (g + 1).exists(NEG):
                        keep(g + 1)
                    g.wait(messages_made)
                    g.wait_slot(out_left, ago=1)
                    inc(v.tensor_copy(e_out[:, g.slot, :, :].rearrange("p c f -> p (c f)"), bank[7]), done_v)

                keep(first(v, 0))
                each_group(v, NEG, 1, step)

            walk(v, lambda phase: edge_phase() if phase["kind"] == "edge" else
                 extra.choose(lambda extra_rounds: node_phase(phase, extra_rounds)))


def kernel(**inputs):
    import numpy as _np
    import concourse.bacc as _bacc
    from concourse import mybir as _mybir
    from concourse.bass_utils import run_bass_kernel_spmd as _run

    a = {name: _np.ascontiguousarray(value) for name, value in inputs.items()}
    dst = _np.concatenate([a["dst"], _np.full(EPAD - E, NP, a["dst"].dtype)])
    src = _np.concatenate([a["src"], _np.zeros(EPAD - E, a["src"].dtype)])
    before = _np.concatenate([_np.full(1, -1, dst.dtype), dst[:EP - 1]])

    def columns(edges):
        return edges[:EP].reshape(NEG, CH, P).transpose(2, 0, 1)

    w1, wg, wt = a["L3_gnn_W1"], a["L3_gnn_Wg"], a["L3_gnn_Wt"]
    made = {"W1_src": w1[:D], "W1_dst": w1[D:2 * D],
            "W1_edge": _np.concatenate([w1[2 * D:], _np.zeros((P - DE, D), w1.dtype)]),
            "Wg_self": wg[:D], "Wt_self": wt[:D], "Wg_agg": wg[D:], "Wt_agg": wt[D:]}
    turned = [n for n in WEIGHTS if n.startswith(("L1_", "L2_"))]
    weights = [made[n] if n in made else a[n].T if n in turned else a[n] for n in WEIGHTS]
    feeds = {
        "x": a["x"], "src_flat": src.reshape(-1, 1), "dst_flat": dst.reshape(-1, 1),
        "dst_before": before.reshape(P, ROW), "dst_after": dst[1:EP + 1].reshape(P, ROW),
        "edge_cols": _np.concatenate([columns(src), columns(dst)], axis=2).reshape(P, -1),
        "edge_attr": a["edge_attr_64"], "weights": _np.concatenate(weights, axis=1),
        "biases": _np.tile(_np.concatenate([a[n] for n in BIASES])[None, :], (P, 1)),
        "b1_col": a["L3_gnn_b1"].reshape(P, 1),
    }
    nc = _bacc.Bacc("TRN2", target_bir_lowering=False, num_devices=1)
    arrays, args = {}, []
    for name, value in feeds.items():
        value = _np.ascontiguousarray(value)
        arrays[f"in_{name}"] = value
        args.append(nc.dram_tensor(f"in_{name}", value.shape, _mybir.dt.from_np(value.dtype),
                                   kind="ExternalInput").ap())
    out = nc.dram_tensor("out_x", (N, D), F32, kind="ExternalOutput").ap()
    gnn_kernel(nc, *args, out)
    return _run(nc, [arrays], core_ids=[0]).results[0]["out_x"]
```

```python
from contextlib import ExitStack

import concourse.bass as bass
from concourse import mybir

F32 = mybir.dt.float32
BF16 = mybir.dt.bfloat16
I32 = mybir.dt.int32
ALU = mybir.AluOpType
ACT = mybir.ActivationFunctionType
AX_X = mybir.AxisListType.X

P = 128
N, D, E, DE = 50000, 128, 25000, 64
TILES = 3
GN = TILES * P
NG = -(-N // GN)
NP = NG * GN
WIN = GN // 2
HALF = WIN // TILES
NW = 2 * NG
WT = -(-NW // P)
ROW = -(-E // P)
EP = ROW * P
EPAD = EP + 2 * P
CH = 4
NEG = EP // P // CH
DVE_TILES = 1
OUTSIDE = 1 << 20
SLOTS = 4
LEAD = 3
INNER_LAG, SUM_LAG, SQUARES_LAG, OUTER_LAG, RESULT_LAG = 1, 2, 3, 4, 5
SPREADS = 3
EDGE_STEPS = -(-NG // SPREADS)
LN_EPS, NORM_EPS = 1e-5, 1e-12
CREDIT = 4

WEIGHTS = ["L0_gnn_W1_l", "L0_gnn_W1_r", "L0_gnn_W2_l", "L0_gnn_W2_r",
           "L1_gnn_W_neigh1", "L1_gnn_W_self1", "L1_gnn_W_neigh2", "L1_gnn_W_self2",
           "L2_gnn_W1_l", "L2_gnn_W1_r", "L2_gnn_W2_l", "L2_gnn_W2_r",
           "W1_src", "W1_dst", "W1_edge", "L3_gnn_W2", "Wg_self", "Wt_self", "Wg_agg", "Wt_agg"]
BIASES = ["L0_gnn_b1", "L0_gnn_b2", "L1_gnn_b_neigh1", "L1_gnn_b_neigh2", "L2_gnn_b1", "L2_gnn_b2",
          "L3_gnn_b2", "L3_gnn_bg", "L3_gnn_bt",
          "L1_gnn_b_self1", "L1_gnn_b_self2", "L3_gnn_gamma", "L3_gnn_beta"]
NB = 9


class Count:

    def __init__(self, sem, unit=1, start=0):
        self.sem, self.unit, self.base = sem, unit, start


class Group:

    def __init__(self, eng, it, c, kept, per=SLOTS):
        self.eng, self.it, self.c, self.kept, self.per = eng, it, c, kept, per

    def __add__(self, k):
        return Group(self.eng, self.it, self.c + k, self.kept, self.per)

    def times(self, n):
        return Group(self.eng, self.it, n * self.c, self.kept, n * self.per)

    def __sub__(self, k):
        return self + -k

    @property
    def slot(self):
        return self.c % SLOTS

    @property
    def turn(self):
        return self.c % 2

    @property
    def number(self):
        return self.c if self.it is None else self.it * self.per + self.c

    def exists(self, n=NG):
        return self.it is not None or 0 <= self.c < n

    def value(self, unit, const):
        if self.it is None:
            return const
        if (unit, const) not in self.kept:
            self.kept[unit, const] = self.eng.snap(self.it * unit + const)
        return self.kept[unit, const]

    def wait(self, *counts, ago=0):
        values = [self.value(self.per * count.unit, count.base + count.unit * (self.c + 1 - ago)) for count in counts]
        for count, value in zip(counts, values):
            self.eng.wait_ge(count.sem, value)

    def wait_slot(self, counts, ago=0):
        count = counts[self.slot]
        const = count.base + count.unit * (self.c // SLOTS + 1 - ago)
        self.eng.wait_ge(count.sem, self.value(self.per // SLOTS * count.unit, const))


def each_group(eng, n, ahead, step, behind=0):
    from_loop, loops = -(-behind // SLOTS), (n - ahead) // SLOTS
    for c in range(SLOTS * from_loop):
        step(Group(eng, None, c, {}))
    with eng.Fori(0, loops - from_loop) as it:
        kept = {}
        for c in range(SLOTS * from_loop, SLOTS * (from_loop + 1)):
            step(Group(eng, it, c, kept))
    for c in range(SLOTS * loops, n + behind):
        step(Group(eng, None, c, {}))


def first(eng, c):
    return Group(eng, None, c, {})


def gnn_kernel(nc, x, src_flat, dst_flat, dst_before, dst_after, edge_cols, edge_attr, weights,
               biases, b1_col, out):
    ctx = ExitStack()
    with ctx:
        def sb(name, shape, dt=F32):
            return ctx.enter_context(nc.sbuf_tensor(name, shape, dt))

        def sem(name):
            return ctx.enter_context(nc.semaphore(name))

        def count(name, start=CREDIT):
            return Count(sem(name), 1, start)

        def ring(name, unit, start=0):
            return [Count(sem(f"{name}{s}"), unit, start) for s in range(SLOTS)]

        h1, x1, h2, x2, h3, x3 = [nc.dram_tensor(n, (NP, D), F32, kind="Internal").ap()
                                  for n in ("h1", "x1", "h2", "x2", "h3", "x3")]
        message_rows = nc.dram_tensor("message_rows", (EPAD, D), F32, kind="Internal").ap()
        spread_rows = nc.dram_tensor("spread_rows", (SPREADS * EDGE_STEPS * GN, D), F32, kind="Internal").ap()
        inv_flat = nc.dram_tensor("inv_flat", (EPAD, 1), F32, kind="Internal").ap()

        w_sb = sb("w_sb", [P, len(WEIGHTS) * P])
        b_sb = sb("b_sb", [P, len(BIASES) * P])
        b1_sb = sb("b1_sb", [P, 1])
        bias_conv = sb("bias_conv", [P, 6, GN], BF16)
        bias_edge = sb("bias_edge", [P, CH * P], BF16)
        bias_gate = sb("bias_gate", [P, 2, 2 * P], BF16)
        ident = sb("ident", [P, P])
        ones_row = sb("ones_row", [1, P])
        ones_b = sb("ones_b", [P, P], BF16)
        node_of_col = sb("node_of_col", [P, WIN])
        eps_ln = sb("eps_ln", [P, 1])
        minus_half = sb("minus_half", [P, 2, TILES])
        t_src = sb("t_src", [P, WT * P])
        t_dst = sb("t_dst", [P, WT * P])
        t_inv = sb("t_inv", [P, WT * P])
        e_idx = sb("e_idx", [P, NEG * 2 * CH], I32)

        own = sb("own", [P, SLOTS, GN])
        res = sb("res", [P, SLOTS, GN])
        msg = sb("msg", [P, SLOTS, 2, P])
        spread = sb("spread", [P, SLOTS, 2, WIN])
        done = sb("done", [P, SLOTS, GN])
        idx = sb("idx", [P, SLOTS, 2 * CH], I32)
        own_t = sb("own_t", [P, 2, GN])
        agg_t = sb("agg_t", [P, 2, GN])
        squares = sb("squares", [P, 2, GN])
        positive = sb("positive", [P, SLOTS, GN])
        gate = sb("gate", [P, 2, GN])
        trans = sb("trans", [P, 2, GN])
        y_all = sb("y", [P, SLOTS, GN])
        u_all = sb("u", [P, SLOTS, GN])
        hb = sb("hb", [P, SLOTS, GN])
        stats_in = sb("stats_in", [P, SLOTS, TILES, 6])
        stats = sb("stats", [P, SLOTS, TILES, 6])
        sums = sb("sums", [P, SLOTS, TILES])
        less_mean = sb("less_mean", [P, SLOTS, TILES])
        mv_in = sb("mv_in", [P, SLOTS, TILES, 2])
        mv = sb("mv", [P, SLOTS, TILES, 2])
        sumsq = sb("sumsq", [P, SLOTS, TILES])
        root = sb("root", [P, SLOTS, TILES])
        root_ln = sb("root_ln", [P, SLOTS, TILES])
        capped = sb("capped", [P, TILES])
        rinv = sb("rinv", [P, TILES])
        rstd = sb("rstd", [P, SLOTS, TILES])
        variances = sb("variances", [P, SLOTS, 2, TILES])
        powers = sb("powers", [P, SLOTS, 2, TILES])
        shift = sb("shift", [P, SLOTS, TILES])
        e_attr = sb("e_attr", [P, SLOTS, CH, DE])
        hs = sb("hs", [P, SLOTS, CH, P])
        hd = sb("hd", [P, SLOTS, CH, P])
        hs_t = sb("hs_t", [P, 2, CH * P])
        hd_t = sb("hd_t", [P, 2, CH * P])
        ea_t = sb("ea_t", [DE, 2, CH * P])
        hidden_t = sb("hidden_t", [P, 2, CH * P])
        e_out = sb("e_out", [P, SLOTS, CH, P])

        pair = [ctx.enter_context(nc.psum_tensor(f"banks{2 * i}", [P, 1024], F32)) for i in range(4)]
        bank = [pair[i // 2][:, 512 * (i % 2):512 * (i % 2) + 512] for i in range(8)]

        def w(name):
            k = WEIGHTS.index(name)
            return w_sb[:, k * P:(k + 1) * P]

        def b(name):
            k = BIASES.index(name)
            return b_sb[:, k * P:(k + 1) * P]

        def tiles(ap):
            return ap.rearrange("p (t f) -> p t f", t=TILES)

        loaded = sem("loaded")
        weights_in = sem("weights_in")
        shaped = sem("shaped")
        prep_v = sem("prep_v")
        cols_ready = sem("cols_ready")
        rows_ready = sem("rows_ready")
        prep_t = sem("prep_t")
        inv_ready = sem("inv_ready")
        inv_out = sem("inv_out")
        rows_wanted = sem("rows_wanted")
        rows_in = sem("rows_in")
        wins_wanted = sem("wins_wanted")
        wins_in = sem("wins_in")
        wins_ready = sem("wins_ready")
        tables_ready = sem("tables_ready")
        tail_in = sem("tail_in")
        tail_out = sem("tail_out")
        pad_out = sem("pad_out")
        more_cols = sem("more_cols")
        more_at = sem("more_at")
        more_in = sem("more_in")
        more_dst = sem("more_dst")
        more_spread = sem("more_spread")
        more_passed_pool, more_passed_pe, more_passed_v = [sem(f"more_passed_{e}") for e in ("pool", "pe", "v")]
        table_in = sem("table_in")
        stores_begun = sem("stores_begun")
        gathers_begun = sem("gathers_begun")
        more_used = sem("more_used")
        phase_done = sem("phase_done")

        own_in = ring("own_in", 16)
        res_in = ring("res_in", 16)
        msg_in = ring("msg_in", 32)
        windows_in = ring("windows_in", 32)
        hs_in = ring("hs_in", 32 * CH)
        out_left = ring("out_left", 16, 16)
        spread_left = ring("spread_left", 16, 16)
        spread_in = ring("spread_in", 16)
        idx_set = count("idx_set")
        own_turned = count("own_turned")
        own_kept = count("own_kept")
        agg_made = count("agg_made")
        agg_kept_a = count("agg_kept_a")
        agg_kept_v = count("agg_kept_v")
        spread_set = count("spread_set")
        out_made = count("out_made")
        biased_done = count("biased_done")
        relu_done = count("relu_done")
        sq_done = count("sq_done")
        root_done = count("root_done")
        cap_done = count("cap_done")
        rinv_done = count("rinv_done")
        sum_res = count("sum_res")
        stats_done = count("stats_done")
        mv_done = count("mv_done")
        std_done = count("std_done")
        rstd_done = count("rstd_done")
        shift_done = count("shift_done")
        done_v = count("done_v")
        done_a = count("done_a")
        hidden_done = count("hidden_done")
        messages_made = count("messages_made")
        gates_done = count("gates_done")
        diff_done = count("diff_done")
        gated_done = count("gated_done")
        upd_done = count("upd_done")
        inner_stats = count("inner_stats")
        inner_mean = count("inner_mean")
        beta_done = count("beta_done")
        gamma_done = count("gamma_done")
        mean_done = count("mean_done")
        variances_set = count("variances_set")
        powers_done = count("powers_done")

        PHASES = [
            dict(kind="unit", own=x, res=None, out=h1, wl="L0_gnn_W1_l", wr="L0_gnn_W1_r", bias=0),
            dict(kind="unit_ln", own=h1, res=x, out=x1, wl="L0_gnn_W2_l", wr="L0_gnn_W2_r", bias=1),
            dict(kind="relu", own=x1, res=None, out=h2, wl="L1_gnn_W_neigh1", wr="L1_gnn_W_self1", bias=2),
            dict(kind="ln", own=h2, res=x1, out=x2, wl="L1_gnn_W_neigh2", wr="L1_gnn_W_self2", bias=3),
            dict(kind="relu", own=x2, res=None, out=h3, wl="L2_gnn_W1_l", wr="L2_gnn_W1_r", bias=4),
            dict(kind="ln", own=h3, res=x2, out=x3, wl="L2_gnn_W2_l", wr="L2_gnn_W2_r", bias=5),
            dict(kind="edge"),
            dict(kind="gate", own=x3, res=None, out=out),
        ]
        NODE = [idx_set, own_turned, own_kept, agg_made, spread_set, out_made]
        UNIT = [agg_kept_a, sq_done, root_done, cap_done, rinv_done]
        NORM = [sum_res, stats_done, mv_done]
        STEPS = {
            "unit": NODE + UNIT + [done_v],
            "unit_ln": NODE + UNIT + [std_done, rstd_done, shift_done, done_v, done_a] + NORM,
            "relu": NODE + [agg_kept_v, biased_done, relu_done],
            "ln": NODE + [agg_kept_a, std_done, rstd_done, shift_done, done_a] + NORM,
            "edge": [idx_set, own_turned, own_kept, agg_kept_v, out_made, hidden_done, messages_made, done_v],
            "gate": [],
        }
        ACT_COUNTS = [idx_set, own_kept, agg_kept_a, sq_done, root_done, std_done, relu_done, hidden_done,
                      gates_done, done_a]
        DVE_COUNTS = [spread_set, agg_kept_v, biased_done, cap_done, rinv_done, sum_res, shift_done,
                      stats_done, mv_done, rstd_done, done_v, gated_done, upd_done,
                      inner_stats, inner_mean, mean_done, variances_set, gamma_done]
        PE_COUNTS = [own_turned, agg_made, out_made, messages_made]
        POOL_COUNTS = [beta_done, diff_done, powers_done]

        def walk(eng, program):
            for c in ACT_COUNTS + DVE_COUNTS + PE_COUNTS + POOL_COUNTS:
                c.base = CREDIT
            for r, start in ((own_in, 0), (res_in, 0), (msg_in, 0), (hs_in, 0), (out_left, 16),
                             (spread_left, 16), (spread_in, 0), (windows_in, 0)):
                for c in r:
                    c.base = start
            for ph, phase in enumerate(PHASES):
                if ph:
                    eng.wait_ge(phase_done, ph)
                program(phase)
                n = NEG if phase["kind"] == "edge" else NG
                for c in STEPS[phase["kind"]]:
                    c.base += n
                if phase["kind"] == "edge":
                    spread_set.base += SPREADS * EDGE_STEPS
                rings = [own_in, out_left, hs_in if phase["kind"] == "edge" else msg_in]
                for r in rings + ([res_in] if phase.get("res") is not None else []):
                    for s, c in enumerate(r):
                        c.base += c.unit * len(range(s, n, SLOTS))

        def both_norms(g):
            inner, outer = (g - INNER_LAG).exists(), (g - OUTER_LAG).exists()
            return slice(0 if inner else 1, 2 if outer else 1) if inner or outer else None

        def of_group(table, g):
            rows = table.shape[0] // GN * GN
            return table[0:rows, :].rearrange("(g p t) f -> p g (t f)", p=P, t=TILES)[
                :, bass.ds(g.number, 1), :].rearrange("p g f -> p (g f)")

        def last_pieces(table, tile):
            at = (NG - 1) * GN
            whole, rest = divmod(N - at, TILES)
            assert rest
            return ((tile[0:whole, :],
                     table[at:at + whole * TILES, :].rearrange("(p t) f -> p (t f)", t=TILES)),
                    (tile[whole:whole + 1, 0:rest * D],
                     table[at + whole * TILES:N, :].rearrange("(p t) f -> p (t f)", t=rest)))

        def of_chunks(table, g):
            rows = CH * P
            whole = table.shape[0] // rows * rows
            return table[0:whole, :].rearrange("(g c p) f -> p (g c) f", p=P, c=CH)[
                :, bass.ds(g.number * CH, CH), :]

        start_row = sb("start_row", [1, WT * P], I32)
        more_row = sb("more_row", [1, NW], I32)
        more_any = sb("more_any", [1, 1], I32)
        x_zero = sb("x_zero", [P, (EPAD - EP) // P * D])
        x_src = sb("x_src", [P, 1], I32)
        x_dst = sb("x_dst", [P, 1], I32)
        x_inv = sb("x_inv", [P, 1])
        x_local = sb("x_local", [P, 1])
        x_msg = sb("x_msg", [P, P])
        x_spread = sb("x_spread", [P, WIN])
        win_base = sb("win_base", [P, NW])

        class Extra:

            def __init__(self, eng, passed):
                self.eng = eng
                self.most = eng.value_load(more_any[:, :], min_val=0, max_val=ROW)
                self.passed = passed
                self.item = eng.alloc_register("extra_item")
                eng.reg_mov(self.item, 0)

            def rounds(self, g, k, body):
                eng = self.eng
                window = g.number * 2 + k
                more = eng.value_load(more_row[:, bass.ds(window, 1)], min_val=0, max_val=ROW)
                with eng.If(more > 0):
                    with eng.Fori(0, more) as r:
                        eng.reg_add(self.item, self.item, 1)
                        body(r, window)
                    eng.nop()
                with eng.Else():
                    eng.nop()

            def choose(self, phase_program):
                with self.eng.If(self.most > 0):
                    phase_program(True)
                    self.eng.nop()
                with self.eng.Else():
                    phase_program(False)
                    self.eng.nop()

            def wait(self, *counted):
                eng = self.eng
                item = eng.snap(self.item, min_val=1, max_val=1 << 20)
                values = [eng.snap(item * unit) for _, unit in counted]
                for (one, _), value in zip(counted, values):
                    eng.wait_ge(one, value)
                eng.sem_inc(self.passed, 1)

        dst_i = sb("dst_i", [P, ROW], I32)
        before_i = sb("before_i", [P, ROW], I32)
        after_i = sb("after_i", [P, ROW], I32)
        pos_i = sb("pos_i", [P, ROW], I32)
        thr_i = sb("thr_i", [P, WT], I32)
        node_i = sb("node_i", [P, WIN], I32)
        part_i = sb("part_i", [P, 1], I32)
        base_i = sb("base_i", [P, NW], I32)
        start_line = sb("start_line", [1, WT * P])
        more_f = sb("more_f", [1, NW])
        more_i = sb("more_i", [1, NW], I32)
        most_f = sb("most_f", [1, 1])
        dst_f = sb("dst_f", [P, ROW])
        before_f = sb("before_f", [P, ROW])
        after_f = sb("after_f", [P, ROW])
        pos_f = sb("pos_f", [P, ROW])
        thr = sb("thr", [P, WT])
        part_f = sb("part_f", [P, 1])
        starts = sb("starts", [P, ROW])
        ends = sb("ends", [P, ROW])
        inv_rows = sb("inv_rows", [P, ROW])
        line = sb("line", [1, 3, P])
        scanned = sb("scanned", [1, 2, P])
        shifted = sb("shifted", [1, 2, P])
        carry = sb("carry", [P, 2])
        junk = sb("junk", [P, ROW])
        cnt = sb("cnt", [P, WT])
        row_f = sb("row_f", [P, WT])
        row_i = sb("row_i", [P, WT], I32)
        got_i = sb("got_i", [P, WT, ROW], I32)
        got_f = sb("got_f", [P, WT, ROW])
        start_f = sb("start_f", [P, WT])
        start_i = sb("start_i", [P, WT], I32)
        win_dst = sb("win_dst", [P, WT, P], I32)
        win_src = sb("win_src", [P, WT, P], I32)
        win_inv = sb("win_inv", [P, WT, P])
        by_win = sb("by_win", [P, 2, WT, P])
        skip = sb("skip", [P, WT, P])
        mask = sb("mask", [P, 3])
        hi = sb("hi", [P, NB * P], BF16)
        mid = sb("mid", [P, NB * P], BF16)
        lo = sb("lo", [P, NB * P], BF16)
        rest_f = sb("rest_f", [P, NB * P])

        LOADS = [(dst_i[:, :], dst_flat[0:EP, :].rearrange("(p k) o -> p (k o)", p=P)),
                 (before_i[:, :], dst_before), (after_i[:, :], dst_after)]
        LATER_LOADS = [(b_sb[:, :], biases), (b1_sb[:, :], b1_col), (e_idx[:, :], edge_cols),
                       (w_sb[:, :], weights)]

        block = ctx.enter_context(nc.Block())

        @block.sync
        def _(sp):
            for tile, source in LOADS:
                sp.dma_start(tile, source).then_inc(loaded, 16)
            for tile, source in LATER_LOADS:
                sp.dma_start(tile, source).then_inc(weights_in, 16)
            sp.wait_ge(inv_ready, 1)
            sp.dma_start(inv_flat[0:EP, :].rearrange("(p k) o -> p (k o)", p=P), inv_rows[:, :]) \
                .then_inc(inv_out, 16)
            sp.dma_start(inv_flat[EP:EPAD, :].rearrange("(p k) o -> p (k o)", k=P), inv_rows[0:2, 0:P]) \
                .then_inc(inv_out, 16)
            sp.wait_ge(shaped, 3)
            sp.dma_start(message_rows[EP:EPAD, :].rearrange("(p k) f -> p (k f)", p=P),
                         x_zero[:, :]).then_inc(pad_out, 16)
            sp.wait_ge(pad_out, 16)
            for c in out_left + spread_left:
                sp.sem_inc(c.sem, 16)
            tails = [0]

            def load_pieces(pieces, into):
                (to, source), (to_rest, source_rest) = pieces
                sp.dma_start(to, source).then_inc(tail_in, 16)
                tails[0] += 1
                sp.wait_ge(tail_in, 16 * tails[0])
                sp.dma_start(to_rest, source_rest).then_inc(into.sem, 16)

            def load(g, table, tile, into):
                if table is x and g.it is None and g.c == NG - 1:
                    load_pieces(last_pieces(x, tile), into)
                else:
                    sp.dma_start(tile, of_group(table, g)).then_inc(into.sem, 16)

            def stores_landed(n):
                for s, c in enumerate(out_left):
                    sp.wait_ge(c.sem, c.base + c.unit * len(range(s, n, SLOTS)))
                sp.sem_inc(phase_done, 1)

            def node_phase(phase):
                last_reads = [diff_done, beta_done] if phase["kind"] == "gate" else [own_turned]
                results, late = {"relu": ([relu_done], 1), "unit": ([done_v], 2), "unit_ln": ([done_v, done_a], 4),
                                 "ln": ([done_a], 4), "gate": ([done_a], RESULT_LAG + 1)}[phase["kind"]]

                def loads(g):
                    if phase["kind"] == "gate":
                        starts_at = [sp.value_load(start_row[:, bass.ds(g.number * 2 + k, 1)], min_val=0, max_val=EP)
                                     for k in range(2)]
                    g.wait(*last_reads, ago=SLOTS)
                    load(g, phase["own"], own[:, g.slot, :], own_in[g.slot])
                    if phase["kind"] == "gate":
                        g.wait(agg_made, ago=SLOTS)
                        for k in range(2):
                            sp.dma_start(msg[:, g.slot, k, :], message_rows[bass.ds(starts_at[k], P), :]) \
                                .then_inc(windows_in[g.slot].sem, 16)
                        load(g, spread_rows, spread[:, g.slot, :, :].rearrange("p k n -> p (k n)"), spread_in[g.slot])
                    if phase["res"] is not None:
                        g.wait(sum_res, ago=SLOTS)
                        load(g, phase["res"], res[:, g.slot, :], res_in[g.slot])

                def step(g):
                    if (g + LEAD).exists():
                        loads(g + LEAD)
                    if (g - late).exists():
                        store(g - late)

                def store(g):
                    for result in results:
                        g.wait(result)
                        if len(results) > 1:
                            sp.sem_inc(stores_begun, 1)
                    if phase["out"] is out and g.it is None and g.c == NG - 1:
                        (tile, rows), (tile_rest, rows_rest) = last_pieces(out, done[:, g.slot, :])
                        sp.dma_start(rows, tile).then_inc(tail_out, 16)
                        sp.dma_start(rows_rest, tile_rest).then_inc(out_left[g.slot].sem, 16)
                        sp.wait_ge(tail_out, 16)
                    else:
                        sp.dma_start(of_group(phase["out"], g), done[:, g.slot, :]) \
                            .then_inc(out_left[g.slot].sem, 16)

                for c in range(LEAD):
                    loads(first(sp, c))
                each_group(sp, NG, LEAD + 1, step, behind=late)
                stores_landed(NG)

            def edge_phase():
                def loads(g):
                    g.wait(own_turned, ago=SLOTS)
                    into = own_in[g.slot]
                    if g.it is None and g.c == NEG - 1:
                        at = g.c * CH * P
                        whole, rest = divmod(E - at, P)
                        split = at + whole * P
                        load_pieces(((e_attr[:, g.slot, 0:whole, :],
                                      edge_attr[at:split, :].rearrange("(c p) f -> p c f", p=P)),
                                     (e_attr[0:rest, g.slot, whole, :], edge_attr[split:E, :])), into)
                    else:
                        sp.dma_start(e_attr[:, g.slot, :, :], of_chunks(edge_attr, g)).then_inc(into.sem, 16)

                def step(g):
                    if (g + LEAD).exists(NEG):
                        loads(g + LEAD)
                    g.wait(done_v)
                    sp.dma_start(of_chunks(message_rows, g), e_out[:, g.slot, :, :]) \
                        .then_inc(out_left[g.slot].sem, 16)
                    if g.exists(EDGE_STEPS):
                        for j in range(SPREADS):
                            store_spread(g.times(SPREADS) + j)

                def store_spread(m):
                    m.wait(spread_set)
                    sp.dma_start(of_group(spread_rows, m), spread[:, m.slot, :, :].rearrange("p k n -> p (k n)")) \
                        .then_inc(spread_left[m.slot].sem, 16)

                for c in range(LEAD):
                    loads(first(sp, c))
                each_group(sp, NEG, NEG - EDGE_STEPS, step)
                for s, c in enumerate(spread_left):
                    sp.wait_ge(c.sem, c.base + c.unit * len(range(s, SPREADS * EDGE_STEPS, SLOTS)))
                stores_landed(NEG)

            walk(sp, lambda phase: edge_phase() if phase["kind"] == "edge" else node_phase(phase))

        @block.gpsimd
        def _(pool):
            for c in POOL_COUNTS:
                pool.sem_inc(c.sem, CREDIT)
            pool.iota(pos_i[:, :], pattern=[[1, ROW]], base=0, channel_multiplier=ROW)
            pool.iota(thr_i[:, :], pattern=[[WIN * P, WT]], base=0, channel_multiplier=WIN)
            pool.iota(node_i[:, :], pattern=[[1, TILES], [TILES, HALF]], base=0, channel_multiplier=0)
            pool.iota(base_i[:, :], pattern=[[WIN, NW]], base=0, channel_multiplier=0)
            pool.iota(part_i[:, :], pattern=[[1, 1]], base=0, channel_multiplier=1).then_inc(shaped, 1)
            pool.memset(ident[:, :], 0.0).then_inc(shaped, 1)
            pool.memset(ones_row[:, :], 1.0)
            pool.memset(ones_b[:, :], 1.0)
            pool.memset(x_zero[:, :], 0.0)
            pool.memset(eps_ln[:, :], LN_EPS)
            pool.memset(minus_half[:, :, :], -0.5)
            pool.memset(msg[:, :, :, :], 0.0)
            pool.memset(hs[:, :, :, :], 0.0)
            pool.memset(hd[:, :, :, :], 0.0).then_inc(shaped, 1)
            pool.wait_ge(shaped, 3)
            pool.affine_select(out=ident[:, :], in_=ident[:, :], compare_op=ALU.not_equal, fill=1.0,
                               base=0, pattern=[[-1, P]], channel_multiplier=1).then_inc(shaped, 1)

            def fetch(into, table, at, bound, counted):
                pool.indirect_dma_start(into, None, table, bass.IndirectOffsetOnAxis(ap=at, axis=0),
                                        bounds_check=bound, oob_is_err=False) \
                    .then_inc(counted, 16)

            pool.wait_ge(rows_wanted, 1)
            dst_rows = dst_flat[0:EP, :].rearrange("(p k) o -> p (k o)", p=P)
            for t in range(WT):
                fetch(got_i[:, t, :], dst_rows, row_i[:, t:t + 1], P - 1, rows_in)
            pool.wait_ge(wins_wanted, 1)
            pool.wait_ge(inv_out, 32)
            for t in range(WT):
                for into, table in ((win_dst, dst_flat), (win_src, src_flat), (win_inv, inv_flat)):
                    fetch(into[:, t, :], table, start_i[:, t:t + 1], EPAD - P, wins_in)

            pool.wait_ge(tables_ready, 1)
            extra = Extra(pool, more_passed_pool)

            def node_phase(phase, extra_rounds):
                last_phase = phase["kind"] == "gate"

                def gather(g):
                    g.wait(idx_set)
                    g.wait(agg_made, ago=SLOTS)
                    pool.sem_inc(gathers_begun, 1)
                    for k in range(2):
                        fetch(msg[:, g.slot, k, :], phase["own"], idx[:, g.slot, k:k + 1], N - 1, msg_in[g.slot].sem)

                def more(g):
                    for k in range(2):
                        extra.rounds(g, k, lambda r, window: fetch_round(r, window))

                def fetch_round(r, window):
                    start = pool.value_load(start_row[:, bass.ds(window, 1)], min_val=0, max_val=EP)
                    at = nc.s_assert_within(start + r * P + P, 0, EPAD - P)
                    extra.wait((more_used, 1))
                    pool.dma_start(x_dst[:, :], dst_flat[bass.ds(at, P), :]).then_inc(more_at, 16)
                    pool.dma_start(x_inv[:, :], inv_flat[bass.ds(at, P), :]).then_inc(more_at, 16)
                    if last_phase:
                        pool.dma_start(x_msg[:, :], message_rows[bass.ds(at, P), :]).then_inc(more_at, 16)
                        extra.wait((more_at, 48))
                        pool.dma_start(x_src[:, :], src_flat[bass.ds(at, P), :]).then_inc(more_in, 16)
                    else:
                        pool.dma_start(x_src[:, :], src_flat[bass.ds(at, P), :]).then_inc(more_at, 16)
                        extra.wait((more_at, 48))
                        fetch(x_msg[:, :], phase["own"], x_src[:, :], N - 1, more_in)

                def add_beta(g):
                    g.wait_slot(own_in)
                    g.wait(sum_res, ago=SLOTS)
                    beta = b("L3_gnn_beta").rearrange("p (o f) -> p o f", o=1).to_broadcast([P, TILES, P])
                    pool.tensor_tensor(tiles(hb[:, g.slot, :]), tiles(own[:, g.slot, :]), beta, ALU.add) \
                        .then_inc(beta_done.sem, 1)

                def subtract_transform(g):
                    g.wait(sum_res, ago=SLOTS)
                    g.wait(gates_done)
                    pool.tensor_tensor(u_all[:, g.slot, :], own[:, g.slot, :], trans[:, g.turn, :], ALU.subtract) \
                        .then_inc(diff_done.sem, 1)

                def raise_variances(g):
                    which = both_norms(g)
                    if which is None:
                        return
                    g.wait(variances_set)
                    pool.tensor_tensor(powers[:, g.slot, which, :], variances[:, g.slot, which, :],
                                       minus_half[:, which, :], ALU.pow).then_inc(powers_done.sem, 1)

                def step(g):
                    if not last_phase and (g + LEAD).exists():
                        gather(g + LEAD)
                    if extra_rounds and (g + 1).exists():
                        more(g + 1)
                    if last_phase:
                        if g.exists():
                            subtract_transform(g)
                        if (g + 1).exists():
                            add_beta(g + 1)
                        raise_variances(g)

                if last_phase:
                    add_beta(first(pool, 0))
                    pool.sem_inc(powers_done.sem, 1)
                for c in range(0 if last_phase else LEAD):
                    gather(first(pool, c))
                if extra_rounds:
                    more(first(pool, 0))
                each_group(pool, NG, LEAD, step, behind=RESULT_LAG if last_phase else 0)

            def edge_phase():
                def gathers(g):
                    g.wait(idx_set)
                    g.wait(own_turned, ago=SLOTS)
                    pool.sem_inc(gathers_begun, 1)
                    for c in range(CH):
                        for k, rows in enumerate((hs, hd)):
                            at = k * CH + c
                            fetch(rows[:, g.slot, c, :], x3, idx[:, g.slot, at:at + 1], N - 1,
                                  hs_in[g.slot].sem)

                each_group(pool, NEG, 0, gathers)

            walk(pool, lambda phase: edge_phase() if phase["kind"] == "edge" else
                 extra.choose(lambda extra_rounds: node_phase(phase, extra_rounds)))

        @block.scalar
        def _(act):
            for c in ACT_COUNTS:
                act.sem_inc(c.sem, CREDIT)
            act.wait_ge(tables_ready, 1)
            act.activation(root[:, 0, :], eps_ln[:, :].to_broadcast([P, TILES]), ACT.Sqrt).then_inc(table_in, 1)
            act.wait_ge(table_in, 1)

            def node_phase(phase):
                kind = phase["kind"]

                def stage(g):
                    act.activation(idx[:, g.slot, 0:2], t_src[:, bass.ds(g.number * 2, 2)], ACT.Copy) \
                        .then_inc(idx_set.sem, 1)

                def keep(g):
                    g.wait(own_turned)
                    g.wait(out_made, ago=2)
                    act.activation(own_t[:, g.turn, :], bank[g.turn][:, 0:GN], ACT.Copy).then_inc(own_kept.sem, 1)
                    if kind != "relu":
                        g.wait(agg_made)
                        act.activation(agg_t[:, g.turn, :], bank[2 + g.turn][:, 0:GN], ACT.Copy) \
                            .then_inc(agg_kept_a.sem, 1)

                def relu(g):
                    g.wait(biased_done)
                    g.wait_slot(out_left, ago=1)
                    act.activation(done[:, g.slot, :], y_all[:, g.slot, :], ACT.Relu) \
                        .then_inc(relu_done.sem, 1)

                def norms(g):
                    made = bank[4 + g.turn][:, 0:GN]
                    g.wait(out_made)
                    g.wait(done_v if kind == "unit" else sum_res, ago=SLOTS)
                    act.activation(positive[:, g.slot, :], made, ACT.Relu)
                    for t in range(TILES):
                        squared = act.activation(squares[:, g.turn, t * P:(t + 1) * P], made[:, t * P:(t + 1) * P], ACT.Square,
                                                 accum_out=sumsq[:, g.slot, t:t + 1])
                    squared.then_inc(sq_done.sem, 1)
                    g.wait(sq_done)
                    act.activation(root[:, g.slot, :], sumsq[:, g.slot, :], ACT.Sqrt).then_inc(root_done.sem, 1)

                def deviation(g):
                    g.wait(mv_done)
                    act.activation(root_ln[:, g.slot, :], mv[:, g.slot, :, 1], ACT.Sqrt, bias=eps_ln[:, :]) \
                        .then_inc(std_done.sem, 1)

                def gates(g):
                    g.wait(out_made)
                    g.wait(upd_done, ago=2)
                    made = pair[2 + g.turn][:, 0:TILES * 2 * P].rearrange("p (t k f) -> p t k f", t=TILES, k=2)
                    act.activation(tiles(gate[:, g.turn, :]), made[:, :, 0, :], ACT.Sigmoid)
                    act.activation(tiles(trans[:, g.turn, :]), made[:, :, 1, :], ACT.Tanh) \
                        .then_inc(gates_done.sem, 1)

                def sum_squares(g):
                    g.wait(mean_done)
                    for t in range(TILES):
                        tile = slice(t * P, (t + 1) * P)
                        squared = act.activation(squares[:, g.turn, tile], y_all[:, g.slot, tile], ACT.Square,
                                                 bias=less_mean[:, g.slot, t:t + 1],
                                                 accum_out=sumsq[:, g.slot, t:t + 1])
                    squared.then_inc(sq_done.sem, 1)

                def normalise(g):
                    g.wait(shift_done)
                    g.wait_slot(out_left, ago=1)
                    own_tiles = range(DVE_TILES if kind == "unit_ln" else 0, TILES)
                    scale = powers[:, (g + OUTER_LAG).slot, 1, :] if kind == "gate" else rstd[:, g.slot, :]
                    for t in own_tiles:
                        tile = slice(t * P, (t + 1) * P)
                        last = act.activation(done[:, g.slot, tile], y_all[:, g.slot, tile], ACT.Identity,
                                              scale=scale[:, t:t + 1], bias=shift[:, g.slot, t:t + 1])
                    last.then_inc(done_a.sem, 1)

                def step(g):
                    if (g + 1).exists():
                        keep(g + 1)
                    if kind != "gate" and (g + SLOTS).exists():
                        g.wait(agg_made)
                        stage(g + SLOTS)
                    late = {"ln": 1, "unit_ln": 2}.get(kind)
                    if late and (g - late).exists():
                        deviation(g - late)
                    if g.exists() and kind != "ln":
                        {"relu": relu, "unit": norms, "unit_ln": norms, "gate": gates}[kind](g)
                    if kind == "gate" and (g - SQUARES_LAG).exists():
                        sum_squares(g - SQUARES_LAG)
                    result = {"unit_ln": 3, "ln": 2, "gate": RESULT_LAG}.get(kind)
                    if result and (g - result).exists():
                        normalise(g - result)

                for c in range(0 if kind == "gate" else SLOTS):
                    stage(first(act, c))
                keep(first(act, 0))
                each_group(act, NG, SLOTS, step, behind={"ln": 2, "unit_ln": 3, "gate": RESULT_LAG}.get(kind, 0))

            def edge_phase():
                def stage(g):
                    act.activation(idx[:, g.slot, :], e_idx[:, bass.ds(g.number * 2 * CH, 2 * CH)], ACT.Copy) \
                        .then_inc(idx_set.sem, 1)

                def keep(g):
                    g.wait(own_turned)
                    g.wait(out_made, ago=2)
                    act.activation(hs_t[:, g.turn, :], bank[g.turn], ACT.Copy).then_inc(own_kept.sem, 1)

                def step(g):
                    if (g + 1).exists(NEG):
                        keep(g + 1)
                    if (g + SLOTS).exists(NEG):
                        g.wait(own_turned)
                        stage(g + SLOTS)
                    g.wait(out_made)
                    g.wait(messages_made, ago=2)
                    act.activation(hidden_t[:, g.turn, :], bank[6], ACT.Silu, bias=b1_sb[:, :]) \
                        .then_inc(hidden_done.sem, 1)

                for c in range(SLOTS):
                    stage(first(act, c))
                keep(first(act, 0))
                each_group(act, NEG, SLOTS, step)

            walk(act, lambda phase: edge_phase() if phase["kind"] == "edge" else node_phase(phase))

        @block.tensor
        def _(pe):
            for c in PE_COUNTS:
                pe.sem_inc(c.sem, CREDIT)
            pe.wait_ge(shaped, 4)
            pe.wait_ge(cols_ready, 1)
            for k, col in enumerate((starts[:, ROW - 1:ROW], ends[:, 0:1], dst_f[:, 0:1])):
                turned = pe.transpose(bank[0][0:1, k * P:(k + 1) * P], col, ident[:, :])
            turned.then_inc(prep_t, 1)
            pe.wait_ge(rows_ready, 1)
            for k in range(2):
                pe.matmul(bank[1][:, k:k + 1], shifted[:, k, :], ones_row[:, 0:1], start=True, stop=True)
            pe.matmul(bank[1][:, P:2 * P], ones_row[:, :], line[:, 2, :], start=True, stop=True) \
                .then_inc(prep_t, 1)
            pe.wait_ge(more_cols, 1)
            for t in range(WT):
                turned = pe.transpose(bank[6][0:1, t * P:(t + 1) * P], start_f[:, t:t + 1], ident[:, :])
            turned.then_inc(prep_t, 1)
            pe.wait_ge(wins_ready, 1)
            for k in range(3):
                for t in range(WT):
                    source = by_win[:, k, t, :] if k < 2 else win_inv[:, t, :]
                    turned = pe.transpose(bank[2 + k][:, t * P:(t + 1) * P], source, ident[:, :])
            turned.then_inc(prep_t, 1)
            pe.wait_ge(tables_ready, 1)
            pe.sem_inc(more_used, 1)
            extra = Extra(pe, more_passed_pe)

            def node_phase(phase, extra_rounds):
                kind = phase["kind"]

                def front(g):
                    g.wait_slot(own_in)
                    g.wait(own_kept, ago=2)
                    for t in range(TILES):
                        turned = pe.transpose(bank[g.turn][:, t * P:(t + 1) * P],
                                              own[:, g.slot, t * P:(t + 1) * P], ident[:, :])
                    turned.then_inc(own_turned.sem, 1)
                    g.wait_slot(windows_in if kind == "gate" else msg_in)
                    if kind == "gate":
                        g.wait_slot(spread_in)
                    else:
                        g.wait(spread_set)
                    g.wait(agg_kept_v if kind == "relu" else agg_kept_a, ago=2)
                    agg = tiles(bank[2 + g.turn][:, 0:GN])
                    half = [agg[:, :, k * HALF:(k + 1) * HALF] for k in range(2)]
                    pe.matmul(half[0], msg[:, g.slot, 0, :], spread[:, g.slot, 0, :], start=True, stop=False)
                    if extra_rounds:
                        for k in range(2):
                            extra.rounds(g, k, lambda r, window: add_round(half[k]))
                    pe.matmul(half[1], msg[:, g.slot, 1, :], spread[:, g.slot, 1, :], start=False,
                              stop=True).then_inc(agg_made.sem, 1)

                def add_round(sums):
                    extra.wait((more_in, 16), (more_spread, 1))
                    pe.matmul(sums, x_msg[:, :], x_spread[:, :], start=False, stop=False) \
                        .then_inc(more_used, 1)

                def convolve(g):
                    g.wait(own_kept)
                    g.wait(agg_kept_v if kind == "relu" else agg_kept_a)
                    g.wait({"relu": biased_done, "unit": sq_done, "unit_ln": sq_done, "ln": sum_res}[kind], ago=2)
                    o = bank[4 + g.turn][:, 0:GN]
                    by_pe = kind != "relu"
                    if by_pe:
                        pe.matmul(o, ones_b[:, :], bias_conv[:, phase["bias"], :], start=True, stop=False)
                    for t in range(TILES):
                        tile = slice(t * P, (t + 1) * P)
                        pe.matmul(o[:, tile], own_t[:, g.turn, tile], w(phase["wr"]),
                                  start=not by_pe and t == 0, stop=False)
                        made = pe.matmul(o[:, tile], agg_t[:, g.turn, tile], w(phase["wl"]), start=False,
                                         stop=t == TILES - 1)
                    made.then_inc(out_made.sem, 1)

                def gates(g):
                    g.wait(own_kept)
                    g.wait(agg_kept_a)
                    g.wait(gates_done, ago=2)
                    o = pair[2 + g.turn]
                    pe.matmul(o[:, 0:4 * P], ones_b[:, :], bias_gate[:, :, :], start=True, stop=False)
                    pe.matmul(o[:, 4 * P:6 * P], ones_b[:, :], bias_gate[:, 0, :], start=True, stop=False)
                    k = WEIGHTS.index("Wg_self") * P
                    for t in range(TILES):
                        tile = slice(t * P, (t + 1) * P)
                        both = o[:, 2 * t * P:2 * (t + 1) * P]
                        pe.matmul(both, own_t[:, g.turn, tile], w_sb[:, k:k + 2 * P], start=False, stop=False)
                        made = pe.matmul(both, agg_t[:, g.turn, tile], w_sb[:, k + 2 * P:k + 4 * P],
                                         start=False, stop=t > 0)
                    made.then_inc(out_made.sem, 1)

                def step(g):
                    if (g + 1).exists():
                        front(g + 1)
                    (gates if kind == "gate" else convolve)(g)

                front(first(pe, 0))
                each_group(pe, NG, 1, step)

            def edge_phase():
                def front(g):
                    g.wait_slot(own_in)
                    g.wait_slot(hs_in)
                    g.wait(own_kept, ago=2)
                    g.wait(agg_kept_v, ago=2)
                    for c in range(CH):
                        chunk = slice(c * P, (c + 1) * P)
                        pe.transpose(bank[g.turn][:, chunk], hs[:, g.slot, c, :], ident[:, :])
                        pe.transpose(bank[2 + g.turn][:, chunk], hd[:, g.slot, c, :], ident[:, :])
                        turned = pe.transpose(bank[4 + g.turn][0:DE, chunk], e_attr[:, g.slot, c, :], ident[:, :])
                    turned.then_inc(own_turned.sem, 1)

                def hidden(g):
                    g.wait(own_kept)
                    g.wait(agg_kept_v)
                    g.wait(hidden_done, ago=1)
                    pe.matmul(bank[6], w("W1_src"), hs_t[:, g.turn, :], start=True, stop=False)
                    pe.matmul(bank[6], w("W1_dst"), hd_t[:, g.turn, :], start=False, stop=False)
                    pe.matmul(bank[6], w("W1_edge")[0:DE, :], ea_t[:, g.turn, :], start=False, stop=True) \
                        .then_inc(out_made.sem, 1)

                def messages(g):
                    g.wait(hidden_done)
                    g.wait(done_v, ago=1)
                    pe.matmul(bank[7], ones_b[:, :], bias_edge[:, :], start=True, stop=False)
                    for c in range(CH):
                        chunk = slice(c * P, (c + 1) * P)
                        made = pe.matmul(bank[7][:, chunk], hidden_t[:, g.turn, chunk], w("L3_gnn_W2"),
                                         start=False, stop=c == CH - 1)
                    made.then_inc(messages_made.sem, 1)

                def step(g):
                    if (g + 1).exists(NEG):
                        front(g + 1)
                    hidden(g)
                    messages(g)

                front(first(pe, 0))
                each_group(pe, NEG, 1, step)

            walk(pe, lambda phase: edge_phase() if phase["kind"] == "edge" else
                 extra.choose(lambda extra_rounds: node_phase(phase, extra_rounds)))

        @block.vector
        def _(v):
            for c in DVE_COUNTS:
                v.sem_inc(c.sem, CREDIT)
            steps = [0]

            def then(ins):
                ins.then_inc(prep_v, 1)
                steps[0] += 1
                v.wait_ge(prep_v, steps[0])

            v.wait_ge(shaped, 1)
            for to, frm in ((pos_f, pos_i), (thr, thr_i), (node_of_col, node_i), (win_base, base_i)):
                v.tensor_copy(to[:, :], frm[:, :])
            then(v.tensor_copy(part_f[:, :], part_i[:, :]))
            v.wait_ge(loaded, 16 * len(LOADS))
            for to, frm in ((dst_f, dst_i), (before_f, before_i)):
                v.tensor_copy(to[:, :], frm[:, :])
            then(v.tensor_copy(after_f[:, :], after_i[:, :]))
            v.tensor_tensor(before_f[:, :], dst_f[:, :], before_f[:, :], ALU.not_equal)
            then(v.tensor_tensor(after_f[:, :], dst_f[:, :], after_f[:, :], ALU.not_equal))
            v.tensor_tensor(before_f[:, :], before_f[:, :], pos_f[:, :], ALU.mult)
            then(v.tensor_scalar(junk[:, :], pos_f[:, :], 1.0 - OUTSIDE, None, ALU.add))
            then(v.tensor_tensor(after_f[:, :], after_f[:, :], junk[:, :], ALU.mult))
            then(v.tensor_scalar(after_f[:, :], after_f[:, :], float(OUTSIDE), None, ALU.add))
            v.tensor_tensor_scan(starts[:, :], before_f[:, :], before_f[:, :], 0.0, ALU.max, ALU.max)
            then(v.tensor_tensor_scan(ends[:, ::-1], after_f[:, ::-1], after_f[:, ::-1], float(OUTSIDE),
                                      ALU.min, ALU.min))
            v.sem_inc(cols_ready, 1)
            v.wait_ge(prep_t, 1)
            then(v.tensor_copy(line[:, :, :], bank[0][0:1, 0:3 * P].rearrange("o (k p) -> o k p", k=3)))
            v.tensor_tensor_scan(scanned[:, 0, :], line[:, 0, :], line[:, 0, :], 0.0, ALU.max, ALU.max)
            v.tensor_tensor_scan(scanned[:, 1, ::-1], line[:, 1, ::-1], line[:, 1, ::-1], float(OUTSIDE),
                                 ALU.min, ALU.min)
            v.memset(shifted[:, 0, 0:1], 0.0)
            then(v.memset(shifted[:, 1, P - 1:P], float(OUTSIDE)))
            v.tensor_copy(shifted[:, 0, 1:P], scanned[:, 0, 0:P - 1])
            v.tensor_copy(shifted[:, 1, 0:P - 1], scanned[:, 1, 1:P]).then_inc(rows_ready, 1)
            v.wait_ge(prep_t, 2)
            then(v.tensor_copy(carry[:, :], bank[1][:, 0:2]))
            v.tensor_scalar(starts[:, :], starts[:, :], carry[:, 0:1], None, ALU.max)
            then(v.tensor_scalar(ends[:, :], ends[:, :], carry[:, 1:2], None, ALU.min))
            then(v.tensor_tensor(ends[:, :], ends[:, :], starts[:, :], ALU.subtract))
            v.reciprocal(inv_rows[:, :], ends[:, :]).then_inc(inv_ready, 1)
            for t in range(WT):
                then(v.tensor_scalar(junk[:, 0:P], bank[1][:, P:2 * P], thr[:, t:t + 1], None, ALU.is_lt,
                                     ALU.add, accum_out=cnt[:, t:t + 1]))
            then(v.tensor_scalar(row_f[:, :], cnt[:, :], -1.0, 0.0, ALU.add, ALU.max))
            v.tensor_copy(row_i[:, :], row_f[:, :]).then_inc(rows_wanted, 1)
            v.wait_ge(rows_in, 16 * WT)
            then(v.tensor_copy(got_f[:, :, :], got_i[:, :, :]))
            for t in range(WT):
                then(v.tensor_scalar(junk[:, :], got_f[:, t, :], thr[:, t:t + 1], None, ALU.is_lt, ALU.add,
                                     accum_out=cnt[:, t:t + 1]))
            then(v.scalar_tensor_tensor(start_f[:, :], row_f[:, :], float(ROW), cnt[:, :], ALU.mult, ALU.add))
            v.tensor_copy(start_i[:, :], start_f[:, :]).then_inc(wins_wanted, 1)
            v.sem_inc(more_cols, 1)
            v.wait_ge(weights_in, 16 * len(LATER_LOADS))
            for one, other in (("L1_gnn_b_neigh1", "L1_gnn_b_self1"), ("L1_gnn_b_neigh2", "L1_gnn_b_self2")):
                then(v.tensor_tensor(b(one), b(one), b(other), ALU.add))
            whole = b_sb[:, 0:NB * P]
            for k in range(3):
                v.tensor_scalar(mask[:, k:k + 1], part_f[:, :], float(k), None, ALU.is_equal)
            then(v.tensor_copy(hi[:, :], whole))
            then(v.tensor_tensor(rest_f[:, :], whole, hi[:, :], ALU.subtract))
            then(v.tensor_copy(mid[:, :], rest_f[:, :]))
            then(v.tensor_tensor(rest_f[:, :], rest_f[:, :], mid[:, :], ALU.subtract))
            then(v.tensor_copy(lo[:, :], rest_f[:, :]))
            then(v.tensor_scalar(hi[:, :], hi[:, :], mask[:, 0:1], None, ALU.mult))
            then(v.scalar_tensor_tensor(hi[:, :], mid[:, :], mask[:, 1:2], hi[:, :], ALU.mult, ALU.add))
            then(v.scalar_tensor_tensor(hi[:, :], lo[:, :], mask[:, 2:3], hi[:, :], ALU.mult, ALU.add))
            for k in range(6):
                for t in range(TILES):
                    v.tensor_copy(bias_conv[:, k, t * P:(t + 1) * P], hi[:, k * P:(k + 1) * P])
            for c in range(CH):
                v.tensor_copy(bias_edge[:, c * P:(c + 1) * P], hi[:, 6 * P:7 * P])
            for k in range(2):
                v.tensor_copy(bias_gate[:, k, :], hi[:, 7 * P:9 * P])
            v.wait_ge(prep_t, 3)
            then(v.tensor_copy(start_line[:, :], bank[6][0:1, 0:WT * P]))
            v.tensor_copy(start_row[:, :], start_line[:, :])
            then(v.tensor_tensor(more_f[:, :], start_line[:, 1:NW + 1], start_line[:, 0:NW], ALU.subtract))
            then(v.tensor_scalar(more_i[:, :], more_f[:, :], float(P - 1), None, ALU.add))
            then(v.tensor_scalar(more_i[:, :], more_i[:, :], P.bit_length() - 1, None, ALU.arith_shift_right))
            then(v.tensor_scalar(more_f[:, :], more_i[:, :], -1.0, 0.0, ALU.add, ALU.max))
            then(v.tensor_reduce(most_f[:, :], more_f[:, :], AX_X, ALU.max))
            v.tensor_copy(more_row[:, :], more_f[:, :])
            v.tensor_copy(more_any[:, :], most_f[:, :])
            v.wait_ge(wins_in, 16 * 3 * WT)
            for t in range(WT):
                last = v.tensor_scalar(by_win[:, 1, t, :], win_dst[:, t, :], thr[:, t:t + 1], None, ALU.subtract)
            then(last)
            then(v.tensor_scalar(skip[:, :, :], by_win[:, 1, :, :], float(WIN), float(OUTSIDE), ALU.is_ge,
                                 ALU.mult))
            v.tensor_tensor(by_win[:, 0, :, :], win_src[:, :, :], skip[:, :, :], ALU.add) \
                .then_inc(wins_ready, 1)
            v.wait_ge(prep_t, 4)
            for k, table in enumerate((t_src, t_dst, t_inv)):
                copied = v.tensor_copy(table[:, :], bank[2 + k][:, 0:WT * P])
            copied.then_inc(tables_ready, 1)
            v.wait_ge(tables_ready, 1)
            extra = Extra(v, more_passed_v)

            def spread_round(r, window):
                extra.wait((more_at, 48))
                v.tensor_tensor(x_local[:, :], x_dst[:, :], win_base[:, bass.ds(window, 1)], ALU.subtract) \
                    .then_inc(more_dst, 1)
                extra.wait((more_dst, 1))
                v.tensor_scalar(x_spread[:, :], node_of_col[:, :], x_local[:, :], x_inv[:, :], ALU.is_equal,
                                ALU.mult).then_inc(more_spread, 1)

            def more(g):
                for k in range(2):
                    extra.rounds(g, k, spread_round)

            def inc(ins, counted):
                ins.then_inc(counted.sem, 1)

            def build_spread(g, k):
                at = bass.ds(g.number * 2 + k, 1)
                return v.tensor_scalar(spread[:, g.slot, k, :], node_of_col[:, :], t_dst[:, at],
                                       t_inv[:, at], ALU.is_equal, ALU.mult)

            def node_phase(phase, extra_rounds):
                kind = phase["kind"]

                def build(g, k):
                    if k == 0:
                        g.wait(agg_made, ago=SLOTS)
                    return build_spread(g, k)

                def build_both(g):
                    build(g, 0)
                    inc(build(g, 1), spread_set)

                def keep(g):
                    if kind == "relu":
                        g.wait(agg_made)
                        g.wait(out_made, ago=2)
                        inc(v.tensor_copy(agg_t[:, g.turn, :], bank[2 + g.turn][:, 0:GN]), agg_kept_v)

                def add_bias(g):
                    bias = b(BIASES[phase["bias"]]).rearrange("p (o f) -> p o f", o=1).to_broadcast([P, TILES, P])
                    g.wait(relu_done, ago=SLOTS)
                    g.wait(out_made)
                    inc(v.tensor_tensor(tiles(y_all[:, g.slot, :]), tiles(bank[4 + g.turn][:, 0:GN]), bias, ALU.add),
                        biased_done)

                def cap_norms(g):
                    inc(v.tensor_scalar(capped[:, :], root[:, g.slot, :], NORM_EPS, None, ALU.max), cap_done)

                def invert_norms(g):
                    g.wait(cap_done)
                    inc(v.reciprocal(rinv[:, :], capped[:, :]), rinv_done)

                def unit_rows(g):
                    g.wait(rinv_done)
                    if kind == "unit":
                        g.wait_slot(out_left, ago=1)
                    else:
                        g.wait_slot(res_in)
                        g.wait(done_a, ago=SLOTS)
                    for t in range(TILES):
                        tile = slice(t * P, (t + 1) * P)
                        if kind == "unit":
                            last = v.tensor_scalar(done[:, g.slot, tile], positive[:, g.slot, tile],
                                                   rinv[:, t:t + 1], None, ALU.mult)
                        else:
                            last = v.scalar_tensor_tensor(y_all[:, g.slot, tile], positive[:, g.slot, tile],
                                                          rinv[:, t:t + 1], res[:, g.slot, tile], ALU.mult, ALU.add)
                    inc(last, done_v if kind == "unit" else sum_res)

                def add_residual(g):
                    g.wait_slot(res_in)
                    g.wait(done_a, ago=SLOTS)
                    g.wait(out_made)
                    inc(v.tensor_tensor(y_all[:, g.slot, :], bank[4 + g.turn][:, 0:GN], res[:, g.slot, :], ALU.add),
                        sum_res)

                def take_stats(g, rows, to, written, counted):
                    g.wait(written)
                    for t in range(TILES):
                        taken = v.bn_stats(to[:, g.slot, t, :], rows[:, g.slot, t * P:(t + 1) * P])
                    inc(taken, counted)

                def take_moments(g, to, source, counted):
                    for t in range(TILES):
                        last = v.bn_aggr(to[:, g.slot, t, :], source[:, g.slot, t, :])
                    inc(last, counted)

                def invert_deviation(g):
                    g.wait(std_done)
                    inc(v.reciprocal(rstd[:, g.slot, :], root_ln[:, g.slot, :]), rstd_done)

                def normalise(g):
                    g.wait(rstd_done)
                    g.wait_slot(out_left, ago=1)
                    for t in range(DVE_TILES):
                        tile = slice(t * P, (t + 1) * P)
                        last = v.tensor_scalar(done[:, g.slot, tile], y_all[:, g.slot, tile], mv[:, g.slot, t, 0:1],
                                               rstd[:, g.slot, t:t + 1], ALU.subtract, ALU.mult)
                    inc(last, done_v)

                def shift_rows(g):
                    g.wait(rstd_done)
                    inc(v.scalar_tensor_tensor(shift[:, g.slot, :], mv[:, g.slot, :, 0], -1.0, rstd[:, g.slot, :],
                                               ALU.mult, ALU.mult), shift_done)

                def unit_step(g, build_first, build_second):
                    if (g - 1).exists():
                        (g - 1).wait(root_done)
                        cap_norms(g - 1)
                    build_first()
                    if (g - 1).exists():
                        invert_norms(g - 1)
                    build_second()
                    if (g - 1).exists():
                        unit_rows(g - 1)

                def unit_ln_step(g, build_first, build_second):
                    if (g - 2).exists():
                        (g - 2).wait(stats_done)
                    if (g - 1).exists():
                        (g - 1).wait(root_done)
                        cap_norms(g - 1)
                    if (g - 2).exists():
                        take_moments(g - 2, mv, stats, mv_done)
                    build_first()
                    if (g - 3).exists():
                        invert_deviation(g - 3)
                    if (g - 1).exists():
                        invert_norms(g - 1)
                    build_second()
                    if (g - 3).exists():
                        shift_rows(g - 3)
                    if (g - 1).exists():
                        unit_rows(g - 1)
                    if (g - 3).exists():
                        normalise(g - 3)
                    if (g - 1).exists():
                        take_stats(g - 1, y_all, stats, sum_res, stats_done)

                def ln_step(g, build_first, build_second):
                    if (g - 1).exists():
                        (g - 1).wait(stats_done)
                    if g.exists():
                        add_residual(g)
                    if (g - 1).exists():
                        take_moments(g - 1, mv, stats, mv_done)
                    if (g - 2).exists():
                        invert_deviation(g - 2)
                    build_first()
                    if (g - 2).exists():
                        shift_rows(g - 2)
                    build_second()
                    if g.exists():
                        take_stats(g, y_all, stats, sum_res, stats_done)

                def gate_step(g):
                    gt, tr, u = gate[:, g.turn, :], trans[:, g.turn, :], u_all[:, g.slot, :]
                    if (g - INNER_LAG).exists():
                        (g - INNER_LAG).wait(inner_stats)
                    if (g - RESULT_LAG).exists():
                        outer_shift(g - RESULT_LAG)
                    if (g - INNER_LAG).exists():
                        take_moments(g - INNER_LAG, mv_in, stats_in, inner_mean)
                    set_variances(g)
                    if g.exists():
                        g.wait(diff_done)
                        inc(v.tensor_tensor(u, u, gt, ALU.mult), gated_done)
                    if (g - INNER_LAG).exists():
                        scale_by_gamma(g - INNER_LAG)
                    if g.exists():
                        g.wait(gated_done)
                        inc(v.tensor_tensor(u, u, tr, ALU.add), upd_done)
                    if (g - SUM_LAG).exists():
                        add_own(g - SUM_LAG)
                    if g.exists():
                        take_stats(g, u_all, stats_in, upd_done, inner_stats)
                    if (g - SUM_LAG).exists():
                        (g - SUM_LAG).wait(sum_res)
                        inc(v.tensor_scalar(less_mean[:, (g - SUM_LAG).slot, :], sums[:, (g - SUM_LAG).slot, :], -1.0 / D, None,
                                            ALU.mult), mean_done)

                def set_variances(g):
                    inner, outer = g - INNER_LAG, g - OUTER_LAG
                    last = None
                    if inner.exists():
                        inner.wait(inner_mean)
                        last = v.tensor_scalar(variances[:, g.slot, 0, :], mv_in[:, inner.slot, :, 1], LN_EPS, None,
                                               ALU.add)
                    if outer.exists():
                        outer.wait(sq_done)
                        last = v.tensor_scalar(variances[:, g.slot, 1, :], sumsq[:, outer.slot, :], 1.0 / D, LN_EPS,
                                               ALU.mult, ALU.add)
                    if last is not None:
                        inc(last, variances_set)

                def scale_by_gamma(g):
                    u = u_all[:, g.slot, :]
                    for t in range(TILES):
                        tile = slice(t * P, (t + 1) * P)
                        last = v.scalar_tensor_tensor(u[:, tile], u[:, tile], mv_in[:, g.slot, t, 0:1],
                                                      b("L3_gnn_gamma"), ALU.subtract, ALU.mult)
                    inc(last, gamma_done)

                def add_own(g):
                    g.wait(gamma_done)
                    g.wait(beta_done)
                    (g + INNER_LAG).wait(powers_done)
                    g.wait(done_a, ago=SLOTS)
                    for t in range(TILES):
                        tile = slice(t * P, (t + 1) * P)
                        last = v.scalar_tensor_tensor(y_all[:, g.slot, tile], u_all[:, g.slot, tile],
                                                      powers[:, (g + INNER_LAG).slot, 0, t:t + 1], hb[:, g.slot, tile],
                                                      ALU.mult, ALU.add, accum_out=sums[:, g.slot, t:t + 1])
                    inc(last, sum_res)

                def outer_shift(g):
                    (g + OUTER_LAG).wait(powers_done)
                    inc(v.tensor_tensor(shift[:, g.slot, :], less_mean[:, g.slot, :], powers[:, (g + OUTER_LAG).slot, 1, :],
                                        ALU.mult), shift_done)

                def step(g):
                    ahead = (g + LEAD).exists()

                    def build_first():
                        if ahead:
                            build(g + LEAD, 0)

                    def build_second():
                        if ahead:
                            inc(build(g + LEAD, 1), spread_set)

                    if extra_rounds and (g + 1).exists():
                        more(g + 1)
                    if kind == "gate":
                        gate_step(g)
                    elif kind == "relu":
                        build_first()
                        build_second()
                        if (g + 1).exists():
                            keep(g + 1)
                        if g.exists():
                            add_bias(g)
                    else:
                        {"unit": unit_step, "unit_ln": unit_ln_step, "ln": ln_step}[kind](g, build_first, build_second)

                if kind == "gate":
                    v.sem_inc(variances_set.sem, 1)
                if kind != "gate":
                    for c in range(LEAD):
                        build_both(first(v, c))
                if extra_rounds:
                    more(first(v, 0))
                keep(first(v, 0))
                each_group(v, NG, LEAD, step, behind={"unit": 1, "unit_ln": 3, "ln": 2, "gate": RESULT_LAG}.get(kind, 0))

            def edge_phase():
                def keep(g):
                    g.wait(own_turned)
                    g.wait(out_made, ago=2)
                    v.tensor_copy(hd_t[:, g.turn, :], bank[2 + g.turn])
                    inc(v.tensor_copy(ea_t[:, g.turn, :], bank[4 + g.turn][0:DE, :]), agg_kept_v)

                def step(g):
                    if (g + 1).exists(NEG):
                        keep(g + 1)
                    g.wait(messages_made)
                    g.wait_slot(out_left, ago=1)
                    inc(v.tensor_copy(e_out[:, g.slot, :, :].rearrange("p c f -> p (c f)"), bank[7]), done_v)
                    if g.exists(EDGE_STEPS):
                        for j in range(SPREADS):
                            m = g.times(SPREADS) + j
                            m.wait_slot(spread_left, ago=1)
                            build_spread(m, 0)
                            inc(build_spread(m, 1), spread_set)

                keep(first(v, 0))
                each_group(v, NEG, NEG - EDGE_STEPS, step)

            walk(v, lambda phase: edge_phase() if phase["kind"] == "edge" else
                 extra.choose(lambda extra_rounds: node_phase(phase, extra_rounds)))


def kernel(**inputs):
    import numpy as _np
    import concourse.bacc as _bacc
    from concourse import mybir as _mybir
    from concourse.bass_utils import run_bass_kernel_spmd as _run

    a = {name: _np.ascontiguousarray(value) for name, value in inputs.items()}
    dst = _np.concatenate([a["dst"], _np.full(EPAD - E, NP, a["dst"].dtype)])
    src = _np.concatenate([a["src"], _np.zeros(EPAD - E, a["src"].dtype)])
    before = _np.concatenate([_np.full(1, -1, dst.dtype), dst[:EP - 1]])

    def columns(edges):
        return edges[:EP].reshape(NEG, CH, P).transpose(2, 0, 1)

    w1, wg, wt = a["L3_gnn_W1"], a["L3_gnn_Wg"], a["L3_gnn_Wt"]
    made = {"W1_src": w1[:D], "W1_dst": w1[D:2 * D],
            "W1_edge": _np.concatenate([w1[2 * D:], _np.zeros((P - DE, D), w1.dtype)]),
            "Wg_self": wg[:D], "Wt_self": wt[:D], "Wg_agg": wg[D:], "Wt_agg": wt[D:]}
    turned = [n for n in WEIGHTS if n.startswith(("L1_", "L2_"))]
    weights = [made[n] if n in made else a[n].T if n in turned else a[n] for n in WEIGHTS]
    feeds = {
        "x": a["x"], "src_flat": src.reshape(-1, 1), "dst_flat": dst.reshape(-1, 1),
        "dst_before": before.reshape(P, ROW), "dst_after": dst[1:EP + 1].reshape(P, ROW),
        "edge_cols": _np.concatenate([columns(src), columns(dst)], axis=2).reshape(P, -1),
        "edge_attr": a["edge_attr_64"], "weights": _np.concatenate(weights, axis=1),
        "biases": _np.tile(_np.concatenate([a[n] for n in BIASES])[None, :], (P, 1)),
        "b1_col": a["L3_gnn_b1"].reshape(P, 1),
    }
    nc = _bacc.Bacc("TRN2", target_bir_lowering=False, num_devices=1)
    arrays, args = {}, []
    for name, value in feeds.items():
        value = _np.ascontiguousarray(value)
        arrays[f"in_{name}"] = value
        args.append(nc.dram_tensor(f"in_{name}", value.shape, _mybir.dt.from_np(value.dtype),
                                   kind="ExternalInput").ap())
    out = nc.dram_tensor("out_x", (N, D), F32, kind="ExternalOutput").ap()
    gnn_kernel(nc, *args, out)
    return _run(nc, [arrays], core_ids=[0]).results[0]["out_x"]
```
